# Optimizing a Trainium2 kernel written in Bass

```python
import numpy as np
import jax
import jax.numpy as jnp

def _softmax(x, axis=-1):
    return jax.nn.softmax(x, axis=axis)

def _gelu(x):
    return jax.nn.gelu(x, approximate=True)

def _silu(x):
    return jax.nn.silu(x)

def _sigmoid(x):
    return jax.nn.sigmoid(x)

def _layernorm(x, axis=-1, eps=1e-05):
    m = jnp.mean(x, axis=axis, keepdims=True)
    v = jnp.var(x, axis=axis, keepdims=True)
    return (x - m) / jnp.sqrt(v + eps)

def _scatter_add(tgt, idx, src, axis=0):
    return tgt.at[idx].add(src)

def _segment_sum(src, seg, n):
    return jax.ops.segment_sum(src, seg, n)
kernel_name = 'mk_decoder_postln_d2_seqx_r4_5a7e97'

def setup_inputs(seed: int=0):
    np.random.seed(seed)
    _w = jnp.asarray

    def _rec_inputs():
        import jax
        import jax.numpy as jnp
        _rk = jax.random.key(seed)
        x = -0.0002928 + 1 * jax.random.normal(jax.random.fold_in(_rk, 1), (8, 256, 256), jnp.float32)
        _lenS = 256 - jax.random.randint(jax.random.fold_in(_rk, 7), (8,), 0, max(1, 256 // 4) + 1, jnp.int32)
        _lenS2 = 256 - jax.random.randint(jax.random.fold_in(_rk, 8), (8,), 0, max(1, 256 // 4) + 1, jnp.int32)
        _ctx_1024P = jax.random.normal(jax.random.fold_in(_rk, 11), (8, 16, 256), jnp.float32)
        _ctx_1024c = jax.random.dirichlet(jax.random.fold_in(_rk, 511), 0.3 * jnp.ones((16,), jnp.float32), (8, 256))
        _ctx_1024t = jnp.einsum('bsk,bkd->bsd', _ctx_1024c, _ctx_1024P)
        _ctx_1024t = _ctx_1024t * jax.lax.rsqrt(jnp.mean(jnp.square(_ctx_1024t)) + 1e-12) * 0.953939
        ctx_1024 = -1.39393e-06 + 0.999914 * (_ctx_1024t + 0.3 * jax.random.normal(jax.random.fold_in(_rk, 611), (8, 256, 256), jnp.float32))
        return (x, ctx_1024)
    x, ctx_1024 = _rec_inputs()

    def _L0_attn_setup():
        import jax, jax.numpy as jnp
        import numpy as np
        SCALING = 1.0
        H, N = (256, 64)
        B, L = (4, 512)
        key = jax.random.key(seed)
        ks = jax.random.split(key, 10)
        x = jax.random.normal(ks[0], (B, L, H), dtype=jnp.float32)
        in_proj = jax.random.normal(ks[1], (H, N), dtype=jnp.float32)
        out_proj = jax.random.normal(ks[2], (N, H), dtype=jnp.float32)
        lo, hi = (np.log(0.01), np.log(100.0))
        frequencies = jnp.exp(jax.random.uniform(ks[3], (N,)) * (hi - lo) + lo) / SCALING
        decays = jnp.full((N,), np.log(0.5), dtype=jnp.float32)
        s = 1.0 / np.sqrt(H)
        ss_W = jax.random.uniform(ks[4], (H, H), minval=-s, maxval=s)
        ss_b = jax.random.uniform(ks[5], (H,), minval=-s, maxval=s)
        gate_W = jax.random.uniform(ks[6], (H, H), minval=-s, maxval=s)
        gate_b = jax.random.uniform(ks[7], (H,), minval=-s, maxval=s)
        fin_W = jax.random.uniform(ks[8], (H, H), minval=-s, maxval=s)
        fin_b = jax.random.uniform(ks[9], (H,), minval=-s, maxval=s)
        return {'x': x, 'in_proj': in_proj, 'out_proj': out_proj, 'frequencies': frequencies, 'decays': decays, 'ss_W': ss_W, 'ss_b': ss_b, 'gate_W': gate_W, 'gate_b': gate_b, 'fin_W': fin_W, 'fin_b': fin_b}
    _L0_attn_all = _L0_attn_setup()
    _L0_attn_in = {k: v for k, v in _L0_attn_all.items() if k in ('in_proj', 'out_proj', 'frequencies', 'decays', 'ss_W', 'ss_b', 'gate_W', 'gate_b', 'fin_W', 'fin_b')}
    del _L0_attn_all

    def _L0_xattn_setup():
        import jax, jax.numpy as jnp
        import numpy as np
        D_MODEL = 256
        NUM_HEADS = 16
        D_K = D_MODEL // NUM_HEADS

        def _split_heads(x):
            B, S, _ = x.shape
            return x.reshape(B, S, NUM_HEADS, D_K).transpose(0, 2, 1, 3)
        key = jax.random.key(seed)
        ks = jax.random.split(key, 7)
        B, S = (2, 512)
        scale = 1.0 / np.sqrt(D_MODEL)
        return {'q': jax.random.normal(ks[0], (B, S, D_MODEL), jnp.float32), 'k': jax.random.normal(ks[1], (B, S, D_MODEL), jnp.float32), 'v': jax.random.normal(ks[2], (B, S, D_MODEL), jnp.float32), 'Wq': jax.random.normal(ks[3], (D_MODEL, D_MODEL), jnp.float32) * scale, 'Wk': jax.random.normal(ks[4], (D_MODEL, D_MODEL), jnp.float32) * scale, 'Wv': jax.random.normal(ks[5], (D_MODEL, D_MODEL), jnp.float32) * scale, 'Wo': jax.random.normal(ks[6], (D_MODEL, D_MODEL), jnp.float32) * scale}
    _L0_xattn_all = _L0_xattn_setup()
    _L0_xattn_in = {k: v for k, v in _L0_xattn_all.items() if k in ('Wq', 'Wk', 'Wv', 'Wo')}
    del _L0_xattn_all

    def _L0_ffn_setup():
        import jax, jax.numpy as jnp
        import numpy as np
        TOP_K = 2
        key = jax.random.key(seed)
        ks = jax.random.split(key, 6)
        B, S, D, U, E = (4, 256, 256, 1024, 8)
        return {'x': jax.random.normal(ks[0], (B, S, D), dtype=jnp.float32), 'w_up': jax.random.normal(ks[1], (E, U, D), dtype=jnp.float32), 'w_down': jax.random.normal(ks[2], (E, D, U), dtype=jnp.float32), 'b_up': jax.random.normal(ks[3], (E, U), dtype=jnp.float32), 'b_down': jax.random.normal(ks[4], (E, D), dtype=jnp.float32), 'w_router': jax.random.normal(ks[5], (E, D), dtype=jnp.float32)}
    _L0_ffn_all = _L0_ffn_setup()
    _L0_ffn_in = {k: v for k, v in _L0_ffn_all.items() if k in ('w_up', 'w_down', 'b_up', 'b_down', 'w_router')}
    del _L0_ffn_all

    def _L1_attn_setup():
        import jax, jax.numpy as jnp
        import numpy as np
        NUM_HEADS = 16
        HIDDEN = 256
        HEAD = HIDDEN // NUM_HEADS
        key = jax.random.key(seed)
        k1, k2 = jax.random.split(key)
        embeddings = jax.random.normal(k1, (4, 512, HIDDEN), dtype=jnp.float32)
        w_qkv = jax.random.normal(k2, (HIDDEN, 3 * HIDDEN), dtype=jnp.float32) * (1.0 / np.sqrt(HIDDEN))
        return {'embeddings': embeddings, 'w_qkv': w_qkv}
    _L1_attn_all = _L1_attn_setup()
    _L1_attn_in = {k: v for k, v in _L1_attn_all.items() if k in ('w_qkv',)}
    del _L1_attn_all

    def _L1_xattn_setup():
        import jax, jax.numpy as jnp
        import numpy as np
        HID, NH, TOPK = (256, 16, 32)
        HD = HID // NH
        SCALE = float(np.sqrt(HD))

        def _split_heads(x, B, L):
            return x.reshape(B, L, NH, HD).transpose(0, 2, 1, 3)
        key = jax.random.key(seed)
        ks = jax.random.split(key, 12)
        B, Q, KV = (2, 512, 1024)
        s = 0.02
        return {'query': jax.random.normal(ks[0], (B, Q, HID), jnp.float32), 'key': jax.random.normal(ks[1], (B, KV, HID), jnp.float32), 'value': jax.random.normal(ks[2], (B, KV, HID), jnp.float32), 'Wq': jax.random.normal(ks[3], (HID, HID), jnp.float32) * s, 'bq': jnp.zeros((HID,), jnp.float32), 'Wk': jax.random.normal(ks[4], (HID, HID), jnp.float32) * s, 'bk': jnp.zeros((HID,), jnp.float32), 'Wv': jax.random.normal(ks[5], (HID, HID), jnp.float32) * s, 'bv': jnp.zeros((HID,), jnp.float32), 'Wo': jax.random.normal(ks[6], (HID, HID), jnp.float32) * s, 'bo': jnp.zeros((HID,), jnp.float32)}
    _L1_xattn_all = _L1_xattn_setup()
    _L1_xattn_in = {k: v for k, v in _L1_xattn_all.items() if k in ('Wq', 'bq', 'Wk', 'bk', 'Wv', 'bv', 'Wo', 'bo')}
    del _L1_xattn_all

    def _L1_ffn_setup():
        import jax, jax.numpy as jnp
        import numpy as np
        B, T, D, E, H, K = (2, 512, 256, 8, 1024, 2)
        key = jax.random.key(seed)
        ks = jax.random.split(key, 8)
        s = 0.02
        return {'x': jax.random.normal(ks[0], (B, T, D), jnp.float32), 'rw1': jax.random.normal(ks[1], (D, D), jnp.float32) * s, 'rb1': jnp.zeros((D,), jnp.float32), 'rw2': jax.random.normal(ks[2], (D, E), jnp.float32) * s, 'rb2': jnp.zeros((E,), jnp.float32), 'we1': jax.random.normal(ks[3], (E, D, H), jnp.float32) * s, 'be1': jnp.zeros((E, H), jnp.float32), 'we2': jax.random.normal(ks[4], (E, H, D), jnp.float32) * s, 'be2': jnp.zeros((E, D), jnp.float32)}
    _L1_ffn_all = _L1_ffn_setup()
    _L1_ffn_in = {k: v for k, v in _L1_ffn_all.items() if k in ('rw1', 'rb1', 'rw2', 'rb2', 'we1', 'be1', 'we2', 'be2')}
    del _L1_ffn_all
    return {'x': x, 'ctx_1024': ctx_1024, 'L0_attn_in_proj': _L0_attn_in['in_proj'], 'L0_attn_out_proj': _L0_attn_in['out_proj'], 'L0_attn_frequencies': _L0_attn_in['frequencies'], 'L0_attn_decays': _L0_attn_in['decays'], 'L0_attn_ss_W': _L0_attn_in['ss_W'], 'L0_attn_ss_b': _L0_attn_in['ss_b'], 'L0_attn_gate_W': _L0_attn_in['gate_W'], 'L0_attn_gate_b': _L0_attn_in['gate_b'], 'L0_attn_fin_W': _L0_attn_in['fin_W'], 'L0_attn_fin_b': _L0_attn_in['fin_b'], 'L0_xattn_Wq': _L0_xattn_in['Wq'], 'L0_xattn_Wk': _L0_xattn_in['Wk'], 'L0_xattn_Wv': _L0_xattn_in['Wv'], 'L0_xattn_Wo': _L0_xattn_in['Wo'], 'L0_ffn_w_up': _L0_ffn_in['w_up'], 'L0_ffn_w_down': _L0_ffn_in['w_down'], 'L0_ffn_b_up': _L0_ffn_in['b_up'], 'L0_ffn_b_down': _L0_ffn_in['b_down'], 'L0_ffn_w_router': _L0_ffn_in['w_router'], 'L1_attn_w_qkv': _L1_attn_in['w_qkv'], 'L1_xattn_Wq': _L1_xattn_in['Wq'], 'L1_xattn_bq': _L1_xattn_in['bq'], 'L1_xattn_Wk': _L1_xattn_in['Wk'], 'L1_xattn_bk': _L1_xattn_in['bk'], 'L1_xattn_Wv': _L1_xattn_in['Wv'], 'L1_xattn_bv': _L1_xattn_in['bv'], 'L1_xattn_Wo': _L1_xattn_in['Wo'], 'L1_xattn_bo': _L1_xattn_in['bo'], 'L1_ffn_rw1': _L1_ffn_in['rw1'], 'L1_ffn_rb1': _L1_ffn_in['rb1'], 'L1_ffn_rw2': _L1_ffn_in['rw2'], 'L1_ffn_rb2': _L1_ffn_in['rb2'], 'L1_ffn_we1': _L1_ffn_in['we1'], 'L1_ffn_be1': _L1_ffn_in['be1'], 'L1_ffn_we2': _L1_ffn_in['we2'], 'L1_ffn_be2': _L1_ffn_in['be2']}

def reference(x, ctx_1024, L0_attn_in_proj, L0_attn_out_proj, L0_attn_frequencies, L0_attn_decays, L0_attn_ss_W, L0_attn_ss_b, L0_attn_gate_W, L0_attn_gate_b, L0_attn_fin_W, L0_attn_fin_b, L0_xattn_Wq, L0_xattn_Wk, L0_xattn_Wv, L0_xattn_Wo, L0_ffn_w_up, L0_ffn_w_down, L0_ffn_b_up, L0_ffn_b_down, L0_ffn_w_router, L1_attn_w_qkv, L1_xattn_Wq, L1_xattn_bq, L1_xattn_Wk, L1_xattn_bk, L1_xattn_Wv, L1_xattn_bv, L1_xattn_Wo, L1_xattn_bo, L1_ffn_rw1, L1_ffn_rb1, L1_ffn_rw2, L1_ffn_rb2, L1_ffn_we1, L1_ffn_be1, L1_ffn_we2, L1_ffn_be2):
    import jax
    import jax.numpy as jnp

    def _L0_attn_ref(x, in_proj, out_proj, frequencies, decays, ss_W, ss_b, gate_W, gate_b, fin_W, fin_b):
        import jax, jax.numpy as jnp
        import numpy as np
        SCALING = 1.0
        B, L, H = x.shape
        fft_len = 2 * L - 1
        freqs = frequencies * (2.0 * jnp.pi * SCALING)
        dec = -jnp.exp(decays) * SCALING
        lam = dec + 1j * freqs
        kernel = jnp.exp(lam[None, :] * jnp.arange(L, dtype=jnp.float32)[:, None])
        k = jnp.einsum('hn,kn,nh->hk', in_proj.astype(kernel.dtype), kernel, out_proj.astype(kernel.dtype)).real
        u = jnp.transpose(x, (0, 2, 1))
        u_f = jnp.fft.fft(u, n=fft_len, axis=-1)
        k_f = jnp.fft.fft(k, n=fft_len, axis=-1)
        conv = jnp.fft.ifft(u_f * k_f[None], axis=-1)[:, :, :L].real
        ss_out = jnp.transpose(conv, (0, 2, 1))
        ss_out = jax.nn.gelu(ss_out @ ss_W.T + ss_b, approximate=False)
        gate = jax.nn.gelu(x @ gate_W.T + gate_b, approximate=False)
        return gate * ss_out @ fin_W.T + fin_b

    def _L0_xattn_ref(q, k, v, Wq, Wk, Wv, Wo):
        import jax, jax.numpy as jnp
        import numpy as np
        D_MODEL = 256
        NUM_HEADS = 16
        D_K = D_MODEL // NUM_HEADS

        def _split_heads(x):
            B, S, _ = x.shape
            return x.reshape(B, S, NUM_HEADS, D_K).transpose(0, 2, 1, 3)
        B, S, _ = q.shape
        qh = _split_heads(q @ Wq.T)
        kh = _split_heads(k @ Wk.T)
        vh = _split_heads(v @ Wv.T)
        scores = jnp.einsum('bhqd,bhkd->bhqk', qh, kh) / np.sqrt(D_K).astype(np.float32)
        causal = jnp.tril(jnp.ones((S, S), dtype=bool))
        scores = jnp.where(causal, scores, -jnp.inf)
        attn = jax.nn.softmax(scores, axis=-1)
        out = jnp.einsum('bhqk,bhkd->bhqd', attn, vh)
        out = out.transpose(0, 2, 1, 3).reshape(B, S, D_MODEL)
        return out @ Wo.T

    def _L0_ffn_ref(x, w_up, w_down, b_up, b_down, w_router):
        import jax, jax.numpy as jnp
        import numpy as np
        TOP_K = 2
        logits = jnp.einsum('bsd,ed->bse', x, w_router)
        top_vals, top_idx = jax.lax.top_k(logits, TOP_K)
        router_weights = jax.nn.softmax(top_vals, axis=-1)
        up = jnp.einsum('eud,bsd->bseu', w_up, x) + b_up
        h = jax.nn.gelu(up, approximate=False)
        down = jnp.einsum('edu,bseu->bsed', w_down, h) + b_down
        sel = jnp.take_along_axis(down, top_idx[..., None], axis=2)
        return jnp.einsum('bskd,bsk->bsd', sel, router_weights)

    def _L1_attn_ref(embeddings, w_qkv):
        import jax, jax.numpy as jnp
        import numpy as np
        NUM_HEADS = 16
        HIDDEN = 256
        HEAD = HIDDEN // NUM_HEADS
        b, s, h = embeddings.shape
        result = embeddings @ w_qkv
        result = result.reshape(b, s, 3, NUM_HEADS, HEAD)
        q = jnp.transpose(result[:, :, 0], (0, 2, 1, 3))
        k = jnp.transpose(result[:, :, 1], (0, 2, 1, 3))
        v = jnp.transpose(result[:, :, 2], (0, 2, 1, 3))
        scores = jnp.einsum('bnqd,bnkd->bnqk', q, k) / jnp.sqrt(jnp.float32(h))
        probs = jax.nn.softmax(scores, axis=-1)
        ctx = jnp.einsum('bnqk,bnkd->bnqd', probs, v)
        out = jnp.transpose(ctx, (0, 2, 1, 3)).reshape(b, s, h)
        return out

    def _L1_xattn_ref(query, key, value, Wq, bq, Wk, bk, Wv, bv, Wo, bo):
        import jax, jax.numpy as jnp
        import numpy as np
        HID, NH, TOPK = (256, 16, 32)
        HD = HID // NH
        SCALE = float(np.sqrt(HD))

        def _split_heads(x, B, L):
            return x.reshape(B, L, NH, HD).transpose(0, 2, 1, 3)
        B, Q, _ = query.shape
        KV = key.shape[1]
        q = _split_heads(query @ Wq.T + bq, B, Q)
        k = _split_heads(key @ Wk.T + bk, B, KV)
        v = _split_heads(value @ Wv.T + bv, B, KV)
        scores = jnp.einsum('bhqd,bhkd->bhqk', q, k) / SCALE
        eff_k = min(TOPK, KV)
        top_scores, top_idx = jax.lax.top_k(scores, eff_k)
        w = jax.nn.softmax(top_scores, axis=-1)
        top_v = jnp.take_along_axis(v[:, :, None, :, :], top_idx[..., None], axis=3)
        out = jnp.einsum('bhqk,bhqkd->bhqd', w, top_v)
        out = out.transpose(0, 2, 1, 3).reshape(B, Q, HID)
        return out @ Wo.T + bo

    def _L1_ffn_ref(x, rw1, rb1, rw2, rb2, we1, be1, we2, be2):
        import jax, jax.numpy as jnp
        import numpy as np
        B, T, D, E, H, K = (2, 512, 256, 8, 1024, 2)
        b, t, d = x.shape
        xt = x.reshape(b * t, d)
        n = xt.shape[0]
        logits = jax.nn.silu(xt @ rw1 + rb1) @ rw2 + rb2
        _, idx = jax.lax.top_k(logits, K)
        mask = jnp.zeros((n, E), bool).at[jnp.arange(n)[:, None], idx].set(True)
        w = jax.nn.softmax(jnp.where(mask, logits, -jnp.inf), axis=1)
        h = jax.nn.silu(jnp.einsum('nd,edh->enh', xt, we1) + be1[:, None, :])
        eo = jnp.einsum('enh,ehd->end', h, we2) + be2[:, None, :]
        y = xt + jnp.einsum('ne,end->nd', w, eo)
        return y.reshape(b, t, d)
    x = _layernorm(x + _L0_attn_ref(x, L0_attn_in_proj, L0_attn_out_proj, L0_attn_frequencies, L0_attn_decays, L0_attn_ss_W, L0_attn_ss_b, L0_attn_gate_W, L0_attn_gate_b, L0_attn_fin_W, L0_attn_fin_b), axis=-1)
    x = _layernorm(x + _L0_xattn_ref(x, ctx_1024, ctx_1024, L0_xattn_Wq, L0_xattn_Wk, L0_xattn_Wv, L0_xattn_Wo), axis=-1)
    x = _layernorm(x + _L0_ffn_ref(x, L0_ffn_w_up, L0_ffn_w_down, L0_ffn_b_up, L0_ffn_b_down, L0_ffn_w_router), axis=-1)
    x = _layernorm(x + _L1_attn_ref(x, L1_attn_w_qkv), axis=-1)
    x = _layernorm(x + _L1_xattn_ref(x, ctx_1024, ctx_1024, L1_xattn_Wq, L1_xattn_bq, L1_xattn_Wk, L1_xattn_bk, L1_xattn_Wv, L1_xattn_bv, L1_xattn_Wo, L1_xattn_bo), axis=-1)
    x = _layernorm(x + _L1_ffn_ref(x, L1_ffn_rw1, L1_ffn_rb1, L1_ffn_rw2, L1_ffn_rb2, L1_ffn_we1, L1_ffn_be1, L1_ffn_we2, L1_ffn_be2), axis=-1)
    return x

_drawn_inputs = setup_inputs


def setup_inputs(seed=0):
    import zlib

    import numpy as np

    out = dict(_drawn_inputs(seed))
    spreads = {'L0_attn_decays': (-0.6931471824645996, 0.2),
     'L1_xattn_bq': (0.0, 0.494),
     'L1_xattn_bk': (0.0, 0.8),
     'L1_xattn_bv': (0.0, 0.1),
     'L1_xattn_bo': (0.0, 0.1),
     'L1_ffn_rb1': (0.0, 0.8),
     'L1_ffn_rb2': (0.0, 0.1),
     'L1_ffn_be1': (0.0, 0.675),
     'L1_ffn_be2': (0.0, 0.1)}
    factors = {'L0_attn_ss_b': 4.413, 'L0_ffn_b_down': 8.0, 'L1_ffn_rw1': 4.943, 'L1_ffn_rw2': 3.872}
    for name, (base, spread) in spreads.items():
        noise = np.random.default_rng([zlib.crc32(name.encode()), seed]).standard_normal(out[name].shape)
        drawn = base * np.exp(spread * noise) if base else spread * noise
        out[name] = jnp.asarray(drawn.astype(out[name].dtype))
    for name, factor in factors.items():
        out[name] = (out[name] * factor).astype(out[name].dtype)
    return out
```

```python
from contextlib import ExitStack

import numpy as np

import concourse.bass as bass
from concourse import mybir

F32 = mybir.dt.float32
BF16 = mybir.dt.bfloat16
I32 = mybir.dt.int32
U32 = mybir.dt.uint32
ALU = mybir.AluOpType
ACT = mybir.ActivationFunctionType
AX = mybir.AxisListType

P = 128
B, S, D = 8, 256, 256
N = B * S
NT = N // P
QT = S // P
KC = D // P
NH, DK = 16, 16
HP = NH // 2
VW = DK + 1
STATES = 64
FFT = 2 * S
NF = FFT // P
E, U, TOPK = 8, 1024, 2
UC = U // P
ROUTED = N * TOPK // P + E - 1
KEPT = 32
EPS = 1e-5
NEG = -3.0e38
STEP = 16


class Core:

    def __init__(self, nc, stack):
        self.nc = nc
        self.stack = stack
        self.sems = []
        stack.callback(self.clear)

    def clear(self):
        if self.sems:
            self.nc.clear_and_free_semaphores(self.sems)
            self.nc.all_engine_barrier()

    def sb(self, name, shape, dtype=F32):
        return self.stack.enter_context(self.nc.sbuf_tensor(name, shape, dtype))

    def ps(self, name, shape=(P, 512), dtype=F32):
        return self.stack.enter_context(self.nc.psum_tensor(name, list(shape), dtype))

    def sem(self, name):
        self.sems.append(self.nc.alloc_semaphore(name))
        return self.sems[-1]


def fold(ap, n):
    return ap.rearrange("p (n c) -> p n c", n=n)


def spread(ap, n, axis):
    shape = list(ap.shape)
    shape.insert(axis, n)
    return ap.unsqueeze(axis).broadcast_to(shape)


def batch_of(x_all, i):
    step = QT * D // STEP
    return x_all[:, bass.ds(i * step, QT * D)]


def tile_of(x_all, i, qt):
    step = QT * D // STEP
    return x_all[:, bass.ds(i * step + qt * D, D)]


def wait_reuse(engine, sem, value):
    if not (isinstance(value, int) and value == 0):
        engine.wait_ge(sem, value)


def each_batch(engine, body, last=(B - 1) * STEP):
    body(0)
    with engine.Fori(STEP, last + 1, STEP) as i:
        body(i)


class Norm:

    def __init__(self, core, tag):
        self.y = core.sb(f"{tag}_y", [P, QT, D])
        self.stats = core.sb(f"{tag}_stats", [P, QT, 6])
        self.moments = core.sb(f"{tag}_moments", [P, QT, 2])
        self.var = core.sb(f"{tag}_var", [P, QT])
        self.rstd = core.sb(f"{tag}_rstd", [P, QT])
        self.summed = core.sem(f"{tag}_summed")
        self.stats_ready = core.sem(f"{tag}_stats_ready")
        self.moments_ready = core.sem(f"{tag}_moments_ready")
        self.var_ready = core.sem(f"{tag}_var_ready")
        self.rstd_ready = core.sem(f"{tag}_rstd_ready")
        self.done = core.sem(f"{tag}_done")
        self.carrier = core.sem(f"{tag}_norm_carrier")

    def vector_moments(self, nc, dve, i):
        dve.wait_ge(self.summed, i + STEP)
        for qt in range(QT):
            last = nc.vector.bn_stats(self.stats[:, qt, :], self.y[:, qt, :])
        last.then_inc(self.stats_ready, STEP)
        dve.wait_ge(self.stats_ready, i + STEP)
        dve.sem_inc(self.carrier, 1)
        for qt in range(QT):
            last = nc.vector.bn_aggr(self.moments[:, qt, :], self.stats[:, qt, :])
        last.then_inc(self.moments_ready, STEP)

    def pool_rstd(self, nc, pool, i, minus_half):
        pool.wait_ge(self.moments_ready, i + STEP)
        nc.gpsimd.tensor_scalar(self.var[:, :], self.moments[:, :, 1], EPS, None, ALU.add)\
            .then_inc(self.var_ready, STEP)
        pool.wait_ge(self.var_ready, i + STEP)
        nc.gpsimd.tensor_tensor(self.rstd[:, :], self.var[:, :], minus_half[:, 0:QT], ALU.pow)\
            .then_inc(self.rstd_ready, STEP)

    def vector_scale(self, nc, dve, i, x_all):
        dve.wait_ge(self.rstd_ready, i + STEP)
        for qt in range(QT):
            last = nc.vector.tensor_scalar(tile_of(x_all, i, qt), self.y[:, qt, :],
                                           self.moments[:, qt, 0:1], self.rstd[:, qt:qt + 1],
                                           ALU.subtract, ALU.mult)
        last.then_inc(self.done, STEP)


def kernel_spectrum(nc, a, g, mx, load_rest):
    with ExitStack() as stack:
        core = Core(nc, stack)
        lag = core.sb("lag", [STATES, S])
        mode = core.sb("mode", [STATES, 6])
        w_in = core.sb("w_in", [STATES, D])
        w_out = core.sb("w_out", [STATES, D])
        w = core.sb("w", [STATES, D])
        damp = core.sb("damp", [STATES, S])
        phase = core.sb("phase", [STATES, S])
        turns = core.sb("turns", [STATES, 2, S])
        rest = core.sb("rest", [STATES, 3, S])
        mag = core.sb("mag", [STATES, 2, S])
        half_pi = core.sb("half_pi", [STATES, 1])
        wave = core.sb("wave", [STATES, S])
        decay_env = core.sb("decay_env", [STATES, S])
        modes = core.sb("modes", [STATES, S])
        k_time = core.sb("k_time", [P, QT, D])
        const = core.sb("const", [P, 3 * P + 2 + ROUTED])
        k_ps = core.ps("k_ps")
        re_ps = core.ps("re_ps")
        im_ps = core.ps("im_ps")
        loaded = core.sem("p0_loaded")
        decayed = core.sem("p0_decayed")
        v = core.sem("p0_vector_step")
        waved = core.sem("p0_waved")
        k_done = core.sem("p0_k_done")
        k_copied = core.sem("p0_k_copied")
        spec_done = core.sem("p0_spec_done")

        with nc.Block() as block:

            @block.sync
            def _(sp):
                sp.dma_start(mode[:, 0:1], a["decays"]).then_inc(loaded, 16)
                sp.dma_start(mode[:, 1:2], a["frequencies"]).then_inc(loaded, 16)
                sp.dma_start(lag[:, :], a["lag"]).then_inc(loaded, 16)
                sp.dma_start(w_in[:, :], a["in_projT"]).then_inc(loaded, 16)
                sp.dma_start(w_out[:, :], a["out_proj"]).then_inc(loaded, 16)
                sp.dma_start(const[:, :], a["const"]).then_inc(g.const_loaded, 16)
                sp.dma_start(fold(g.x_all[:, :], NT), a["x"].rearrange("(t p) c -> p t c", p=P))\
                    .then_inc(g.x_loaded, 16)
                load_rest(sp)

            @block.scalar
            def _(act):
                act.wait_ge(loaded, 5 * 16)
                nc.scalar.activation(mode[:, 2:3], mode[:, 0:1], ACT.Exp).then_inc(decayed, 1)
                act.wait_ge(v, 2)
                nc.scalar.activation(decay_env[:, :], damp[:, :], ACT.Exp, scale=-1.0)\
                    .then_inc(decayed, 1)
                act.wait_ge(v, 12)
                nc.scalar.activation(wave[:, :], mag[:, 1, :], ACT.Sin, bias=half_pi[:, 0:1], scale=-1.0)\
                    .then_inc(waved, 1)
                for t in range(QT):
                    act.wait_ge(k_done, QT)
                    nc.scalar.activation(k_time[:, t, :], k_ps[:, t * D:(t + 1) * D], ACT.Copy)\
                        .then_inc(k_copied, 1)

            @block.vector
            def _(dve):
                def step(instruction, n):
                    instruction.then_inc(v, 1)
                    dve.wait_ge(v, n)

                nc.vector.memset(half_pi[:, :], float(np.pi / 2)).then_inc(v, 1)
                dve.wait_ge(decayed, 1)
                nc.vector.tensor_scalar(damp[:, :], lag[:, :], mode[:, 2:3], None, ALU.mult)\
                    .then_inc(v, 1)
                step(nc.vector.tensor_scalar(mode[:, 3:4], mode[:, 1:2], float(np.float32(2 * np.pi)),
                                             None, ALU.mult), 3)
                step(nc.vector.tensor_scalar(phase[:, :], lag[:, :], mode[:, 3:4], None, ALU.mult), 4)
                step(nc.vector.tensor_scalar(turns[:, 0, :], phase[:, :], float(1 / (2 * np.pi)),
                                             None, ALU.mult), 5)
                step(nc.vector.tensor_scalar(turns[:, 1, :], turns[:, 0, :], 12582912.0, None, ALU.add), 6)
                step(nc.vector.tensor_scalar(turns[:, 0, :], turns[:, 1, :], -12582912.0, None, ALU.add), 7)
                part1 = 6.28125
                part2 = float(np.round((2 * np.pi - part1) * 2.0**17) / 2.0**17)
                part3 = float(2 * np.pi - part1 - part2)
                step(nc.vector.scalar_tensor_tensor(rest[:, 0, :], turns[:, 0, :], -part1, phase[:, :],
                                                    ALU.mult, ALU.add), 8)
                step(nc.vector.scalar_tensor_tensor(rest[:, 1, :], turns[:, 0, :], -part2, rest[:, 0, :],
                                                    ALU.mult, ALU.add), 9)
                step(nc.vector.scalar_tensor_tensor(rest[:, 2, :], turns[:, 0, :], -part3, rest[:, 1, :],
                                                    ALU.mult, ALU.add), 10)
                step(nc.vector.tensor_scalar(mag[:, 0, :], rest[:, 2, :], -1.0, None, ALU.mult), 11)
                nc.vector.tensor_tensor(mag[:, 1, :], rest[:, 2, :], mag[:, 0, :], ALU.max).then_inc(v, 1)
                nc.vector.tensor_tensor(w[:, :], w_in[:, :], w_out[:, :], ALU.mult)
                dve.wait_ge(waved, 1)
                dve.wait_ge(decayed, 2)
                nc.vector.tensor_tensor(modes[:, :], wave[:, :], decay_env[:, :], ALU.mult).then_inc(v, 1)
                dve.wait_ge(spec_done, 1)
                half = KC * D
                nc.vector.tensor_copy(mx.spec_re[:, :], re_ps[:, 0:half])
                nc.vector.tensor_copy(mx.spec_re2[:, :], re_ps[:, 0:half])
                nc.vector.tensor_copy(mx.spec_im[:, :], im_ps[:, 0:half]).then_inc(v, 1)
                dve.wait_ge(v, 14)
                nc.vector.tensor_copy(mx.spec_re2[0:1, 0:D], im_ps[0:1, 0:D])
                nc.vector.memset(mx.spec_im[0:1, 0:D], 0.0)

            @block.tensor
            def _(pe):
                pe.wait_ge(v, 13)
                for t in range(QT):
                    nc.tensor.matmul(k_ps[:, t * D:(t + 1) * D], modes[:, t * P:(t + 1) * P], w[:, :],
                                     start=True, stop=True).then_inc(k_done, 1)
                pe.wait_ge(k_copied, QT)
                pe.wait_ge(mx.dft_loaded, 16)
                for f in range(NF):
                    out = (re_ps, im_ps)[f // 2][:, (f % 2) * D:(f % 2 + 1) * D]
                    for t in range(QT):
                        last = nc.tensor.matmul(out, mx.dft[:, t * FFT + f * P:t * FFT + (f + 1) * P],
                                                k_time[:, t, :], start=t == 0, stop=t == QT - 1)
                last.then_inc(spec_done, 1)

            @block.gpsimd
            def _(pool):
                nc.gpsimd.memset(g.zeros[:, :], 0.0).then_inc(g.zero_ready, 1)
                nc.gpsimd.memset(g.minus_half[:, :], -0.5)
                nc.gpsimd.memset(g.ones16[:, :], 1.0)
                pool.wait_ge(g.const_loaded, 16)
                nc.gpsimd.tensor_copy(g.ident[:, :], const[:, 0:P])
                nc.gpsimd.tensor_copy(g.ident16[:, :], const[:, 0:P])
                nc.gpsimd.tensor_copy(g.before16[:, :], const[:, P:2 * P])
                for h in range(2):
                    nc.gpsimd.tensor_copy(g.causal16[:, h, :], const[:, 2 * P:3 * P])
                nc.gpsimd.tensor_copy(g.pair_mask[:, :], const[:, 3 * P:3 * P + 2])
                nc.gpsimd.tensor_copy(g.iota[:, :], const[:, 3 * P + 2:])


def mixer_phase(nc, a, g, mx):
    with ExitStack() as stack:
        core = Core(nc, stack)
        xb = core.sb("m_xb", [P, QT, D])
        xT = core.sb("m_xT", [P, KC, S])
        prod = core.sb("m_prod", [P, 4, KC * D])
        yf = core.sb("m_yf", [P, NF, D])
        yT = core.sb("m_yT", [P, KC, S])
        ssT = core.sb("m_ssT", [P, KC, S])
        gateT = core.sb("m_gateT", [P, KC, S])
        mixT = core.sb("m_mixT", [P, KC, S])
        xr = core.sb("m_xr", [P, QT, D])
        norm = Norm(core, "m")
        ps_xT, ps_re, ps_im, ps_gate, ps_y, ps_ss, ps_out = (core.ps(f"m_ps{n}") for n in range(7))
        xb_ready, xT_ps, xT_ready, u_ps, prod_ready, yf_ready = (
            core.sem(f"m_{n}") for n in ("xb_ready", "xT_ps", "xT_ready", "u_ps", "prod_ready", "yf_ready"))
        gate_ps, gate_ready, y_ps, yT_ready, ss_ps, ss_ready, mix_ready, out_ps, xr_ready = (
            core.sem(f"m_{n}") for n in ("gate_ps", "gate_ready", "y_ps", "yT_ready", "ss_ps", "ss_ready",
                                         "mix_ready", "out_ps", "xr_ready"))
        last_base = (B - 1) * STEP

        with nc.Block() as block:

            @block.gpsimd
            def _(pool):
                def take(j):
                    wait_reuse(pool, u_ps, j)
                    nc.gpsimd.tensor_copy(xb[:, :, :].rearrange("p t c -> p (t c)"), batch_of(g.x_all, j))\
                        .then_inc(xb_ready, STEP)

                def spectrum(j):
                    pool.wait_ge(prod_ready, j + STEP)
                    wait_reuse(pool, y_ps, j)
                    nc.gpsimd.tensor_tensor(yf[:, 0:KC, :], fold(prod[:, 0, :], KC), fold(prod[:, 1, :], KC),
                                            ALU.subtract)
                    nc.gpsimd.tensor_tensor(yf[:, KC:NF, :], fold(prod[:, 2, :], KC), fold(prod[:, 3, :], KC),
                                            ALU.add).then_inc(yf_ready, STEP)

                def back(i):
                    wait_reuse(pool, norm.summed, i)
                    nc.gpsimd.tensor_tensor(xr[:, :, :], fold(batch_of(g.x_all, i), QT),
                                            spread(mx.fin_b[:, :], QT, 1), ALU.add).then_inc(xr_ready, STEP)
                    pool.wait_ge(ss_ready, i + STEP)
                    pool.wait_ge(gate_ready, i + STEP)
                    wait_reuse(pool, out_ps, i)
                    nc.gpsimd.tensor_tensor(mixT[:, :, :], ssT[:, :, :], gateT[:, :, :], ALU.mult)\
                        .then_inc(mix_ready, STEP)

                pool.wait_ge(g.x_loaded, 16)
                pool.wait_ge(mx.loaded, mx.loads)
                take(0)
                spectrum(0)
                def batch(i):
                    take(i + STEP)
                    back(i)
                    spectrum(i + STEP)
                    norm.pool_rstd(nc, pool, i, g.minus_half)

                each_batch(pool, batch, last_base - STEP)
                back(last_base)
                norm.pool_rstd(nc, pool, last_base, g.minus_half)

            @block.tensor
            def _(pe):
                def front(j):
                    pe.wait_ge(xb_ready, j + STEP)
                    wait_reuse(pe, xT_ready, j)
                    for k in range(KC):
                        for t in range(QT):
                            last = nc.tensor.transpose(ps_xT[:, k * S + t * P:k * S + (t + 1) * P],
                                                       xb[:, t, k * P:(k + 1) * P], g.ident[:, :])
                    last.then_inc(xT_ps, STEP)
                    wait_reuse(pe, prod_ready, j)
                    for f in range(NF):
                        out = (ps_re, ps_im)[f // 2][:, (f % 2) * D:(f % 2 + 1) * D]
                        for t in range(QT):
                            last = nc.tensor.matmul(out, mx.dft[:, t * FFT + f * P:t * FFT + (f + 1) * P],
                                                    xb[:, t, :], start=t == 0, stop=t == QT - 1)
                    last.then_inc(u_ps, STEP)

                def gate(j):
                    pe.wait_ge(xT_ready, j + STEP)
                    wait_reuse(pe, gate_ready, j)
                    for m in range(KC):
                        for k in range(KC):
                            last = nc.tensor.matmul(ps_gate[:, m * S:(m + 1) * S],
                                                    mx.gate_w[:, k * D + m * P:k * D + (m + 1) * P],
                                                    xT[:, k, :], start=k == 0, stop=k == KC - 1)
                    last.then_inc(gate_ps, STEP)

                def inverse(i):
                    pe.wait_ge(yf_ready, i + STEP)
                    wait_reuse(pe, yT_ready, i)
                    for m in range(KC):
                        for f in range(NF):
                            last = nc.tensor.matmul(ps_y[:, m * S:(m + 1) * S], yf[:, f, m * P:(m + 1) * P],
                                                    mx.idft[:, f * S:(f + 1) * S], start=f == 0, stop=f == NF - 1)
                    last.then_inc(y_ps, STEP)

                def state(i):
                    pe.wait_ge(yT_ready, i + STEP)
                    wait_reuse(pe, ss_ready, i)
                    for m in range(KC):
                        for k in range(KC):
                            last = nc.tensor.matmul(ps_ss[:, m * S:(m + 1) * S],
                                                    mx.ss_w[:, k * D + m * P:k * D + (m + 1) * P],
                                                    yT[:, k, :], start=k == 0, stop=k == KC - 1)
                    last.then_inc(ss_ps, STEP)

                def project(i):
                    pe.wait_ge(mix_ready, i + STEP)
                    wait_reuse(pe, norm.summed, i)
                    for t in range(QT):
                        for k in range(KC):
                            last = nc.tensor.matmul(ps_out[:, t * D:(t + 1) * D], mixT[:, k, t * P:(t + 1) * P],
                                                    mx.fin_w[:, k * D:(k + 1) * D], start=k == 0, stop=k == KC - 1)
                    last.then_inc(out_ps, STEP)

                pe.wait_ge(mx.loaded, mx.loads)
                front(0)
                gate(0)
                def batch(i):
                    inverse(i)
                    front(i + STEP)
                    state(i)
                    gate(i + STEP)
                    project(i)

                each_batch(pe, batch, last_base - STEP)
                inverse(last_base)
                state(last_base)
                project(last_base)

            @block.scalar
            def _(act):
                def take(j):
                    act.wait_ge(xT_ps, j + STEP)
                    wait_reuse(act, gate_ps, j)
                    nc.scalar.activation(xT[:, :, :], fold(ps_xT[:, :], KC), ACT.Copy).then_inc(xT_ready, STEP)

                def gate(j):
                    act.wait_ge(gate_ps, j + STEP)
                    wait_reuse(act, mix_ready, j)
                    for m in range(KC):
                        last = nc.scalar.activation(gateT[:, m, :], ps_gate[:, m * S:(m + 1) * S], ACT.Gelu,
                                                    bias=mx.gate_b[:, m:m + 1])
                    last.then_inc(gate_ready, STEP)

                def back(i):
                    act.wait_ge(y_ps, i + STEP)
                    wait_reuse(act, ss_ps, i)
                    nc.scalar.activation(yT[:, :, :], fold(ps_y[:, :], KC), ACT.Copy).then_inc(yT_ready, STEP)

                def state(i):
                    act.wait_ge(ss_ps, i + STEP)
                    wait_reuse(act, mix_ready, i)
                    for m in range(KC):
                        last = nc.scalar.activation(ssT[:, m, :], ps_ss[:, m * S:(m + 1) * S], ACT.Gelu,
                                                    bias=mx.ss_b[:, m:m + 1])
                    last.then_inc(ss_ready, STEP)

                take(0)
                gate(0)
                def batch(i):
                    back(i)
                    take(i + STEP)
                    state(i)
                    gate(i + STEP)

                each_batch(act, batch, last_base - STEP)
                back(last_base)
                state(last_base)

            @block.vector
            def _(dve):
                def spectrum(j):
                    dve.wait_ge(u_ps, j + STEP)
                    wait_reuse(dve, yf_ready, j)
                    nc.vector.tensor_tensor(prod[:, 0, :], ps_re[:, :], mx.spec_re[:, :], ALU.mult)
                    nc.vector.tensor_tensor(prod[:, 1, :], ps_im[:, :], mx.spec_im[:, :], ALU.mult)
                    nc.vector.tensor_tensor(prod[:, 2, :], ps_re[:, :], mx.spec_im[:, :], ALU.mult)
                    nc.vector.tensor_tensor(prod[:, 3, :], ps_im[:, :], mx.spec_re2[:, :], ALU.mult)\
                        .then_inc(prod_ready, STEP)

                def back(i):
                    dve.wait_ge(out_ps, i + STEP)
                    dve.wait_ge(xr_ready, i + STEP)
                    wait_reuse(dve, norm.done, i)
                    nc.vector.tensor_tensor(norm.y[:, :, :], fold(ps_out[:, :], QT), xr[:, :, :], ALU.add)\
                        .then_inc(norm.summed, STEP)
                    norm.vector_moments(nc, dve, i)
                    norm.vector_scale(nc, dve, i, g.x_all)

                spectrum(0)
                def batch(i):
                    spectrum(i + STEP)
                    back(i)

                each_batch(dve, batch, last_base - STEP)
                back(last_base)


def attention_phase(nc, a, g, tag, w, *, cross, causal, top, project, scale,
                    loads=()):
    UNITS = QT * HP
    HALF = UNITS // QT
    with ExitStack() as stack:
        core = Core(nc, stack)
        xb = core.sb(f"{tag}_xb", [P, QT, D])
        xT = core.sb(f"{tag}_xT", [P, KC, S])
        cT = core.sb(f"{tag}_cT", [P, KC, S]) if cross else xT
        qT = core.sb(f"{tag}_qT", [P, KC, S])
        kz = core.sb(f"{tag}_kz", [P, KC, 2, S])
        val = core.sb(f"{tag}_val", [P, QT, NH, VW])
        prob = core.sb(f"{tag}_prob", [P, 2, 2, S])
        probT = core.sb(f"{tag}_probT", [P, 2, 2, QT, P])
        ctx = core.sb(f"{tag}_ctx", [P, QT, D])
        sums = core.sb(f"{tag}_sums", [P, QT, NH])
        top8 = core.sb(f"{tag}_top8", [P, 2, 2, 4, 8]) if top else None
        neg_max = core.sb(f"{tag}_neg_max", [P, 4, 2])
        scores = core.sb(f"{tag}_scores", [P, 2, 2, S]) if top else None
        rest = core.sb(f"{tag}_rest", [P, 2, 2, 2, S]) if top else None
        kept = core.sb(f"{tag}_kept", [P, 2, 2, S]) if top else None
        ctxT = core.sb(f"{tag}_ctxT", [P, QT, KC, P]) if project else None
        xr = core.sb(f"{tag}_xr", [P, QT, D]) if project else None
        bq = core.sb(f"{tag}_bq_scaled", [P, KC]) if w.bq is not None else None
        carrier = core.sem(f"{tag}_carrier")
        bq_ready = core.sem(f"{tag}_bq_ready")
        norm = Norm(core, tag)
        s_bank = [core.ps(f"{tag}_s{n}") for n in range(2)]
        t_bank = [core.ps(f"{tag}_t{n}") for n in range(2)]
        o_bank = [core.ps(f"{tag}_o{n}") for n in range(QT)]
        j_bank = [core.ps(f"{tag}_j{n}") for n in range(2)]
        names = ("xb_ready cT_loaded xT_ps xT_ready q_ps q_ready k_ps k_ready v_ps v_ready s_ps s_read "
                 "max_ready topk_ready top_step neg_ready kept_ready dropped_ready p_ready tp_ps "
                 "pt_ready av_ps sums_ready ctx_ready ctxT_ps ctxT_ready o_ps xr_ready ones_ready").split()
        (xb_ready, cT_loaded, xT_ps, xT_ready, q_ps, q_ready, k_ps, k_ready, v_ps, v_ready, s_ps, s_read,
         max_ready, topk_ready, top_step, neg_ready, kept_ready, dropped_ready, p_ready, tp_ps,
         pt_ready, av_ps, sums_ready, ctx_ready, ctxT_ps, ctxT_ready, o_ps, xr_ready, ones_ready) = (
            core.sem(f"{tag}_{n}") for n in names)
        if not top:
            s_read = p_ready
        last_base = (B - 1) * STEP
        per_qt = STEP // QT

        def keys(qt):
            return qt + 1 if causal else QT

        def pair(hp):
            return hp // 4, slice(32 * (hp % 4), 32 * (hp % 4) + 32)

        with nc.Block() as block:

            @block.sync
            def _(sp):
                def load(j):
                    wait_reuse(sp, v_ps, j)
                    b_rows = KC * P // STEP
                    src = a["ctxT"][bass.ds(j * b_rows, KC * P), :]
                    sp.dma_start(cT[:, :, :], src.rearrange("(k p) s -> p k s", p=P)).then_inc(cT_loaded, 16)

                for load_more in loads:
                    load_more(sp)
                if cross:
                    each_batch(sp, load)

            @block.gpsimd
            def _(pool):
                def take(j):
                    wait_reuse(pool, xT_ps, j)
                    nc.gpsimd.tensor_copy(xb[:, :, :].rearrange("p t c -> p (t c)"), batch_of(g.x_all, j))\
                        .then_inc(xb_ready, STEP)

                def residual(i):
                    wait_reuse(pool, norm.summed, i)
                    if w.bo is None:
                        nc.gpsimd.tensor_copy(xr[:, :, :].rearrange("p t c -> p (t c)"),
                                              batch_of(g.x_all, i)).then_inc(xr_ready, STEP)
                    else:
                        nc.gpsimd.tensor_tensor(xr[:, :, :], fold(batch_of(g.x_all, i), QT),
                                                spread(w.bo[:, :], QT, 1), ALU.add).then_inc(xr_ready, STEP)

                def weights(i):
                    for u in range(UNITS):
                        s = u % 2
                        pool.wait_ge(dropped_ready, i + u + 1)
                        nc.gpsimd.tensor_tensor(prob[:, s, :, :], kept[:, s, :, :], prob[:, s, :, :],
                                                ALU.subtract).then_inc(p_ready, 1)

                nc.gpsimd.memset(val[:, :, :, DK:VW], 1.0).then_inc(ones_ready, 1)
                pool.wait_ge(w.loaded, w.loads)
                take(0)
                def batch(i):
                    if top:
                        weights(i)
                    take(i + STEP)
                    if project:
                        residual(i)
                    norm.pool_rstd(nc, pool, i, g.minus_half)

                each_batch(pool, batch, last_base - STEP)
                if top:
                    weights(last_base)
                if project:
                    residual(last_base)
                norm.pool_rstd(nc, pool, last_base, g.minus_half)

            @block.tensor
            def _(pe):
                def front(j, summed):
                    pe.wait_ge(xb_ready, j + STEP)
                    wait_reuse(pe, norm.summed, summed)
                    for k in range(KC):
                        for t in range(QT):
                            last = nc.tensor.transpose(j_bank[0][:, k * S + t * P:k * S + (t + 1) * P],
                                                       xb[:, t, k * P:(k + 1) * P], g.ident[:, :])
                    last.then_inc(xT_ps, STEP)
                    pe.wait_ge(xT_ready, j + STEP)
                    wait_reuse(pe, q_ready, j)
                    for m in range(KC):
                        for k in range(KC):
                            last = nc.tensor.matmul(j_bank[1][:, m * S:(m + 1) * S],
                                                    w.wq[:, k * D + m * P:k * D + (m + 1) * P],
                                                    xT[:, k, :], start=k == 0, stop=k == KC - 1)
                    last.then_inc(q_ps, STEP)
                    if cross:
                        pe.wait_ge(cT_loaded, j + STEP)
                    wait_reuse(pe, s_read, j)
                    for m in range(KC):
                        for k in range(KC):
                            last = nc.tensor.matmul(s_bank[0][:, m * S:(m + 1) * S],
                                                    w.wk[:, k * D + m * P:k * D + (m + 1) * P],
                                                    cT[:, k, :], start=k == 0, stop=k == KC - 1)
                    last.then_inc(k_ps, STEP)
                    for t in range(QT):
                        for k in range(KC):
                            last = nc.tensor.matmul(s_bank[1][:, t * D:(t + 1) * D], cT[:, k, t * P:(t + 1) * P],
                                                    w.wv[:, k * D:(k + 1) * D], start=k == 0, stop=k == KC - 1)
                    last.then_inc(v_ps, STEP)

                def score(i, u):
                    qt, hp = divmod(u, HALF)
                    m, rows = pair(hp)
                    if u == 0:
                        pe.wait_ge(q_ready, i + STEP)
                        pe.wait_ge(k_ready, i + STEP)
                    elif u == 1:
                        pe.wait_ge(v_ready, i + STEP)
                    else:
                        pe.wait_ge(s_read, i + u - 1)
                    n = keys(qt) * P
                    out = fold(s_bank[u % 2][:, :], 2)[:, :, 0:n]
                    last = nc.tensor.matmul(out, qT[rows, m, qt * P:(qt + 1) * P], kz[rows, m, :, 0:n],
                                            start=True, stop=not causal)
                    if causal:
                        last = nc.tensor.matmul(out[:, :, qt * P:(qt + 1) * P], g.ident16[:, :],
                                                g.causal16[:, :, :], start=False, stop=True)
                    last.then_inc(s_ps, 1)

                def turn(i, u):
                    qt = u // HALF
                    pe.wait_ge(p_ready, i + u + 1)
                    if u >= 2:
                        pe.wait_ge(pt_ready, i + u - 1)
                    elif project:
                        wait_reuse(pe, ctxT_ready, i)
                    for h in range(2):
                        for kt in range(keys(qt)):
                            c = (h * QT + kt) * P
                            last = nc.tensor.transpose(t_bank[u % 2][:, c:c + P],
                                                       prob[:, u % 2, h, kt * P:(kt + 1) * P], g.ident[:, :])
                    last.then_inc(tp_ps, 1)

                def gather(i, u):
                    qt, hp = divmod(u, HALF)
                    pe.wait_ge(pt_ready, i + u + 1)
                    if hp == 0:
                        wait_reuse(pe, ctx_ready, i)
                    for h in range(2):
                        head = 2 * hp + h
                        for kt in range(keys(qt)):
                            last = nc.tensor.matmul(o_bank[qt][:, head * VW:(head + 1) * VW],
                                                    probT[:, u % 2, h, kt, :], val[:, kt, head, :],
                                                    start=kt == 0, stop=kt == keys(qt) - 1)
                    last.then_inc(av_ps, 1)

                def units(i):
                    score(i, 0)
                    score(i, 1)
                    for u in range(UNITS):
                        turn(i, u)
                        if u + 2 < UNITS:
                            score(i, u + 2)
                        if u >= 1:
                            gather(i, u - 1)
                    gather(i, UNITS - 1)

                def tail(i, ahead):
                    for qt in range(QT):
                        pe.wait_ge(ctx_ready, i + (qt + 1) * per_qt)
                        for k in range(KC):
                            last = nc.tensor.transpose(t_bank[qt][:, k * P:(k + 1) * P],
                                                       ctx[:, qt, k * P:(k + 1) * P], g.ident[:, :])
                        last.then_inc(ctxT_ps, per_qt)
                    if ahead:
                        pe.wait_ge(q_ready, i + 2 * STEP)
                    for qt in range(QT):
                        pe.wait_ge(ctxT_ready, i + (qt + 1) * per_qt)
                        for k in range(KC):
                            last = nc.tensor.matmul(j_bank[qt][:, 0:D], ctxT[:, qt, k, :],
                                                    w.wo[:, k * D:(k + 1) * D], start=k == 0, stop=k == KC - 1)
                    last.then_inc(o_ps, STEP)

                pe.wait_ge(w.loaded, w.loads)
                pe.wait_ge(ones_ready, 1)
                front(0, 0)
                def batch(i):
                    units(i)
                    front(i + STEP, i)
                    if project:
                        tail(i, True)

                each_batch(pe, batch, last_base - STEP)
                units(last_base)
                if project:
                    tail(last_base, False)

            @block.scalar
            def _(act):
                if w.bq is not None:
                    act.wait_ge(w.loaded, w.loads)
                    nc.scalar.mul(bq[:, :], w.bq[:, :], scale).then_inc(bq_ready, 1)
                    act.wait_ge(bq_ready, 1)

                def front(j):
                    act.wait_ge(xT_ps, j + STEP)
                    wait_reuse(act, v_ps, j)
                    nc.scalar.activation(xT[:, :, :], fold(j_bank[0][:, :], KC), ACT.Copy)\
                        .then_inc(xT_ready, STEP)
                    act.wait_ge(q_ps, j + STEP)
                    wait_reuse(act, s_ps, j)
                    if w.bq is None:
                        last = nc.scalar.activation(qT[:, :, :], fold(j_bank[1][:, :], KC), ACT.Copy, scale=scale)
                    else:
                        for m in range(KC):
                            last = nc.scalar.activation(qT[:, m, :], j_bank[1][:, m * S:(m + 1) * S],
                                                        ACT.Identity, bias=bq[:, m:m + 1], scale=scale)
                    last.then_inc(q_ready, STEP)

                def exponentials(i, u):
                    qt = u // HALF
                    n = keys(qt) * P
                    act.wait_ge(max_ready, i + u + 1)
                    if u >= 2:
                        act.wait_ge(tp_ps, i + u - 1)
                    for h in range(2):
                        last = nc.scalar.activation(prob[:, u % 2, h, 0:n],
                                                    s_bank[u % 2][:, h * S:h * S + n], ACT.Exp,
                                                    bias=neg_max[:, u % 4, h:h + 1])
                    last.then_inc(p_ready, 1)

                def copy_scores(i, u):
                    act.wait_ge(s_ps, i + u + 1)
                    if u >= 2:
                        act.wait_ge(kept_ready, i + u - 1)
                    nc.scalar.activation(scores[:, u % 2, :, :], fold(s_bank[u % 2][:, :], 2), ACT.Copy)\
                        .then_inc(s_read, 1)

                def top_exponentials(i, u):
                    act.wait_ge(topk_ready, i + u + 1)
                    if u >= 2:
                        act.wait_ge(p_ready, i + u - 1)
                        act.wait_ge(tp_ps, i + u - 1)
                    nc.scalar.mul(neg_max[:, u % 4, :], top8[:, u % 2, :, 0, 0], -1.0).then_inc(neg_ready, 1)
                    act.wait_ge(neg_ready, i + u + 1)
                    for h in range(2):
                        last = nc.scalar.activation(kept[:, u % 2, h, :], scores[:, u % 2, h, :], ACT.Exp,
                                                    bias=neg_max[:, u % 4, h:h + 1])
                    last.then_inc(kept_ready, 1)
                    for h in range(2):
                        last = nc.scalar.activation(prob[:, u % 2, h, :], rest[:, u % 2, 1, h, :], ACT.Exp,
                                                    bias=neg_max[:, u % 4, h:h + 1])
                    last.then_inc(dropped_ready, 1)

                def turned(i, u):
                    act.wait_ge(tp_ps, i + u + 1)
                    if u >= 2:
                        act.wait_ge(av_ps, i + u - 1)
                    nc.scalar.activation(probT[:, u % 2, :, :, :].rearrange("p h k c -> p (h k c)"),
                                         t_bank[u % 2][:, :], ACT.Copy).then_inc(pt_ready, 1)

                def units(i):
                    if not top:
                        for u in range(UNITS):
                            exponentials(i, u)
                        return
                    copy_scores(i, 0)
                    for u in range(UNITS):
                        if u + 1 < UNITS:
                            copy_scores(i, u + 1)
                        top_exponentials(i, u)
                        if u >= 1:
                            turned(i, u - 1)
                    turned(i, UNITS - 1)

                def tail(i):
                    for qt in range(QT):
                        act.wait_ge(ctxT_ps, i + (qt + 1) * per_qt)
                        if qt == 0:
                            wait_reuse(act, o_ps, i)
                        nc.scalar.activation(ctxT[:, qt, :, :].rearrange("p k c -> p (k c)"),
                                             t_bank[qt][:, 0:D], ACT.Copy).then_inc(ctxT_ready, per_qt)

                front(0)
                def batch(i):
                    units(i)
                    front(i + STEP)
                    if project:
                        tail(i)

                each_batch(act, batch, last_base - STEP)
                units(last_base)
                if project:
                    tail(last_base)

            @block.vector
            def _(dve):
                def front(j):
                    dve.wait_ge(k_ps, j + STEP)
                    wait_reuse(dve, s_ps, j)
                    for h in range(2):
                        for m in range(KC):
                            src = s_bank[0][:, m * S:(m + 1) * S]
                            if w.bk is None:
                                last = nc.vector.tensor_scalar(kz[:, m, h, :], src, g.pair_mask[:, h:h + 1],
                                                               None, ALU.mult)
                            else:
                                last = nc.vector.tensor_scalar(kz[:, m, h, :], src, w.bk[:, m:m + 1],
                                                               g.pair_mask[:, h:h + 1], ALU.add, ALU.mult)
                    last.then_inc(k_ready, STEP)
                    dve.wait_ge(v_ps, j + STEP)
                    wait_reuse(dve, av_ps, j)
                    for t in range(QT):
                        src = fold(s_bank[1][:, t * D:(t + 1) * D], NH)
                        if w.bv is None:
                            last = nc.vector.tensor_copy(val[:, t, :, 0:DK], src)
                        else:
                            last = nc.vector.tensor_tensor(val[:, t, :, 0:DK], src, fold(w.bv[:, :], NH), ALU.add)
                    last.then_inc(v_ready, STEP)

                def maxima(i, u):
                    n = keys(u // HALF) * P
                    dve.wait_ge(s_ps, i + u + 1)
                    nc.vector.tensor_reduce(neg_max[:, u % 4, :], fold(s_bank[u % 2][:, :], 2)[:, :, 0:n],
                                            AX.X, ALU.max, negate=True).then_inc(max_ready, 1)

                def turned(i, u):
                    qt = u // HALF
                    dve.wait_ge(tp_ps, i + u + 1)
                    if u >= 2:
                        dve.wait_ge(av_ps, i + u - 1)
                    src = t_bank[u % 2][:, :].rearrange("p (h k c) -> p h k c", h=2, k=QT)
                    nc.vector.tensor_copy(probT[:, u % 2, :, 0:keys(qt), :], src[:, :, 0:keys(qt), :])\
                        .then_inc(pt_ready, 1)

                def select(i, u):
                    dve.wait_ge(s_read, i + u + 1)
                    if u >= 2:
                        dve.wait_ge(dropped_ready, i + u - 1)
                    dve.sem_inc(carrier, 1)
                    rounds = KEPT // 8
                    steps = 4 * rounds - 1
                    base = (i + u) * steps
                    for r in range(rounds):
                        src = [scores[:, u % 2, h, :] if r == 0 else rest[:, u % 2, (r - 1) % 2, h, :]
                               for h in range(2)]
                        for h in range(2):
                            if r > 0:
                                dve.wait_ge(top_step, base + 4 * r - 1 + h)
                                dve.sem_inc(carrier, 1)
                            nc.vector.max(top8[:, u % 2, h, r, :], src[h]).then_inc(top_step, 1)
                        for h in range(2):
                            dve.wait_ge(top_step, base + 4 * r + 1 + h)
                            dve.sem_inc(carrier, 1)
                            last = nc.vector.match_replace(rest[:, u % 2, r % 2, h, :],
                                                           top8[:, u % 2, h, r, :], src[h], NEG)
                            last.then_inc(*((top_step, 1) if (r, h) != (rounds - 1, 1) else (topk_ready, 1)))

                def normalise(i, qt):
                    dve.wait_ge(av_ps, i + (qt + 1) * per_qt)
                    heads = fold(o_bank[qt][:, 0:NH * VW], NH)
                    nc.vector.reciprocal(sums[:, qt, :], heads[:, :, DK]).then_inc(sums_ready, per_qt)
                    dve.wait_ge(sums_ready, i + (qt + 1) * per_qt)
                    if project and qt == 0:
                        wait_reuse(dve, ctxT_ps, i)
                    nc.vector.tensor_tensor(fold(ctx[:, qt, :], NH), heads[:, :, 0:DK],
                                            spread(sums[:, qt, :], DK, 2), ALU.mult).then_inc(ctx_ready, per_qt)

                def units(i):
                    for u in range(UNITS):
                        if top:
                            select(i, u)
                        else:
                            maxima(i, u)
                            if u >= 1:
                                turned(i, u - 1)
                        if u == HALF + 2:
                            normalise(i, 0)
                    if not top:
                        turned(i, UNITS - 1)
                    normalise(i, 1)

                def tail(i):
                    wait_reuse(dve, norm.done, i)
                    if project:
                        dve.wait_ge(o_ps, i + STEP)
                        dve.wait_ge(xr_ready, i + STEP)
                        for qt in range(QT):
                            last = nc.vector.tensor_tensor(norm.y[:, qt, :], j_bank[qt][:, 0:D], xr[:, qt, :],
                                                           ALU.add)
                    else:
                        dve.wait_ge(ctx_ready, i + STEP)
                        last = nc.vector.tensor_tensor(norm.y[:, :, :], ctx[:, :, :],
                                                       fold(batch_of(g.x_all, i), QT), ALU.add)
                    last.then_inc(norm.summed, STEP)
                    norm.vector_moments(nc, dve, i)
                    norm.vector_scale(nc, dve, i, g.x_all)

                front(0)
                def batch(i):
                    units(i)
                    front(i + STEP)
                    tail(i)

                each_batch(dve, batch, last_base - STEP)
                units(last_base)
                tail(last_base)


def route_phase(nc, a, g, tag, w, r, xs):
    with ExitStack() as stack:
        core = Core(nc, stack)
        xb = core.sb(f"{tag}_xb", [P, QT, D])
        xT = core.sb(f"{tag}_xT", [P, KC, S])
        hid = core.sb(f"{tag}_hid", [P, KC, S]) if w.rw1 is not None else xT
        logits = core.sb(f"{tag}_logits", [P, NT, E])
        top8 = core.sb(f"{tag}_top8", [P, NT, 8])
        index = core.sb(f"{tag}_index", [P, NT, 8], U32)
        choice = core.sb(f"{tag}_choice", [P, NT, TOPK])
        gap = core.sb(f"{tag}_gap", [P, 3, NT])
        hot = core.sb(f"{tag}_hot", [P, TOPK, NT, E])
        hot16 = core.sb(f"{tag}_hot16", [P, NT * E], BF16)
        total = core.sb(f"{tag}_total", [P, 2, NT, E])
        count = core.sb(f"{tag}_count", [P, NT, E])
        tiles = core.sb(f"{tag}_tiles", [P, 6, E])
        place = core.sb(f"{tag}_place", [P, NT, E])
        placed = core.sb(f"{tag}_placed", [P, TOPK, NT, E])
        slot = core.sb(f"{tag}_slot", [P, TOPK, NT])
        owner = core.sb(f"{tag}_owner", [P, ROUTED, E])
        owned = core.sb(f"{tag}_owned", [P, 2, ROUTED])
        xT_bank, hid_bank, logit_bank, sum_bank = (core.ps(f"{tag}_b{n}") for n in range(4))
        xb_ready, xT_ps, xT_ready, hid_ps, hid_ready, logit_ps, logit_ready = (
            core.sem(f"{tag}_{n}") for n in ("xb_ready", "xT_ps", "xT_ready", "hid_ps", "hid_ready", "logit_ps",
                                             "logit_ready"))
        v, exp_ready, count_ps, hot_ready, scattered, bias_loaded, bias_split, bias_stored, bias_placed = (
            core.sem(f"{tag}_{n}") for n in ("vector_step", "exp_ready", "count_ps", "hot_ready", "scattered",
                                             "bias_loaded", "bias_split", "bias_stored", "bias_placed"))
        bias = core.sb(f"{tag}_bias", [P, 3, E * (U + D) // P])
        parts = core.sb(f"{tag}_parts", [P, 3, E * (U + D) // P], BF16)
        nu = E * U // P

        with nc.Block() as block:

            @block.sync
            def _(sp):
                w.load(sp)
                sp.dma_start(bias[:, 0, 0:nu], w.b_up).then_inc(bias_loaded, 16)
                sp.dma_start(bias[:, 0, nu:], w.b_down).then_inc(bias_loaded, 16)
                sp.wait_ge(bias_split, 5)
                for n in range(3):
                    sp.dma_start(r.bias_dram[n, 0:E * U].rearrange("(p c) -> p c", p=P), parts[:, n, 0:nu])\
                        .then_inc(bias_stored, 16)
                    sp.dma_start(r.bias_dram[n, E * U:].rearrange("(p c) -> p c", p=P), parts[:, n, nu:])\
                        .then_inc(bias_stored, 16)
                sp.wait_ge(bias_stored, 6 * 16)
                sp.dma_start(r.bias[:, :], r.bias_dram[:, :]).then_inc(bias_placed, 16)
                sp.wait_ge(bias_placed, 16)

            @block.gpsimd
            def _(pool):
                def batch(i):
                    wait_reuse(pool, xT_ps, i)
                    nc.gpsimd.tensor_copy(xb[:, :, :].rearrange("p t c -> p (t c)"), batch_of(g.x_all, i))\
                        .then_inc(xb_ready, STEP)

                each_batch(pool, batch)
                pool.wait_ge(bias_loaded, 2 * 16)
                for n in range(3):
                    nc.gpsimd.tensor_copy(parts[:, n, :], bias[:, n, :]).then_inc(bias_split, 1)
                    if n < 2:
                        pool.wait_ge(bias_split, 2 * n + 1)
                        nc.gpsimd.tensor_tensor(bias[:, n + 1, :], bias[:, n, :], parts[:, n, :], ALU.subtract)\
                            .then_inc(bias_split, 1)
                        pool.wait_ge(bias_split, 2 * n + 2)
                pool.wait_ge(g.zeroed, 2 * 16)
                pool.wait_ge(r.slots_ready, 1)
                for k in range(TOPK):
                    for t in range(NT):
                        pool.indirect_dma_start(
                            out=xs[:, :], out_offset=bass.IndirectOffsetOnAxis(
                                ap=r.slots[:, k * NT + t:k * NT + t + 1], axis=0),
                            in_=g.x_all[:, t * D:(t + 1) * D], in_offset=None).then_inc(scattered, 16)
                pool.wait_ge(scattered, TOPK * NT * 16)

            @block.tensor
            def _(pe):
                pe.wait_ge(w.loaded, w.loads)
                def batch(i):
                    pe.wait_ge(xb_ready, i + STEP)
                    wait_reuse(pe, xT_ready, i)
                    for k in range(KC):
                        for t in range(QT):
                            last = nc.tensor.transpose(xT_bank[:, k * S + t * P:k * S + (t + 1) * P],
                                                       xb[:, t, k * P:(k + 1) * P], g.ident[:, :])
                    last.then_inc(xT_ps, STEP)
                    pe.wait_ge(xT_ready, i + STEP)
                    if w.rw1 is not None:
                        wait_reuse(pe, hid_ready, i)
                        for m in range(KC):
                            for k in range(KC):
                                last = nc.tensor.matmul(hid_bank[:, m * S:(m + 1) * S],
                                                        w.rw1[:, k * D + m * P:k * D + (m + 1) * P],
                                                        xT[:, k, :], start=k == 0, stop=k == KC - 1)
                        last.then_inc(hid_ps, STEP)
                        pe.wait_ge(hid_ready, i + STEP)
                    wait_reuse(pe, logit_ready, i)
                    for t in range(QT):
                        for k in range(KC):
                            last = nc.tensor.matmul(logit_bank[:, t * E:(t + 1) * E], hid[:, k, t * P:(t + 1) * P],
                                                    w.router[:, k * E:(k + 1) * E], start=k == 0, stop=k == KC - 1)
                    last.then_inc(logit_ps, STEP)

                each_batch(pe, batch)
                pe.wait_ge(hot_ready, 1)
                nc.tensor.matmul(sum_bank[:, 0:NT * E], g.before16[:, :], hot16[:, :], start=True, stop=True)
                nc.tensor.matmul(sum_bank[:, NT * E:2 * NT * E], g.ones16[:, :], hot16[:, :],
                                 start=True, stop=True).then_inc(count_ps, 1)

            @block.scalar
            def _(act):
                def batch(i):
                    act.wait_ge(xT_ps, i + STEP)
                    wait_reuse(act, logit_ps, i)
                    nc.scalar.activation(xT[:, :, :], fold(xT_bank[:, :], KC), ACT.Copy).then_inc(xT_ready, STEP)
                    if w.rw1 is not None:
                        act.wait_ge(hid_ps, i + STEP)
                        for m in range(KC):
                            last = nc.scalar.activation(hid[:, m, :], hid_bank[:, m * S:(m + 1) * S], ACT.Silu,
                                                        bias=w.rb1[:, m:m + 1])
                        last.then_inc(hid_ready, STEP)

                each_batch(act, batch)
                act.wait_ge(v, 2)
                nc.scalar.activation(gap[:, 1, :], gap[:, 0, :], ACT.Exp).then_inc(exp_ready, 1)

            @block.vector
            def _(dve):
                done = [0]

                def step(instruction):
                    done[0] += 1
                    instruction.then_inc(v, 1)
                    dve.wait_ge(v, done[0])

                def batch(i):
                    dve.wait_ge(logit_ps, i + STEP)
                    step_e = QT * E // STEP
                    out = fold(logits[:, :, :].rearrange("p t e -> p (t e)")[:, bass.ds(i * step_e, QT * E)], QT)
                    src = fold(logit_bank[:, 0:QT * E], QT)
                    if w.rb2 is None:
                        nc.vector.tensor_copy(out, src).then_inc(logit_ready, STEP)
                    else:
                        nc.vector.tensor_tensor(out, src, spread(w.rb2[:, :], QT, 1), ALU.add)\
                            .then_inc(logit_ready, STEP)

                each_batch(dve, batch)
                dve.wait_ge(logit_ready, B * STEP)
                for t in range(NT):
                    last = nc.vector.max(top8[:, t, :], logits[:, t, :])
                step(last)
                step(nc.vector.tensor_tensor(gap[:, 0, :], top8[:, :, 1], top8[:, :, 0], ALU.subtract))
                for t in range(NT):
                    last = nc.vector.max_index(index[:, t, :], top8[:, t, :], logits[:, t, :])
                step(last)
                step(nc.vector.tensor_copy(choice[:, :, :], index[:, :, 0:TOPK]))
                for k in range(TOPK):
                    last = nc.vector.tensor_tensor(hot[:, k, :, :], spread(choice[:, :, k], E, 2),
                                                   spread(g.iota[:, 0:E], NT, 1), ALU.is_equal)
                step(last)
                nc.vector.tensor_tensor(hot16[:, :], hot[:, 0, :, :].rearrange("p t e -> p (t e)"),
                                        hot[:, 1, :, :].rearrange("p t e -> p (t e)"), ALU.add)\
                    .then_inc(hot_ready, 1)
                dve.wait_ge(exp_ready, 1)
                step(nc.vector.tensor_scalar(gap[:, 2, :], gap[:, 1, :], 1.0, None, ALU.add))
                step(nc.vector.reciprocal(r.weights[:, 0:NT], gap[:, 2, :]))
                nc.vector.tensor_tensor(r.weights[:, NT:2 * NT], gap[:, 1, :], r.weights[:, 0:NT], ALU.mult)
                dve.wait_ge(count_ps, 1)
                nc.vector.tensor_copy(place[:, :, :], fold(sum_bank[:, 0:NT * E], NT))
                nc.vector.tensor_copy(count[:, :, :], fold(sum_bank[:, NT * E:2 * NT * E], NT))
                step(nc.vector.tensor_copy(total[:, 0, :, :], fold(sum_bank[:, NT * E:2 * NT * E], NT)))
                side, reach = 0, 1
                while reach < NT:
                    nc.vector.tensor_copy(total[:, 1 - side, 0:reach, :], total[:, side, 0:reach, :])
                    step(nc.vector.tensor_tensor(total[:, 1 - side, reach:, :], total[:, side, reach:, :],
                                                 total[:, side, 0:NT - reach, :], ALU.add))
                    side, reach = 1 - side, 2 * reach
                step(nc.vector.tensor_scalar(tiles[:, 0, :], total[:, side, NT - 1, :], 127.0, 1.0 / P,
                                             ALU.add, ALU.mult))
                step(nc.vector.tensor_scalar(tiles[:, 1, :], tiles[:, 0, :], -127.0 / 256, None, ALU.add))
                step(nc.vector.tensor_scalar(tiles[:, 2, :], tiles[:, 1, :], 12582912.0, None, ALU.add))
                step(nc.vector.tensor_scalar(tiles[:, 3, :], tiles[:, 2, :], -12582912.0, None, ALU.add))
                src, other, reach = 3, 4, 1
                while reach < E:
                    nc.vector.tensor_copy(tiles[:, other, 0:reach], tiles[:, src, 0:reach])
                    step(nc.vector.tensor_tensor(tiles[:, other, reach:], tiles[:, src, reach:],
                                                 tiles[:, src, 0:E - reach], ALU.add))
                    src, other, reach = other, (5 if other == 4 else 4), 2 * reach
                end = src
                free = 9 - end
                step(nc.vector.tensor_tensor(total[:, 1 - side, :, :], total[:, side, :, :], count[:, :, :],
                                             ALU.subtract))
                step(nc.vector.tensor_tensor(place[:, :, :], place[:, :, :], total[:, 1 - side, :, :], ALU.add))
                nc.vector.memset(tiles[:, free, 0:1], 0.0)
                step(nc.vector.tensor_scalar(tiles[:, free, 1:E], tiles[:, end, 0:E - 1], float(P), None,
                                             ALU.mult))
                step(nc.vector.tensor_tensor(place[:, :, :], place[:, :, :], spread(tiles[:, free, :], NT, 1),
                                             ALU.add))
                for k in range(TOPK):
                    last = nc.vector.tensor_tensor(placed[:, k, :, :], hot[:, k, :, :], place[:, :, :], ALU.mult)
                step(last)
                for k in range(TOPK):
                    last = nc.vector.tensor_reduce(slot[:, k, :], placed[:, k, :, :], AX.X, ALU.add)
                step(last)
                nc.vector.tensor_copy(r.slots[:, :], slot[:, :, :].rearrange("p k t -> p (k t)"))\
                    .then_inc(r.slots_ready, 1)
                step(nc.vector.tensor_tensor(owner[:, :, :], spread(g.iota[:, 0:ROUTED], E, 2),
                                             spread(tiles[:, end, :], ROUTED, 1), ALU.is_ge))
                step(nc.vector.tensor_reduce(owned[:, 0, :], owner[:, :, :], AX.X, ALU.add))
                step(nc.vector.tensor_scalar(owned[:, 1, :], owned[:, 0, :], float(E - 1), None, ALU.min))
                nc.vector.tensor_copy(r.expert[:, 0:ROUTED], owned[:, 1, :])


def each_tile(engine, body, n):
    body(0)
    with engine.Fori(1, n) as j:
        body(j)


def expert_phase(nc, a, g, tag, r, xs, ys, func):
    with ExitStack() as stack:
        core = Core(nc, stack)
        xg = core.sb(f"{tag}_xg", [P, D])
        xgT = core.sb(f"{tag}_xgT", [P, KC, P])
        hid = core.sb(f"{tag}_hid", [P, U])
        hidT = core.sb(f"{tag}_hidT", [P, UC, P])
        y = core.sb(f"{tag}_y", [P, D])
        up_bank = [core.ps(f"{tag}_u{n}") for n in range(2)]
        t_bank = [core.ps(f"{tag}_t{n}") for n in range(2)]
        x_bank = core.ps(f"{tag}_x")
        y_bank = core.ps(f"{tag}_yb")
        xg_loaded, xgT_ps, xgT_ready, up_ps, hid_ready, hidT_ps, hidT_ready, down_ps, y_ready, y_stored = (
            core.sem(f"{tag}_{n}") for n in ("xg_loaded", "xgT_ps", "xgT_ready", "up_ps", "hid_ready", "hidT_ps",
                                             "hidT_ready", "down_ps", "y_ready", "y_stored"))
        CH = U // 512
        last_tile = ROUTED - 1

        with nc.Block() as block:

            @block.sync
            def _(sp):
                def load(j):
                    wait_reuse(sp, xgT_ps, j)
                    sp.dma_start(xg[:, :], xs[bass.ds(j * P, P), :]).then_inc(xg_loaded, 16)

                each_tile(sp, load, ROUTED)

            @block.gpsimd
            def _(pool):
                with pool.Fori(0, ROUTED) as j:
                    pool.wait_ge(y_ready, j + 1)
                    pool.dma_start(ys[bass.ds(j * P, P), :], y[:, :]).then_inc(y_stored, 16)
                pool.wait_ge(y_stored, ROUTED * 16)

            @block.tensor
            def _(pe):
                def take(j):
                    pe.wait_ge(xg_loaded, (j + 1) * 16)
                    wait_reuse(pe, xgT_ready, j)
                    for k in range(KC):
                        last = nc.tensor.transpose(x_bank[:, k * P:(k + 1) * P], xg[:, k * P:(k + 1) * P],
                                                   g.ident[:, :])
                    last.then_inc(xgT_ps, 1)

                def up(j):
                    e = pe.value_load(r.expert[0:1, bass.ds(j, 1)], min_val=0, max_val=E - 1)
                    pe.wait_ge(xgT_ready, j + 1)
                    wait_reuse(pe, hid_ready, j * CH)
                    for c in range(CH):
                        for k in range(KC):
                            at = e * (KC * U) + (k * U + c * 512)
                            nc.tensor.matmul(up_bank[c][:, :], xgT[:, k, :], g.w_up[:, bass.ds(at, 512)],
                                             start=k == 0, stop=False)
                        at = e * U + c * 512
                        nc.tensor.matmul(up_bank[c][:, :], g.ones16[0:3, :], r.bias[:, bass.ds(at, 512)],
                                         start=False, stop=True).then_inc(up_ps, 1)

                def turn(j):
                    for c in range(CH):
                        pe.wait_ge(hid_ready, j * CH + c + 1)
                        if c == 0:
                            wait_reuse(pe, hidT_ready, j * CH)
                        for n in range(UC // CH):
                            last = nc.tensor.transpose(t_bank[c][:, n * P:(n + 1) * P],
                                                       hid[:, c * 512 + n * P:c * 512 + (n + 1) * P], g.ident[:, :])
                        last.then_inc(hidT_ps, 1)

                def down(j):
                    e = pe.value_load(r.expert[0:1, bass.ds(j, 1)], min_val=0, max_val=E - 1)
                    wait_reuse(pe, y_ready, j)
                    for c in range(CH):
                        pe.wait_ge(hidT_ready, j * CH + c + 1)
                        for n in range(c * UC // CH, (c + 1) * UC // CH):
                            at = e * (UC * D) + n * D
                            nc.tensor.matmul(y_bank[:, 0:D], hidT[:, n, :], g.w_down[:, bass.ds(at, D)],
                                             start=n == 0, stop=False)
                    at = e * D + E * U
                    nc.tensor.matmul(y_bank[:, 0:D], g.ones16[0:3, :], r.bias[:, bass.ds(at, D)],
                                     start=False, stop=True).then_inc(down_ps, 1)

                pe.wait_ge(g.experts_loaded, (r.layer + 1) * 2 * E * 16)
                take(0)
                up(0)
                take(1)

                def tile(j):
                    turn(j)
                    up(j + 1)
                    take(j + 2)
                    down(j)

                each_tile(pe, tile, last_tile - 1)
                turn(last_tile - 1)
                up(last_tile)
                down(last_tile - 1)
                turn(last_tile)
                down(last_tile)

            @block.scalar
            def _(act):
                def activate(j):
                    for c in range(CH):
                        act.wait_ge(up_ps, j * CH + c + 1)
                        if c == 0:
                            wait_reuse(act, hidT_ps, j * CH)
                        nc.scalar.activation(hid[:, c * 512:(c + 1) * 512], up_bank[c][:, :], func)\
                            .then_inc(hid_ready, 1)

                def result(j):
                    act.wait_ge(down_ps, j + 1)
                    wait_reuse(act, y_stored, j * 16)
                    nc.scalar.activation(y[:, :], y_bank[:, 0:D], ACT.Copy).then_inc(y_ready, 1)

                activate(0)

                def tile(j):
                    activate(j + 1)
                    result(j)

                each_tile(act, tile, last_tile)
                result(last_tile)

            @block.vector
            def _(dve):
                def take(j):
                    dve.wait_ge(xgT_ps, j + 1)
                    wait_reuse(dve, up_ps, j * CH)
                    nc.vector.tensor_copy(xgT[:, :, :], fold(x_bank[:, 0:KC * P], KC)).then_inc(xgT_ready, 1)

                def turned(j):
                    for c in range(CH):
                        dve.wait_ge(hidT_ps, j * CH + c + 1)
                        if c == 0:
                            wait_reuse(dve, down_ps, j)
                        half = UC // CH
                        nc.vector.tensor_copy(hidT[:, c * half:(c + 1) * half, :], fold(t_bank[c][:, :], half))\
                            .then_inc(hidT_ready, 1)

                take(0)
                take(1)

                def tile(j):
                    turned(j)
                    take(j + 2)

                each_tile(dve, tile, last_tile - 1)
                turned(last_tile - 1)
                turned(last_tile)


def combine_phase(nc, a, g, tag, r, ys, twice, out, extra):
    with ExitStack() as stack:
        core = Core(nc, stack)
        rows = core.sb(f"{tag}_rows", [P, 2, TOPK, QT, D])
        index = core.sb(f"{tag}_index", [P, 2, TOPK, QT], U32)
        part = core.sb(f"{tag}_part", [P, 2, QT, D])
        norm = Norm(core, tag)
        index_ready = core.sem(f"{tag}_index_ready")
        part_ready = core.sem(f"{tag}_part_ready")
        both_ready = core.sem(f"{tag}_both_ready")
        carrier = core.sem(f"{tag}_carrier")
        gathered = [core.sem(f"{tag}_gathered{n}") for n in range(2)]
        stored = core.sem(f"{tag}_stored")
        per_pair = TOPK * QT * 16

        with nc.Block() as block:

            @block.gpsimd
            def _(pool):
                def gather(j, s):
                    for k in range(TOPK):
                        col = j // (STEP // QT) + k * NT
                        last = nc.gpsimd.tensor_copy(index[:, s, k, :], r.slots[:, bass.ds(col, QT)])
                    last.then_inc(index_ready, STEP)
                    pool.wait_ge(index_ready, j + STEP)
                    pool.sem_inc(carrier, 1)
                    for k in range(TOPK):
                        for qt in range(QT):
                            pool.indirect_dma_start(
                                out=rows[:, s, k, qt, :], out_offset=None, in_=ys[:, :],
                                in_offset=bass.IndirectOffsetOnAxis(ap=index[:, s, k, qt:qt + 1], axis=0))\
                                .then_inc(gathered[s], 16)

                gather(0, 0)
                gather(STEP, 1)
                with pool.Fori(0, (B - 4) * STEP + 1, 2 * STEP) as i:
                    for s in range(2):
                        norm.pool_rstd(nc, pool, i + s * STEP, g.minus_half)
                        gather(i + (2 + s) * STEP, s)
                for s in range(2):
                    norm.pool_rstd(nc, pool, (B - 2 + s) * STEP, g.minus_half)

            @block.vector
            def _(dve):
                def pair(p):
                    for s in range(2):
                        i = p + s * STEP
                        dve.wait_ge(gathered[s], p * (per_pair // (2 * STEP)) + per_pair)
                        col = i // (STEP // QT)
                        wait_reuse(dve, norm.done, i)
                        for qt in range(QT):
                            last = nc.vector.scalar_tensor_tensor(
                                part[:, 0, qt, :], rows[:, s, 0, qt, :], r.weights[:, bass.ds(col + qt, 1)],
                                tile_of(g.x_all, i, qt), ALU.mult, ALU.add)
                        last.then_inc(part_ready, STEP)
                        dve.wait_ge(part_ready, i + STEP)
                        for qt in range(QT):
                            last = nc.vector.scalar_tensor_tensor(
                                (part[:, 1, qt, :] if twice else norm.y[:, qt, :]), rows[:, s, 1, qt, :],
                                r.weights[:, bass.ds(NT + col + qt, 1)], part[:, 0, qt, :],
                                ALU.mult, ALU.add)
                        if twice:
                            last.then_inc(both_ready, STEP)
                            dve.wait_ge(both_ready, i + STEP)
                            last = nc.vector.tensor_tensor(norm.y[:, :, :], part[:, 1, :, :],
                                                           fold(batch_of(g.x_all, i), QT), ALU.add)
                        last.then_inc(norm.summed, STEP)
                        norm.vector_moments(nc, dve, i)
                        norm.vector_scale(nc, dve, i, g.x_all)

                pair(0)
                with dve.Fori(2 * STEP, (B - 2) * STEP + 1, 2 * STEP) as p:
                    pair(p)

            @block.sync
            def _(sp):
                if extra is not None:
                    extra(sp)
                if out is not None:
                    def batch(i):
                        sp.wait_ge(norm.done, i + STEP)
                        sp.dma_start(out[bass.ds(i * (S // STEP), S), :]
                                     .rearrange("(t p) c -> p t c", p=P),
                                     fold(batch_of(g.x_all, i), QT)).then_inc(stored, 16)

                    each_batch(sp, batch)
                    sp.wait_ge(stored, B * 16)


class Weights:
    wq = wk = wv = wo = bq = bk = bv = bo = rw1 = rb1 = rb2 = router = None

    def __init__(self, core, a, tag, mats=(), cols=(), rows=(), narrow=()):
        self.loaded = core.sem(f"{tag}_loaded")
        self.parts = []
        for attribute, name in mats:
            self.add(attribute, core.sb(f"{tag}_{attribute}", [P, KC * D]),
                     a[name].rearrange("(k p) c -> p k c", p=P), KC)
        for attribute, name in narrow:
            self.add(attribute, core.sb(f"{tag}_{attribute}", [P, KC * E]),
                     a[name].rearrange("(k p) c -> p k c", p=P), KC)
        for attribute, name in cols:
            self.add(attribute, core.sb(f"{tag}_{attribute}", [P, KC]), a[name], 0)
        for attribute, name in rows:
            n = a[name].shape[1]
            self.add(attribute, core.sb(f"{tag}_{attribute}", [P, n]), a[name].broadcast_to([P, n]), 0)
        self.loads = 16 * len(self.parts)

    def add(self, attribute, tile, source, n):
        if attribute == "wq":
            self.wq = tile
        elif attribute == "wk":
            self.wk = tile
        elif attribute == "wv":
            self.wv = tile
        elif attribute == "wo":
            self.wo = tile
        elif attribute == "bq":
            self.bq = tile
        elif attribute == "bk":
            self.bk = tile
        elif attribute == "bv":
            self.bv = tile
        elif attribute == "bo":
            self.bo = tile
        elif attribute == "rw1":
            self.rw1 = tile
        elif attribute == "rb1":
            self.rb1 = tile
        elif attribute == "rb2":
            self.rb2 = tile
        elif attribute == "router":
            self.router = tile
        self.parts.append((fold(tile[:, :], n) if n else tile[:, :], source))

    def load(self, queue):
        for tile, source in self.parts:
            queue.dma_start(tile, source).then_inc(self.loaded, 16)


class Routing:

    def __init__(self, nc, core, tag):
        self.slots = core.sb(f"{tag}_slots", [P, TOPK * NT], U32)
        self.weights = core.sb(f"{tag}_weights", [P, TOPK * NT])
        self.expert = core.sb(f"{tag}_expert", [P, ROUTED + 1], I32)
        self.slots_ready = core.sem(f"{tag}_slots_ready")
        self.bias = core.sb(f"{tag}_bias3", [3, E * (U + D)], BF16)
        self.bias_dram = nc.dram_tensor(f"{tag}_bias_dram", (3, E * (U + D)), BF16)


class Shared:

    def __init__(self, nc, core, a):
        self.nc, self.a = nc, a
        self.x_all = core.sb("x_all", [P, NT * D])
        self.w_up = core.sb("w_up", [P, E * KC * U])
        self.w_down = core.sb("w_down", [P, E * UC * D])
        self.ident = core.sb("ident", [P, P])
        self.ident16 = core.sb("ident16", [P, P], BF16)
        self.before16 = core.sb("before16", [P, P], BF16)
        self.ones16 = core.sb("ones16", [P, P], BF16)
        self.causal16 = core.sb("causal16", [P, 2, P], BF16)
        self.pair_mask = core.sb("pair_mask", [P, 2])
        self.iota = core.sb("iota", [P, ROUTED])
        self.minus_half = core.sb("minus_half", [P, QT])
        self.zeros = core.sb("zeros", [P, D])
        self.x_loaded = core.sem("x_loaded")
        self.const_loaded = core.sem("const_loaded")
        self.experts_loaded = core.sem("experts_loaded")
        self.zeroed = core.sem("zeroed")
        self.zero_ready = core.sem("zero_ready")

    def load_experts(self, queue, up, down):
        for e in range(E):
            queue.dma_start(fold(self.w_up[:, e * KC * U:(e + 1) * KC * U], KC),
                            up[e].rearrange("(k p) u -> p k u", p=P)).then_inc(self.experts_loaded, 16)
            queue.dma_start(fold(self.w_down[:, e * UC * D:(e + 1) * UC * D], UC),
                            down[e].rearrange("(n p) c -> p n c", p=P)).then_inc(self.experts_loaded, 16)


class Mixer:

    def __init__(self, core):
        self.dft = core.sb("dft", [P, QT * FFT])
        self.idft = core.sb("idft", [P, NF * S])
        self.spec_re = core.sb("spec_re", [P, KC * D])
        self.spec_re2 = core.sb("spec_re2", [P, KC * D])
        self.spec_im = core.sb("spec_im", [P, KC * D])
        self.ss_w = core.sb("ss_w", [P, KC * D])
        self.gate_w = core.sb("gate_w", [P, KC * D])
        self.fin_w = core.sb("fin_w", [P, KC * D])
        self.ss_b = core.sb("ss_b", [P, KC])
        self.gate_b = core.sb("gate_b", [P, KC])
        self.fin_b = core.sb("fin_b", [P, D])
        self.dft_loaded = core.sem("dft_loaded")
        self.loaded = core.sem("mixer_loaded")
        self.loads = 7 * 16

    def load(self, queue, a):
        queue.dma_start(fold(self.dft[:, :], QT), a["dft"].rearrange("(t p) f -> p t f", p=P))\
            .then_inc(self.dft_loaded, 16)
        for tile, name, n in ((self.idft, "idft", NF), (self.ss_w, "ss_wT", KC), (self.gate_w, "gate_wT", KC),
                              (self.fin_w, "fin_wT", KC)):
            queue.dma_start(fold(tile[:, :], n), a[name].rearrange("(t p) f -> p t f", p=P))\
                .then_inc(self.loaded, 16)
        queue.dma_start(self.ss_b[:, :], a["ss_b"]).then_inc(self.loaded, 16)
        queue.dma_start(self.gate_b[:, :], a["gate_b"]).then_inc(self.loaded, 16)
        queue.dma_start(self.fin_b[:, :], a["fin_b"].broadcast_to([P, D])).then_inc(self.loaded, 16)


def decoder(nc, a, out):
    xs = [nc.dram_tensor(f"xs{n}", (ROUTED * P, D), F32) for n in range(2)]
    ys = [nc.dram_tensor(f"ys{n}", (ROUTED * P, D), F32) for n in range(2)]
    with ExitStack() as stack:
        core = Core(nc, stack)
        g = Shared(nc, core, a)

        with ExitStack() as first:
            early = Core(nc, first)
            mx = Mixer(early)
            w0 = Weights(early, a, "c0", mats=(("wq", "L0_wqT"), ("wk", "L0_wkT"), ("wv", "L0_wvT"),
                                               ("wo", "L0_woT")))

            def load_first(sp):
                mx.load(sp, a)
                w0.load(sp)
                sp.wait_ge(g.zero_ready, 1)
                for n in range(2):
                    sp.dma_start(xs[n].rearrange("(t p) c -> p t c", p=P),
                                 spread(g.zeros[:, :], ROUTED, 1)).then_inc(g.zeroed, 16)
                g.load_experts(sp, a["L0_up"], a["L0_down"])

            kernel_spectrum(nc, a, g, mx, load_first)
            mixer_phase(nc, a, g, mx)
            attention_phase(nc, a, g, "c0", w0, cross=True, causal=True, top=False, project=True,
                            scale=DK ** -0.5)
        experts(nc, a, g, 0, xs[0], ys[0], out)
        with ExitStack() as second:
            late = Core(nc, second)
            wc = Weights(late, a, "c1", mats=(("wq", "L1_wqT"), ("wk", "L1_wkT"), ("wv", "L1_wvT"),
                                              ("wo", "L1_woT")),
                         cols=(("bq", "L1_bq"), ("bk", "L1_bk")), rows=(("bv", "L1_bv"), ("bo", "L1_bo")))

            def prefetch(sp):
                wc.load(sp)
                g.load_experts(sp, a["L1_up"], a["L1_down"])

            with ExitStack() as inner:
                ws = Weights(Core(nc, inner), a, "s1", mats=(("wq", "L1_wq"), ("wk", "L1_wk"),
                                                             ("wv", "L1_wv")))
                attention_phase(nc, a, g, "s1", ws, cross=False, causal=False, top=False, project=False,
                                scale=D ** -0.5, loads=(ws.load, prefetch))
            attention_phase(nc, a, g, "c1", wc, cross=True, causal=False, top=True,
                            project=True, scale=DK ** -0.5)
        experts(nc, a, g, 1, xs[1], ys[1], out)


def experts(nc, a, g, layer, xs, ys, out):
    with ExitStack() as stack:
        core = Core(nc, stack)
        r = Routing(nc, core, f"r{layer}")
        r.layer = layer
        if layer == 0:
            w = Weights(core, a, "t0", narrow=(("router", "L0_router"),))
            w.b_up, w.b_down, func = a["L0_b_up"], a["L0_b_down"], ACT.Gelu
        else:
            w = Weights(core, a, "t1", mats=(("rw1", "L1_rw1"),), narrow=(("router", "L1_rw2"),),
                        cols=(("rb1", "L1_rb1"),), rows=(("rb2", "L1_rb2"),))
            w.b_up, w.b_down, func = a["L1_b_up"], a["L1_b_down"], ACT.Silu
        route_phase(nc, a, g, f"t{layer}", w, r, xs)
        expert_phase(nc, a, g, f"e{layer}", r, xs, ys, func)
        combine_phase(nc, a, g, f"k{layer}", r, ys, layer == 1, out if layer == 1 else None, None)



def _laid_out(i):
    c = np.ascontiguousarray

    def col(v):
        return c(v.reshape(KC, P).T)

    f = np.arange(FFT // 2)
    t = np.arange(S)
    turn = 2 * np.pi * np.outer(t, f) / FFT
    nyquist = (-1.0) ** t
    dft = np.concatenate([np.cos(turn), -np.sin(turn)], axis=1)
    dft[:, FFT // 2] = nyquist
    idft = 2 * np.concatenate([np.cos(turn.T), -np.sin(turn.T)], axis=0) / FFT
    idft[0] = 1 / FFT
    idft[FFT // 2] = nyquist / FFT
    p = np.arange(P)
    const = np.zeros((P, 3 * P + 2 + ROUTED), np.float32)
    const[:, 0:P] = np.eye(P)
    const[:, P:2 * P] = p[:, None] < p[None, :]
    const[:, 2 * P:3 * P] = np.where(p[None, :] > p[:, None], -1e30, 0)
    const[:, 3 * P] = (p // DK) % 2 == 0
    const[:, 3 * P + 1] = (p // DK) % 2 == 1
    const[:, 3 * P + 2:] = np.arange(ROUTED)
    qkv = i["L1_attn_w_qkv"]
    return {
        "x": i["x"].reshape(N, D),
        "ctxT": c(i["ctx_1024"].transpose(0, 2, 1)).reshape(B * D, S),
        "decays": i["L0_attn_decays"].reshape(STATES, 1),
        "frequencies": i["L0_attn_frequencies"].reshape(STATES, 1),
        "in_projT": c(i["L0_attn_in_proj"].T),
        "out_proj": i["L0_attn_out_proj"],
        "lag": np.tile(np.arange(S, dtype=np.float32), (STATES, 1)),
        "dft": dft.astype(np.float32), "idft": idft.astype(np.float32), "const": const,
        "ss_wT": c(i["L0_attn_ss_W"].T), "gate_wT": c(i["L0_attn_gate_W"].T), "fin_wT": c(i["L0_attn_fin_W"].T),
        "ss_b": col(i["L0_attn_ss_b"]), "gate_b": col(i["L0_attn_gate_b"]),
        "fin_b": i["L0_attn_fin_b"].reshape(1, D),
        "L0_wqT": c(i["L0_xattn_Wq"].T), "L0_wkT": c(i["L0_xattn_Wk"].T), "L0_wvT": c(i["L0_xattn_Wv"].T),
        "L0_woT": c(i["L0_xattn_Wo"].T),
        "L0_up": c(i["L0_ffn_w_up"].transpose(0, 2, 1)), "L0_down": c(i["L0_ffn_w_down"].transpose(0, 2, 1)),
        "L0_b_up": i["L0_ffn_b_up"].reshape(P, -1), "L0_b_down": i["L0_ffn_b_down"].reshape(P, -1),
        "L0_router": c(i["L0_ffn_w_router"].T),
        "L1_wq": c(qkv[:, 0:D]), "L1_wk": c(qkv[:, D:2 * D]), "L1_wv": c(qkv[:, 2 * D:]),
        "L1_wqT": c(i["L1_xattn_Wq"].T), "L1_wkT": c(i["L1_xattn_Wk"].T), "L1_wvT": c(i["L1_xattn_Wv"].T),
        "L1_woT": c(i["L1_xattn_Wo"].T),
        "L1_bq": col(i["L1_xattn_bq"]), "L1_bk": col(i["L1_xattn_bk"]),
        "L1_bv": i["L1_xattn_bv"].reshape(1, D), "L1_bo": i["L1_xattn_bo"].reshape(1, D),
        "L1_rw1": i["L1_ffn_rw1"], "L1_rb1": col(i["L1_ffn_rb1"]), "L1_rw2": i["L1_ffn_rw2"],
        "L1_rb2": i["L1_ffn_rb2"].reshape(1, E),
        "L1_up": i["L1_ffn_we1"], "L1_down": i["L1_ffn_we2"],
        "L1_b_up": i["L1_ffn_be1"].reshape(P, -1), "L1_b_down": i["L1_ffn_be2"].reshape(P, -1),
    }


def kernel(**inputs):
    import concourse.bacc as bacc
    from concourse.bass_utils import run_bass_kernel_spmd

    arrays = {n: np.ascontiguousarray(v) for n, v in
              _laid_out({n: np.asarray(v) for n, v in inputs.items()}).items()}
    nc = bacc.Bacc("TRN2", target_bir_lowering=False, num_devices=1)
    a = {n: nc.dram_tensor(f"in_{n}", v.shape, F32, kind="ExternalInput").ap() for n, v in arrays.items()}
    out = nc.dram_tensor("out", (N, D), F32, kind="ExternalOutput").ap()
    decoder(nc, a, out)
    result = run_bass_kernel_spmd(nc, [{f"in_{n}": v for n, v in arrays.items()}], core_ids=[0])
    return result.results[0]["out"].reshape(B, S, D)
```

```python
from contextlib import ExitStack

import numpy as np

import concourse.bass as bass
from concourse import mybir

F32 = mybir.dt.float32
BF16 = mybir.dt.bfloat16
I32 = mybir.dt.int32
U32 = mybir.dt.uint32
ALU = mybir.AluOpType
ACT = mybir.ActivationFunctionType
AX = mybir.AxisListType

P = 128
B, S, D = 8, 256, 256
N = B * S
NT = N // P
QT = S // P
KC = D // P
NH, DK = 16, 16
HP = NH // 2
STATES = 64
FFT = 2 * S
NF = FFT // P
E, U, TOPK = 8, 1024, 2
UC = U // P
ROUTED = N * TOPK // P + E - 1
KEPT = 32
EPS = 1e-5
NEG = -3.0e38
STEP = 16


class Core:

    def __init__(self, nc, stack):
        self.nc = nc
        self.stack = stack
        self.sems = []
        stack.callback(self.clear)

    def clear(self):
        if self.sems:
            self.nc.clear_and_free_semaphores(self.sems)
            self.nc.all_engine_barrier()

    def sb(self, name, shape, dtype=F32):
        return self.stack.enter_context(self.nc.sbuf_tensor(name, shape, dtype))

    def ps(self, name, shape=(P, 512), dtype=F32):
        return self.stack.enter_context(self.nc.psum_tensor(name, list(shape), dtype))

    def sem(self, name):
        self.sems.append(self.nc.alloc_semaphore(name))
        return self.sems[-1]


def fold(ap, n):
    return ap.rearrange("p (n c) -> p n c", n=n)


def spread(ap, n, axis):
    shape = list(ap.shape)
    shape.insert(axis, n)
    return ap.unsqueeze(axis).broadcast_to(shape)


def batch_of(x_all, i):
    step = QT * D // STEP
    return x_all[:, bass.ds(i * step, QT * D)]


def tile_of(x_all, i, qt):
    step = QT * D // STEP
    return x_all[:, bass.ds(i * step + qt * D, D)]


def wait_reuse(engine, sem, value):
    if not (isinstance(value, int) and value <= 0):
        engine.wait_ge(sem, value)


def each_batch(engine, body, last=(B - 1) * STEP):
    body(0)
    with engine.Fori(STEP, last + 1, STEP) as i:
        body(i)


class Norm:

    def __init__(self, core, tag):
        self.y = core.sb(f"{tag}_y", [P, QT, D])
        self.stats = core.sb(f"{tag}_stats", [P, QT, 6])
        self.moments = core.sb(f"{tag}_moments", [P, QT, 2])
        self.var = core.sb(f"{tag}_var", [P, QT])
        self.rstd = core.sb(f"{tag}_rstd", [P, QT])
        self.summed = core.sem(f"{tag}_summed")
        self.stats_ready = core.sem(f"{tag}_stats_ready")
        self.moments_ready = core.sem(f"{tag}_moments_ready")
        self.var_ready = core.sem(f"{tag}_var_ready")
        self.rstd_ready = core.sem(f"{tag}_rstd_ready")
        self.done = core.sem(f"{tag}_done")
        self.carrier = core.sem(f"{tag}_norm_carrier")

    def vector_moments(self, nc, dve, i):
        dve.wait_ge(self.summed, i + STEP)
        for qt in range(QT):
            last = nc.vector.bn_stats(self.stats[:, qt, :], self.y[:, qt, :])
        last.then_inc(self.stats_ready, STEP)
        dve.wait_ge(self.stats_ready, i + STEP)
        dve.sem_inc(self.carrier, 1)
        for qt in range(QT):
            last = nc.vector.bn_aggr(self.moments[:, qt, :], self.stats[:, qt, :])
        last.then_inc(self.moments_ready, STEP)

    def pool_rstd(self, nc, pool, i, minus_half):
        pool.wait_ge(self.moments_ready, i + STEP)
        nc.gpsimd.tensor_scalar(self.var[:, :], self.moments[:, :, 1], EPS, None, ALU.add)\
            .then_inc(self.var_ready, STEP)
        pool.wait_ge(self.var_ready, i + STEP)
        nc.gpsimd.tensor_tensor(self.rstd[:, :], self.var[:, :], minus_half[:, 0:QT], ALU.pow)\
            .then_inc(self.rstd_ready, STEP)

    def vector_scale(self, nc, dve, i, x_all):
        dve.wait_ge(self.rstd_ready, i + STEP)
        for qt in range(QT):
            last = nc.vector.tensor_scalar(tile_of(x_all, i, qt), self.y[:, qt, :],
                                           self.moments[:, qt, 0:1], self.rstd[:, qt:qt + 1],
                                           ALU.subtract, ALU.mult)
        last.then_inc(self.done, STEP)


def kernel_spectrum(nc, a, g, mx, load_rest):
    with ExitStack() as stack:
        core = Core(nc, stack)
        lag = core.sb("lag", [STATES, S])
        mode = core.sb("mode", [STATES, 6])
        w_in = core.sb("w_in", [STATES, D])
        w_out = core.sb("w_out", [STATES, D])
        w = core.sb("w", [STATES, D])
        damp = core.sb("damp", [STATES, S])
        phase = core.sb("phase", [STATES, S])
        turns = core.sb("turns", [STATES, 2, S])
        rest = core.sb("rest", [STATES, 3, S])
        mag = core.sb("mag", [STATES, 2, S])
        half_pi = core.sb("half_pi", [STATES, 1])
        wave = core.sb("wave", [STATES, S])
        decay_env = core.sb("decay_env", [STATES, S])
        modes = core.sb("modes", [STATES, S])
        k_time = core.sb("k_time", [P, QT, D])
        const = core.sb("const", [P, 3 * P + 2 + NH // KC + ROUTED])
        k_ps = core.ps("k_ps")
        re_ps = core.ps("re_ps")
        im_ps = core.ps("im_ps")
        loaded = core.sem("p0_loaded")
        decayed = core.sem("p0_decayed")
        v = core.sem("p0_vector_step")
        waved = core.sem("p0_waved")
        k_done = core.sem("p0_k_done")
        k_copied = core.sem("p0_k_copied")
        spec_done = core.sem("p0_spec_done")

        with nc.Block() as block:

            @block.sync
            def _(sp):
                sp.dma_start(mode[:, 0:1], a["decays"]).then_inc(loaded, 16)
                sp.dma_start(mode[:, 1:2], a["frequencies"]).then_inc(loaded, 16)
                sp.dma_start(lag[:, :], a["lag"]).then_inc(loaded, 16)
                sp.dma_start(w_in[:, :], a["in_projT"]).then_inc(loaded, 16)
                sp.dma_start(w_out[:, :], a["out_proj"]).then_inc(loaded, 16)
                sp.dma_start(const[:, :], a["const"]).then_inc(g.const_loaded, 16)
                sp.dma_start(fold(g.x_all[:, :], NT), a["x"].rearrange("(t p) c -> p t c", p=P))\
                    .then_inc(g.x_loaded, 16)
                load_rest(sp)

            @block.scalar
            def _(act):
                act.wait_ge(loaded, 5 * 16)
                nc.scalar.activation(mode[:, 2:3], mode[:, 0:1], ACT.Exp).then_inc(decayed, 1)
                act.wait_ge(v, 2)
                nc.scalar.activation(decay_env[:, :], damp[:, :], ACT.Exp, scale=-1.0)\
                    .then_inc(decayed, 1)
                act.wait_ge(v, 12)
                nc.scalar.activation(wave[:, :], mag[:, 1, :], ACT.Sin, bias=half_pi[:, 0:1], scale=-1.0)\
                    .then_inc(waved, 1)
                for t in range(QT):
                    act.wait_ge(k_done, QT)
                    nc.scalar.activation(k_time[:, t, :], k_ps[:, t * D:(t + 1) * D], ACT.Copy)\
                        .then_inc(k_copied, 1)

            @block.vector
            def _(dve):
                def step(instruction, n):
                    instruction.then_inc(v, 1)
                    dve.wait_ge(v, n)

                nc.vector.memset(half_pi[:, :], float(np.pi / 2)).then_inc(v, 1)
                dve.wait_ge(decayed, 1)
                nc.vector.tensor_scalar(damp[:, :], lag[:, :], mode[:, 2:3], None, ALU.mult)\
                    .then_inc(v, 1)
                step(nc.vector.tensor_scalar(mode[:, 3:4], mode[:, 1:2], float(np.float32(2 * np.pi)),
                                             None, ALU.mult), 3)
                step(nc.vector.tensor_scalar(phase[:, :], lag[:, :], mode[:, 3:4], None, ALU.mult), 4)
                step(nc.vector.tensor_scalar(turns[:, 0, :], phase[:, :], float(1 / (2 * np.pi)),
                                             None, ALU.mult), 5)
                step(nc.vector.tensor_scalar(turns[:, 1, :], turns[:, 0, :], 12582912.0, None, ALU.add), 6)
                step(nc.vector.tensor_scalar(turns[:, 0, :], turns[:, 1, :], -12582912.0, None, ALU.add), 7)
                part1 = 6.28125
                part2 = float(np.round((2 * np.pi - part1) * 2.0**17) / 2.0**17)
                part3 = float(2 * np.pi - part1 - part2)
                step(nc.vector.scalar_tensor_tensor(rest[:, 0, :], turns[:, 0, :], -part1, phase[:, :],
                                                    ALU.mult, ALU.add), 8)
                step(nc.vector.scalar_tensor_tensor(rest[:, 1, :], turns[:, 0, :], -part2, rest[:, 0, :],
                                                    ALU.mult, ALU.add), 9)
                step(nc.vector.scalar_tensor_tensor(rest[:, 2, :], turns[:, 0, :], -part3, rest[:, 1, :],
                                                    ALU.mult, ALU.add), 10)
                step(nc.vector.tensor_scalar(mag[:, 0, :], rest[:, 2, :], -1.0, None, ALU.mult), 11)
                nc.vector.tensor_tensor(mag[:, 1, :], rest[:, 2, :], mag[:, 0, :], ALU.max).then_inc(v, 1)
                nc.vector.tensor_tensor(w[:, :], w_in[:, :], w_out[:, :], ALU.mult)
                dve.wait_ge(waved, 1)
                dve.wait_ge(decayed, 2)
                nc.vector.tensor_tensor(modes[:, :], wave[:, :], decay_env[:, :], ALU.mult).then_inc(v, 1)
                dve.wait_ge(spec_done, 1)
                half = KC * D
                nc.vector.tensor_copy(mx.spec_re[:, :], re_ps[:, 0:half])
                nc.vector.tensor_copy(mx.spec_re2[:, :], re_ps[:, 0:half])
                nc.vector.tensor_copy(mx.spec_im[:, :], im_ps[:, 0:half]).then_inc(v, 1)
                dve.wait_ge(v, 14)
                nc.vector.tensor_copy(mx.spec_re2[0:1, 0:D], im_ps[0:1, 0:D])
                nc.vector.memset(mx.spec_im[0:1, 0:D], 0.0)

            @block.tensor
            def _(pe):
                pe.wait_ge(v, 13)
                for t in range(QT):
                    nc.tensor.matmul(k_ps[:, t * D:(t + 1) * D], modes[:, t * P:(t + 1) * P], w[:, :],
                                     start=True, stop=True).then_inc(k_done, 1)
                pe.wait_ge(k_copied, QT)
                pe.wait_ge(mx.dft_loaded, 16)
                for f in range(NF):
                    out = (re_ps, im_ps)[f // 2][:, (f % 2) * D:(f % 2 + 1) * D]
                    for t in range(QT):
                        last = nc.tensor.matmul(out, mx.dft[:, t * FFT + f * P:t * FFT + (f + 1) * P],
                                                k_time[:, t, :], start=t == 0, stop=t == QT - 1)
                last.then_inc(spec_done, 1)

            @block.gpsimd
            def _(pool):
                nc.gpsimd.memset(g.zeros[:, :], 0.0).then_inc(g.zero_ready, 1)
                nc.gpsimd.memset(g.minus_half[:, :], -0.5)
                nc.gpsimd.memset(g.minus_one[:, :], -1.0)
                nc.gpsimd.memset(g.ones16[:, :], 1.0)
                pool.wait_ge(g.const_loaded, 16)
                nc.gpsimd.tensor_copy(g.ident[:, :], const[:, 0:P])
                nc.gpsimd.tensor_copy(g.ident16[:, :], const[:, 0:P])
                nc.gpsimd.tensor_copy(g.before16[:, :], const[:, P:2 * P])
                for h in range(2):
                    nc.gpsimd.tensor_copy(g.causal16[:, h, :], const[:, 2 * P:3 * P])
                nc.gpsimd.tensor_copy(g.pair_mask[:, :], const[:, 3 * P:3 * P + 2])
                nc.gpsimd.tensor_copy(g.head_mask[:, :], const[:, 3 * P + 2:3 * P + 2 + NH // KC])
                nc.gpsimd.tensor_copy(g.iota[:, :], const[:, 3 * P + 2 + NH // KC:])


def mixer_phase(nc, a, g, mx):
    with ExitStack() as stack:
        core = Core(nc, stack)
        xb = core.sb("m_xb", [P, QT, D])
        xT = core.sb("m_xT", [P, KC, S])
        prod = core.sb("m_prod", [P, 4, KC * D])
        yf = core.sb("m_yf", [P, NF, D])
        yT = core.sb("m_yT", [P, KC, S])
        ssT = core.sb("m_ssT", [P, KC, S])
        gateT = core.sb("m_gateT", [P, KC, S])
        mixT = core.sb("m_mixT", [P, KC, S])
        xr = core.sb("m_xr", [P, QT, D])
        norm = Norm(core, "m")
        ps_xT, ps_re, ps_im, ps_gate, ps_y, ps_ss, ps_out = (core.ps(f"m_ps{n}") for n in range(7))
        xb_ready, xT_ps, xT_ready, u_ps, prod_ready, yf_ready = (
            core.sem(f"m_{n}") for n in ("xb_ready", "xT_ps", "xT_ready", "u_ps", "prod_ready", "yf_ready"))
        gate_ps, gate_ready, y_ps, yT_ready, ss_ps, ss_ready, mix_ready, out_ps, xr_ready = (
            core.sem(f"m_{n}") for n in ("gate_ps", "gate_ready", "y_ps", "yT_ready", "ss_ps", "ss_ready",
                                         "mix_ready", "out_ps", "xr_ready"))
        last_base = (B - 1) * STEP

        with nc.Block() as block:

            @block.gpsimd
            def _(pool):
                def take(j):
                    wait_reuse(pool, u_ps, j)
                    nc.gpsimd.tensor_copy(xb[:, :, :].rearrange("p t c -> p (t c)"), batch_of(g.x_all, j))\
                        .then_inc(xb_ready, STEP)

                def spectrum(j):
                    pool.wait_ge(prod_ready, j + STEP)
                    wait_reuse(pool, y_ps, j)
                    nc.gpsimd.tensor_tensor(yf[:, 0:KC, :], fold(prod[:, 0, :], KC), fold(prod[:, 1, :], KC),
                                            ALU.subtract)
                    nc.gpsimd.tensor_tensor(yf[:, KC:NF, :], fold(prod[:, 2, :], KC), fold(prod[:, 3, :], KC),
                                            ALU.add).then_inc(yf_ready, STEP)

                def back(i):
                    wait_reuse(pool, norm.summed, i)
                    nc.gpsimd.tensor_tensor(xr[:, :, :], fold(batch_of(g.x_all, i), QT),
                                            spread(mx.fin_b[:, :], QT, 1), ALU.add).then_inc(xr_ready, STEP)
                    pool.wait_ge(ss_ready, i + STEP)
                    pool.wait_ge(gate_ready, i + STEP)
                    wait_reuse(pool, out_ps, i)
                    nc.gpsimd.tensor_tensor(mixT[:, :, :], ssT[:, :, :], gateT[:, :, :], ALU.mult)\
                        .then_inc(mix_ready, STEP)

                pool.wait_ge(g.x_loaded, 16)
                pool.wait_ge(mx.loaded, mx.loads)
                take(0)
                spectrum(0)
                def batch(i):
                    take(i + STEP)
                    back(i)
                    spectrum(i + STEP)
                    norm.pool_rstd(nc, pool, i, g.minus_half)

                each_batch(pool, batch, last_base - STEP)
                back(last_base)
                norm.pool_rstd(nc, pool, last_base, g.minus_half)

            @block.tensor
            def _(pe):
                def front(j):
                    pe.wait_ge(xb_ready, j + STEP)
                    wait_reuse(pe, xT_ready, j)
                    for k in range(KC):
                        for t in range(QT):
                            last = nc.tensor.transpose(ps_xT[:, k * S + t * P:k * S + (t + 1) * P],
                                                       xb[:, t, k * P:(k + 1) * P], g.ident[:, :])
                    last.then_inc(xT_ps, STEP)
                    wait_reuse(pe, prod_ready, j)
                    for f in range(NF):
                        out = (ps_re, ps_im)[f // 2][:, (f % 2) * D:(f % 2 + 1) * D]
                        for t in range(QT):
                            last = nc.tensor.matmul(out, mx.dft[:, t * FFT + f * P:t * FFT + (f + 1) * P],
                                                    xb[:, t, :], start=t == 0, stop=t == QT - 1)
                    last.then_inc(u_ps, STEP)

                def gate(j):
                    pe.wait_ge(xT_ready, j + STEP)
                    wait_reuse(pe, gate_ready, j)
                    for m in range(KC):
                        for k in range(KC):
                            last = nc.tensor.matmul(ps_gate[:, m * S:(m + 1) * S],
                                                    mx.gate_w[:, k * D + m * P:k * D + (m + 1) * P],
                                                    xT[:, k, :], start=k == 0, stop=k == KC - 1)
                    last.then_inc(gate_ps, STEP)

                def inverse(i):
                    pe.wait_ge(yf_ready, i + STEP)
                    wait_reuse(pe, yT_ready, i)
                    for m in range(KC):
                        for f in range(NF):
                            last = nc.tensor.matmul(ps_y[:, m * S:(m + 1) * S], yf[:, f, m * P:(m + 1) * P],
                                                    mx.idft[:, f * S:(f + 1) * S], start=f == 0, stop=f == NF - 1)
                    last.then_inc(y_ps, STEP)

                def state(i):
                    pe.wait_ge(yT_ready, i + STEP)
                    wait_reuse(pe, ss_ready, i)
                    for m in range(KC):
                        for k in range(KC):
                            last = nc.tensor.matmul(ps_ss[:, m * S:(m + 1) * S],
                                                    mx.ss_w[:, k * D + m * P:k * D + (m + 1) * P],
                                                    yT[:, k, :], start=k == 0, stop=k == KC - 1)
                    last.then_inc(ss_ps, STEP)

                def project(i):
                    pe.wait_ge(mix_ready, i + STEP)
                    wait_reuse(pe, norm.summed, i)
                    for t in range(QT):
                        for k in range(KC):
                            last = nc.tensor.matmul(ps_out[:, t * D:(t + 1) * D], mixT[:, k, t * P:(t + 1) * P],
                                                    mx.fin_w[:, k * D:(k + 1) * D], start=k == 0, stop=k == KC - 1)
                    last.then_inc(out_ps, STEP)

                pe.wait_ge(mx.loaded, mx.loads)
                front(0)
                gate(0)
                def batch(i):
                    inverse(i)
                    front(i + STEP)
                    state(i)
                    gate(i + STEP)
                    project(i)

                each_batch(pe, batch, last_base - STEP)
                inverse(last_base)
                state(last_base)
                project(last_base)

            @block.scalar
            def _(act):
                def take(j):
                    act.wait_ge(xT_ps, j + STEP)
                    wait_reuse(act, gate_ps, j)
                    nc.scalar.activation(xT[:, :, :], fold(ps_xT[:, :], KC), ACT.Copy).then_inc(xT_ready, STEP)

                def gate(j):
                    act.wait_ge(gate_ps, j + STEP)
                    wait_reuse(act, mix_ready, j)
                    for m in range(KC):
                        last = nc.scalar.activation(gateT[:, m, :], ps_gate[:, m * S:(m + 1) * S], ACT.Gelu,
                                                    bias=mx.gate_b[:, m:m + 1])
                    last.then_inc(gate_ready, STEP)

                def back(i):
                    act.wait_ge(y_ps, i + STEP)
                    wait_reuse(act, ss_ps, i)
                    nc.scalar.activation(yT[:, :, :], fold(ps_y[:, :], KC), ACT.Copy).then_inc(yT_ready, STEP)

                def state(i):
                    act.wait_ge(ss_ps, i + STEP)
                    wait_reuse(act, mix_ready, i)
                    for m in range(KC):
                        last = nc.scalar.activation(ssT[:, m, :], ps_ss[:, m * S:(m + 1) * S], ACT.Gelu,
                                                    bias=mx.ss_b[:, m:m + 1])
                    last.then_inc(ss_ready, STEP)

                take(0)
                gate(0)
                def batch(i):
                    back(i)
                    take(i + STEP)
                    state(i)
                    gate(i + STEP)

                each_batch(act, batch, last_base - STEP)
                back(last_base)
                state(last_base)

            @block.vector
            def _(dve):
                def spectrum(j):
                    dve.wait_ge(u_ps, j + STEP)
                    wait_reuse(dve, yf_ready, j)
                    nc.vector.tensor_tensor(prod[:, 0, :], ps_re[:, :], mx.spec_re[:, :], ALU.mult)
                    nc.vector.tensor_tensor(prod[:, 1, :], ps_im[:, :], mx.spec_im[:, :], ALU.mult)
                    nc.vector.tensor_tensor(prod[:, 2, :], ps_re[:, :], mx.spec_im[:, :], ALU.mult)
                    nc.vector.tensor_tensor(prod[:, 3, :], ps_im[:, :], mx.spec_re2[:, :], ALU.mult)\
                        .then_inc(prod_ready, STEP)

                def back(i):
                    dve.wait_ge(out_ps, i + STEP)
                    dve.wait_ge(xr_ready, i + STEP)
                    wait_reuse(dve, norm.done, i)
                    nc.vector.tensor_tensor(norm.y[:, :, :], fold(ps_out[:, :], QT), xr[:, :, :], ALU.add)\
                        .then_inc(norm.summed, STEP)
                    norm.vector_moments(nc, dve, i)
                    norm.vector_scale(nc, dve, i, g.x_all)

                spectrum(0)
                def batch(i):
                    spectrum(i + STEP)
                    back(i)

                each_batch(dve, batch, last_base - STEP)
                back(last_base)


def attention_phase(nc, a, g, tag, w, *, cross, causal, top, project, scale,
                    loads=()):
    UNITS = QT * HP
    HALF = UNITS // KC
    PAIRS = HP // KC
    GROUP = 1 if top else PAIRS
    PROBS = 2 if top else 4
    TURNED = 2 * GROUP
    LAG = 1 if top else 2
    AHEAD = 2 if top else 3

    def unit(u):
        u %= UNITS
        return u // HALF, u // PAIRS % QT, u % PAIRS

    def keys(qt):
        return qt + 1 if causal else QT

    with ExitStack() as stack:
        core = Core(nc, stack)
        xb = core.sb(f"{tag}_xb", [P, QT, D])
        xT = core.sb(f"{tag}_xT", [P, KC, S])
        cT = core.sb(f"{tag}_cT", [P, KC, S]) if cross else xT
        qT = core.sb(f"{tag}_qT", [P, KC, S])
        kz = core.sb(f"{tag}_kz", [P, KC, 2 if top else NH // KC, S])
        val = core.sb(f"{tag}_val", [P, QT, HP * 4 * DK])
        prob = core.sb(f"{tag}_prob", [P, PROBS, 2, S])
        if top:
            turned_weights = core.sb(f"{tag}_probT", [P, TURNED, 2, QT, P])
        else:
            group_weights = [core.sb(f"{tag}_probT{qt}", [P, GROUP, 2, keys(qt), P]) for qt in range(QT)]
        sums = core.sb(f"{tag}_sums", [P, PROBS, 2])
        inverse = core.sb(f"{tag}_inverse", [P, PROBS, 2])
        neg_max = core.sb(f"{tag}_neg_max", [P, 4, 2])
        ctxT = core.sb(f"{tag}_ctxT", [P, KC, S])
        if top:
            top8 = core.sb(f"{tag}_top8", [P, 2, 2, KEPT // 8, 8])
            top_exp = core.sb(f"{tag}_top_exp", [P, 2, KEPT])
            scores = core.sb(f"{tag}_scores", [P, 2, 2, S])
            rest = core.sb(f"{tag}_rest", [P, 2, 2, 2, S])
            kept = core.sb(f"{tag}_kept", [P, 2, 2, S])
            bk = core.sb(f"{tag}_bk_masked", [P, KC, 2])
        bq = core.sb(f"{tag}_bq_scaled", [P, KC]) if w.bq is not None else None
        carrier = core.sem(f"{tag}_carrier")
        bq_ready = core.sem(f"{tag}_bq_ready")
        norm = Norm(core, tag)
        s_banks = [core.ps(f"{tag}_s{n}") for n in range(AHEAD)]
        t_bank = [core.ps(f"{tag}_t{n}") for n in range(2)]
        o_banks = [core.ps(f"{tag}_o{n}") for n in range(5 - AHEAD - 1)]
        j_bank = [core.ps(f"{tag}_j{n}") for n in range(2)]
        names = ("xb_ready cT_loaded xT_ps xT_ready q_ready qk_ps k_ready v_ps v_ready s_ps s_read "
                 "max_ready topk_ready top_step neg_ready kept_ready dropped_ready subtracted inverse_ready p_ready tp_ps "
                 "pt_ready av_ps ctx_ready o_ps xr_ready val_zeroed bk_ready").split()
        (xb_ready, cT_loaded, xT_ps, xT_ready, q_ready, qk_ps, k_ready, v_ps, v_ready, s_ps, s_read,
         max_ready, topk_ready, top_step, neg_ready, kept_ready, dropped_ready, subtracted, inverse_ready, p_ready, tp_ps,
         pt_ready, av_ps, ctx_ready, o_ps, xr_ready, val_zeroed, bk_ready) = (
            core.sem(f"{tag}_{n}") for n in names)
        last_base = (B - 1) * STEP

        def probT(u):
            if top:
                return turned_weights[:, u % TURNED, :, :, :]
            _, qt, j = unit(u)
            return group_weights[qt][:, j, :, :, :]

        def s_bank(n, u):
            return s_banks[(UNITS * n + u) % AHEAD]

        def o_bank(m):
            return o_banks[m][:, 0:S] if len(o_banks) == KC else o_banks[0][:, m * S:(m + 1) * S]

        def batches(engine, body):
            body(0, 0, True, False)
            assert (B - 2) % AHEAD == 0
            with engine.Fori(STEP, last_base - AHEAD * STEP + 1, AHEAD * STEP) as i:
                for n in range(AHEAD):
                    body(i + n * STEP if n else i, (n + 1) % AHEAD, False, False)
            body(last_base, (B - 1) % AHEAD, False, True)

        with nc.Block() as block:

            @block.sync
            def _(sp):
                def load(j):
                    wait_reuse(sp, v_ps, j)
                    b_rows = KC * P // STEP
                    src = a["ctxT"][bass.ds(j * b_rows, KC * P), :]
                    sp.dma_start(cT[:, :, :], src.rearrange("(k p) s -> p k s", p=P)).then_inc(cT_loaded, 16)

                for load_more in loads:
                    load_more(sp)
                if cross:
                    each_batch(sp, load)

            @block.gpsimd
            def _(pool):
                def take(j):
                    wait_reuse(pool, xT_ps, j)
                    nc.gpsimd.tensor_copy(xb[:, :, :].rearrange("p t c -> p (t c)"), batch_of(g.x_all, j))\
                        .then_inc(xb_ready, STEP)

                def residual(i):
                    wait_reuse(pool, norm.done, i)
                    if w.bo is None:
                        nc.gpsimd.tensor_copy(norm.y[:, :, :].rearrange("p t c -> p (t c)"),
                                              batch_of(g.x_all, i)).then_inc(xr_ready, STEP)
                    else:
                        nc.gpsimd.tensor_tensor(norm.y[:, :, :], fold(batch_of(g.x_all, i), QT),
                                                spread(w.bo[:, :], QT, 1), ALU.add).then_inc(xr_ready, STEP)

                def weights(i, u):
                    slot = prob[:, u % PROBS, :, :]
                    if top:
                        pool.wait_ge(dropped_ready, i + u + 1)
                        nc.gpsimd.tensor_tensor(inverse[:, u % PROBS, :], sums[:, u % PROBS, :],
                                                g.minus_one[:, :], ALU.pow).then_inc(inverse_ready, 1)
                        nc.gpsimd.tensor_tensor(slot, kept[:, u % 2, :, :], slot, ALU.subtract)\
                            .then_inc(subtracted, 1)
                        pool.wait_ge(subtracted, i + u + 1)
                        n = S
                    else:
                        n = keys(unit(u)[1]) * P
                    pool.wait_ge(inverse_ready, i + u + 1)
                    nc.gpsimd.tensor_tensor(slot[:, :, 0:n], slot[:, :, 0:n],
                                            spread(inverse[:, u % PROBS, :], n, 2), ALU.mult)\
                        .then_inc(p_ready, 1)

                nc.gpsimd.memset(val[:, :, :], 0.0).then_inc(val_zeroed, 1)
                pool.wait_ge(w.loaded, w.loads)
                take(0)

                def body(i, n, first, last):
                    for u in range(UNITS):
                        weights(i, u)
                        if u == 3 and not last:
                            take(i + STEP)
                        if u == 8 and not first:
                            norm.pool_rstd(nc, pool, i - STEP, g.minus_half)
                        if u == 12:
                            residual(i)

                batches(pool, body)
                norm.pool_rstd(nc, pool, last_base, g.minus_half)

            @block.tensor
            def _(pe):
                def turn_x(j):
                    pe.wait_ge(xb_ready, j + STEP)
                    wait_reuse(pe, v_ready, j)
                    for k in range(KC):
                        for t in range(QT):
                            last = nc.tensor.transpose(j_bank[1][:, k * S + t * P:k * S + (t + 1) * P],
                                                       xb[:, t, k * P:(k + 1) * P], g.ident[:, :])
                    last.then_inc(xT_ps, STEP)

                def project_q(j, m):
                    if m == 0:
                        pe.wait_ge(xT_ready, j + STEP)
                        if cross:
                            pe.wait_ge(cT_loaded, j + STEP)
                        wait_reuse(pe, norm.summed, j - STEP)
                    else:
                        pe.wait_ge(v_ready, j + HALF)
                    for k in range(KC):
                        nc.tensor.matmul(j_bank[m][:, 0:S], w.wq[:, k * D + m * P:k * D + (m + 1) * P],
                                         xT[:, k, :], start=k == 0, stop=k == KC - 1)

                def project_k(j, m):
                    for k in range(KC):
                        last = nc.tensor.matmul(j_bank[m][:, S:2 * S], w.wk[:, k * D + m * P:k * D + (m + 1) * P],
                                                cT[:, k, :], start=k == 0, stop=k == KC - 1)
                    last.then_inc(qk_ps, HALF)

                def project_v(j, m, t):
                    if m == 1 and t == 0:
                        pe.wait_ge(q_ready, j + STEP)
                        pe.wait_ge(k_ready, j + STEP)
                    for k in range(KC):
                        last = nc.tensor.matmul(j_bank[1][:, t * P:(t + 1) * P], cT[:, k, t * P:(t + 1) * P],
                                                w.wv[:, k * D + m * P:k * D + (m + 1) * P],
                                                start=k == 0, stop=k == KC - 1)
                    if t == QT - 1:
                        last.then_inc(v_ps, HALF)

                def score(i, n, u):
                    m, qt, j = unit(u)
                    if u % HALF == 0:
                        pe.wait_ge(q_ready, i + u + HALF)
                    if qt == 0 and (not top or j == 0):
                        pe.wait_ge(k_ready, i + u // HALF * HALF + (HALF if top else 2 * j + 2))
                    wait_reuse(pe, s_read, i + u + 1 - AHEAD)
                    seen = keys(qt) * P
                    out = fold(s_bank(n, u)[:, :], 2)[:, :, 0:seen]
                    if top:
                        rows = slice(32 * j, 32 * j + 32)
                        moving = kz[rows, m, :, 0:seen]
                    else:
                        rows = slice(0, P)
                        moving = kz[:, m, 2 * j:2 * j + 2, 0:seen]
                    last = nc.tensor.matmul(out, qT[rows, m, qt * P:(qt + 1) * P], moving,
                                            start=True, stop=not causal)
                    if causal:
                        last = nc.tensor.matmul(out[:, :, qt * P:(qt + 1) * P], g.ident16[:, :],
                                                g.causal16[:, :, :], start=False, stop=True)
                    last.then_inc(s_ps, 1)

                def turn(i, u):
                    n_keys = keys(unit(u)[1])
                    pe.wait_ge(p_ready, i + u + 1)
                    wait_reuse(pe, pt_ready, i + u - 1)
                    for h in range(2):
                        for kt in range(n_keys):
                            c = (h * QT + kt) * P
                            last = nc.tensor.transpose(t_bank[u % 2][:, c:c + P],
                                                       prob[:, u % PROBS, h, kt * P:(kt + 1) * P], g.ident[:, :])
                    last.then_inc(tp_ps, 1)

                def gather(i, u):
                    m, qt, j = unit(u)
                    pe.wait_ge(pt_ready, i + u + 1)
                    if (u + 1) % HALF == GROUP % HALF:
                        pe.wait_ge(v_ready, i + (u // HALF + 1) * HALF)
                        wait_reuse(pe, ctx_ready, i + (u // HALF + 1 - len(o_banks)) * HALF)
                    steps = [(h, kt) for h in range(2) for kt in range(keys(qt))]
                    for h, kt in steps:
                        for member in range(u - GROUP + 1, u + 1):
                            pair = unit(member)[2]
                            at = ((m * PAIRS + pair) * 2 + h) * 2 * DK
                            last = nc.tensor.matmul(
                                o_bank(m)[32 * pair:32 * pair + 32, qt * P:(qt + 1) * P],
                                val[:, kt, at:at + 2 * DK], probT(member)[:, h, kt, :],
                                start=(h, kt) == steps[0], stop=(h, kt) == steps[-1])
                    last.then_inc(av_ps, GROUP)

                def tail(i, qt):
                    if qt == 0:
                        pe.wait_ge(ctx_ready, i + STEP)
                    for k in range(KC):
                        piece = ctxT[:, k, qt * P:(qt + 1) * P]
                        if project:
                            last = nc.tensor.matmul(j_bank[0][:, qt * D:(qt + 1) * D], piece,
                                                    w.wo[:, k * D:(k + 1) * D], start=k == 0, stop=k == KC - 1)
                        else:
                            last = nc.tensor.transpose(j_bank[0][:, qt * D + k * P:qt * D + (k + 1) * P],
                                                       piece, g.ident[:, :])
                    if qt == QT - 1:
                        last.then_inc(o_ps, STEP)

                def behind(i, first, u):
                    if u >= LAG or not first:
                        turn(i, u - LAG)
                    if (u - LAG) % GROUP == 0 and (u > LAG or not first):
                        gather(i, u - LAG - 1)

                pe.wait_ge(w.loaded, w.loads)
                pe.wait_ge(val_zeroed, 1)
                turn_x(0)
                project_q(0, 0)
                project_k(0, 0)
                project_v(0, 0, 0)
                project_v(0, 0, 1)
                for u in range(AHEAD):
                    score(0, 0, u)

                def body(i, n, first, last):
                    for u in range(UNITS):
                        if u + AHEAD < UNITS or not last:
                            score(i, n, u + AHEAD)
                        behind(i, first, u)
                        if u == 1:
                            project_q(i, 1)
                        if u == 2:
                            project_k(i, 1)
                        if u in (4, 5) and not first:
                            tail(i - STEP, u - 4)
                        if u in (7, 8):
                            project_v(i, 1, u - 7)
                        if u == 9 and not last:
                            turn_x(i + STEP)
                        if u == 10 and not last:
                            project_q(i + STEP, 0)
                        if u == 11 and not last:
                            project_k(i + STEP, 0)
                        if u in (12, 13) and not last:
                            project_v(i + STEP, 0, u - 12)

                batches(pe, body)
                for u in range(UNITS, UNITS + LAG):
                    behind(last_base, False, u)
                gather(last_base, UNITS - 1)
                for qt in range(QT):
                    tail(last_base, qt)

            @block.scalar
            def _(act):
                if w.bq is not None:
                    act.wait_ge(w.loaded, w.loads)
                    nc.scalar.mul(bq[:, :], w.bq[:, :], scale).then_inc(bq_ready, 1)
                    act.wait_ge(bq_ready, 1)
                if top:
                    act.wait_ge(bk_ready, 1)
                act.wait_ge(val_zeroed, 1)

                def take_x(j):
                    act.wait_ge(xT_ps, j + STEP)
                    wait_reuse(act, v_ps, j)
                    nc.scalar.activation(xT[:, :, :], fold(j_bank[1][:, :], KC), ACT.Copy)\
                        .then_inc(xT_ready, STEP)

                def queries(j, m):
                    act.wait_ge(qk_ps, j + (m + 1) * HALF)
                    wait_reuse(act, s_ps, j + (m - 1) * HALF)
                    if w.bq is None:
                        last = nc.scalar.activation(qT[:, m, :], j_bank[m][:, 0:S], ACT.Copy, scale=scale)
                    else:
                        last = nc.scalar.activation(qT[:, m, :], j_bank[m][:, 0:S], ACT.Identity,
                                                    bias=bq[:, m:m + 1], scale=scale)
                    last.then_inc(q_ready, HALF)
                    if top:
                        for h in range(2):
                            last = nc.scalar.activation(kz[:, m, h, :], j_bank[m][:, S:2 * S], ACT.Identity,
                                                        bias=bk[:, m, h:h + 1], scale=g.pair_mask[:, h:h + 1])
                        last.then_inc(k_ready, HALF)

                def key_rows(j, m, pair):
                    if pair == 0:
                        act.wait_ge(qk_ps, j + (m + 1) * HALF)
                        wait_reuse(act, s_ps, j + (m - 1) * HALF)
                    for h in (2 * pair, 2 * pair + 1):
                        nc.scalar.activation(kz[:, m, h, :], j_bank[m][:, S:2 * S], ACT.Copy,
                                             scale=g.head_mask[:, h:h + 1]).then_inc(k_ready, 1)

                def values(j, m):
                    act.wait_ge(v_ps, j + (m + 1) * HALF)
                    wait_reuse(act, av_ps, j + (m - 1) * HALF)
                    for t in range(QT):
                        width = PAIRS * 4 * DK
                        out = val[:, t, m * width:(m + 1) * width].rearrange(
                            "p (pair group c) -> p pair group c", pair=PAIRS, c=DK)[:, :, 0:4:3, :]
                        src = j_bank[1][:, t * P:(t + 1) * P].rearrange(
                            "p (pair head c) -> p pair head c", pair=PAIRS, c=DK)
                        last = nc.scalar.activation(out, src, ACT.Copy)
                    last.then_inc(v_ready, HALF)

                def exponentials(i, n, u):
                    seen = keys(unit(u)[1]) * P
                    act.wait_ge(max_ready, i + u + 1)
                    wait_reuse(act, tp_ps, i + u + 1 - PROBS)
                    for h in range(2):
                        last = nc.scalar.activation(prob[:, u % PROBS, h, 0:seen],
                                                    s_bank(n, u)[:, h * S:h * S + seen], ACT.Exp,
                                                    bias=neg_max[:, u % 4, h:h + 1],
                                                    accum_out=sums[:, u % PROBS, h:h + 1])
                    last.then_inc(s_read, 1)

                def copy_scores(i, n, u):
                    act.wait_ge(s_ps, i + u + 1)
                    wait_reuse(act, kept_ready, i + u - 1)
                    nc.scalar.activation(scores[:, u % 2, :, :], fold(s_bank(n, u)[:, :], 2), ACT.Copy)\
                        .then_inc(s_read, 1)

                def top_exponentials(i, u):
                    act.wait_ge(topk_ready, i + u + 1)
                    wait_reuse(act, subtracted, i + u - 1)
                    wait_reuse(act, tp_ps, i + u - 1)
                    nc.scalar.mul(neg_max[:, u % 4, :], top8[:, u % 2, :, 0, 0], -1.0).then_inc(neg_ready, 1)
                    act.wait_ge(neg_ready, i + u + 1)
                    for h in range(2):
                        last = nc.scalar.activation(kept[:, u % 2, h, :], scores[:, u % 2, h, :], ACT.Exp,
                                                    bias=neg_max[:, u % 4, h:h + 1])
                    last.then_inc(kept_ready, 1)
                    for h in range(2):
                        nc.scalar.activation(top_exp[:, h, :], top8[:, u % 2, h, :, :].rearrange("p r c -> p (r c)"),
                                             ACT.Exp, bias=neg_max[:, u % 4, h:h + 1],
                                             accum_out=sums[:, u % PROBS, h:h + 1])
                    for h in range(2):
                        last = nc.scalar.activation(prob[:, u % 2, h, :], rest[:, u % 2, 1, h, :], ACT.Exp,
                                                    bias=neg_max[:, u % 4, h:h + 1])
                    last.then_inc(dropped_ready, 1)

                def turned(i, u):
                    act.wait_ge(tp_ps, i + u + 1)
                    wait_reuse(act, av_ps, i + u + 1 - TURNED)
                    nc.scalar.activation(probT(u).rearrange("p h k c -> p (h k c)"),
                                         t_bank[u % 2][:, :], ACT.Copy).then_inc(pt_ready, 1)

                def context(i, m):
                    act.wait_ge(av_ps, i + (m + 1) * HALF)
                    if m == 0:
                        wait_reuse(act, o_ps, i)
                    nc.scalar.activation(ctxT[:, m, :], o_bank(m), ACT.Copy).then_inc(ctx_ready, HALF)

                take_x(0)
                queries(0, 0)
                if not top:
                    for pair in range(PAIRS):
                        key_rows(0, 0, pair)
                if w.bv is None:
                    values(0, 0)
                if top:
                    copy_scores(0, 0, 0)

                def body(i, n, first, last):
                    for u in range(UNITS):
                        if top:
                            if u + 1 < UNITS or not last:
                                copy_scores(i, n, u + 1)
                            top_exponentials(i, u)
                            if u >= 1 or not first:
                                turned(i, u - 1)
                        else:
                            exponentials(i, n, u)
                        if u == 3:
                            if not first:
                                context(i - STEP, 1)
                            queries(i, 1)
                        if not top and u in (3, 4, 5, 6):
                            key_rows(i, 1, u - 3)
                        if u == 9 and w.bv is None:
                            values(i, 1)
                        if u == 10 and not last:
                            take_x(i + STEP)
                        if u == 11:
                            context(i, 0)
                        if u == 12 and not last:
                            queries(i + STEP, 0)
                        if not top and u in (12, 13, 14, 15) and not last:
                            key_rows(i + STEP, 0, u - 12)
                        if u == 14 and not last and w.bv is None:
                            values(i + STEP, 0)

                batches(act, body)
                if top:
                    turned(last_base, UNITS - 1)
                context(last_base, 1)

            @block.vector
            def _(dve):
                def values(j, m):
                    dve.wait_ge(v_ps, j + (m + 1) * HALF)
                    wait_reuse(dve, av_ps, j + (m - 1) * HALF)
                    for t in range(QT):
                        width = PAIRS * 4 * DK
                        out = val[:, t, m * width:(m + 1) * width].rearrange(
                            "p (pair group c) -> p pair group c", pair=PAIRS, c=DK)[:, :, 0:4:3, :]
                        src = j_bank[1][:, t * P:(t + 1) * P].rearrange(
                            "p (pair head c) -> p pair head c", pair=PAIRS, c=DK)
                        bias = w.bv[:, m * P:(m + 1) * P].rearrange(
                            "p (pair head c) -> p pair head c", pair=PAIRS, c=DK)
                        last = nc.vector.tensor_tensor(out, src, bias, ALU.add)
                    last.then_inc(v_ready, HALF)

                def maxima(i, n, u):
                    seen = keys(unit(u)[1]) * P
                    dve.wait_ge(s_ps, i + u + 1)
                    nc.vector.tensor_reduce(neg_max[:, u % 4, :], fold(s_bank(n, u)[:, :], 2)[:, :, 0:seen],
                                            AX.X, ALU.max, negate=True).then_inc(max_ready, 1)

                def invert(i, u):
                    dve.wait_ge(s_read, i + u + 1)
                    nc.vector.reciprocal(inverse[:, u % PROBS, :], sums[:, u % PROBS, :])\
                        .then_inc(inverse_ready, 1)

                def turned(i, u):
                    n_keys = keys(unit(u)[1])
                    dve.wait_ge(tp_ps, i + u + 1)
                    wait_reuse(dve, av_ps, i + GROUP * ((u - TURNED) // GROUP + 1))
                    src = t_bank[u % 2][:, :].rearrange("p (h k c) -> p h k c", h=2, k=QT)
                    nc.vector.tensor_copy(probT(u), src[:, :, 0:n_keys, :])\
                        .then_inc(pt_ready, 1)

                def select(i, u):
                    dve.wait_ge(s_read, i + u + 1)
                    wait_reuse(dve, dropped_ready, i + u - 1)
                    dve.sem_inc(carrier, 1)
                    rounds = KEPT // 8
                    steps = 4 * rounds - 1
                    base = (i + u) * steps
                    for r in range(rounds):
                        src = [scores[:, u % 2, h, :] if r == 0 else rest[:, u % 2, (r - 1) % 2, h, :]
                               for h in range(2)]
                        for h in range(2):
                            if r > 0:
                                dve.wait_ge(top_step, base + 4 * r - 1 + h)
                                dve.sem_inc(carrier, 1)
                            nc.vector.max(top8[:, u % 2, h, r, :], src[h]).then_inc(top_step, 1)
                        for h in range(2):
                            dve.wait_ge(top_step, base + 4 * r + 1 + h)
                            dve.sem_inc(carrier, 1)
                            last = nc.vector.match_replace(rest[:, u % 2, r % 2, h, :],
                                                           top8[:, u % 2, h, r, :], src[h], NEG)
                            last.then_inc(*((top_step, 1) if (r, h) != (rounds - 1, 1) else (topk_ready, 1)))

                def add(i):
                    dve.wait_ge(o_ps, i + STEP)
                    dve.wait_ge(xr_ready, i + STEP)
                    nc.vector.tensor_tensor(norm.y[:, :, :], fold(j_bank[0][:, :], QT), norm.y[:, :, :], ALU.add)\
                        .then_inc(norm.summed, STEP)

                dve.wait_ge(w.loaded, w.loads)
                if top:
                    for m in range(KC):
                        last = nc.vector.tensor_scalar(bk[:, m, :], g.pair_mask[:, :], w.bk[:, m:m + 1], None,
                                                       ALU.mult)
                    last.then_inc(bk_ready, 1)
                dve.wait_ge(val_zeroed, 1)
                if w.bv is not None:
                    values(0, 0)

                if not top:
                    maxima(0, 0, 0)

                def body(i, n, first, last):
                    for u in range(UNITS):
                        if top:
                            select(i, u)
                        else:
                            if u + 1 < UNITS or not last:
                                maxima(i, n, u + 1)
                            if u >= 1 or not first:
                                invert(i, u - 1)
                            if u > LAG or not first:
                                turned(i, u - LAG - 1)
                        if u == 6 and not first:
                            add(i - STEP)
                        if u == 7 and not first:
                            norm.vector_moments(nc, dve, i - STEP)
                        if u == 9 and w.bv is not None:
                            values(i, 1)
                        if u == 10 and not first:
                            norm.vector_scale(nc, dve, i - STEP, g.x_all)
                        if u == 14 and not last and w.bv is not None:
                            values(i + STEP, 0)

                batches(dve, body)
                if not top:
                    invert(last_base, UNITS - 1)
                    for u in range(UNITS, UNITS + LAG + 1):
                        turned(last_base, u - LAG - 1)
                add(last_base)
                norm.vector_moments(nc, dve, last_base)
                norm.vector_scale(nc, dve, last_base, g.x_all)


def route_phase(nc, a, g, tag, w, r, xs):
    with ExitStack() as stack:
        core = Core(nc, stack)
        xb = core.sb(f"{tag}_xb", [P, QT, D])
        xT = core.sb(f"{tag}_xT", [P, KC, S])
        hid = core.sb(f"{tag}_hid", [P, KC, S]) if w.rw1 is not None else xT
        logits = core.sb(f"{tag}_logits", [P, NT, E])
        top8 = core.sb(f"{tag}_top8", [P, NT, 8])
        index = core.sb(f"{tag}_index", [P, NT, 8], U32)
        choice = core.sb(f"{tag}_choice", [P, NT, TOPK])
        gap = core.sb(f"{tag}_gap", [P, 3, NT])
        hot = core.sb(f"{tag}_hot", [P, TOPK, NT, E])
        hot16 = core.sb(f"{tag}_hot16", [P, NT * E], BF16)
        total = core.sb(f"{tag}_total", [P, 2, NT, E])
        count = core.sb(f"{tag}_count", [P, NT, E])
        tiles = core.sb(f"{tag}_tiles", [P, 6, E])
        place = core.sb(f"{tag}_place", [P, NT, E])
        placed = core.sb(f"{tag}_placed", [P, TOPK, NT, E])
        slot = core.sb(f"{tag}_slot", [P, TOPK, NT])
        owner = core.sb(f"{tag}_owner", [P, ROUTED, E])
        owned = core.sb(f"{tag}_owned", [P, 2, ROUTED])
        xT_bank, hid_bank, logit_bank, sum_bank = (core.ps(f"{tag}_b{n}") for n in range(4))
        xb_ready, xT_ps, xT_ready, hid_ps, hid_ready, logit_ps, logit_ready = (
            core.sem(f"{tag}_{n}") for n in ("xb_ready", "xT_ps", "xT_ready", "hid_ps", "hid_ready", "logit_ps",
                                             "logit_ready"))
        v, exp_ready, count_ps, hot_ready, scattered, bias_loaded, bias_split, bias_stored, bias_placed = (
            core.sem(f"{tag}_{n}") for n in ("vector_step", "exp_ready", "count_ps", "hot_ready", "scattered",
                                             "bias_loaded", "bias_split", "bias_stored", "bias_placed"))
        bias = core.sb(f"{tag}_bias", [P, 3, E * (U + D) // P])
        parts = core.sb(f"{tag}_parts", [P, 3, E * (U + D) // P], BF16)
        nu = E * U // P

        with nc.Block() as block:

            @block.sync
            def _(sp):
                w.load(sp)
                sp.dma_start(bias[:, 0, 0:nu], w.b_up).then_inc(bias_loaded, 16)
                sp.dma_start(bias[:, 0, nu:], w.b_down).then_inc(bias_loaded, 16)
                sp.wait_ge(bias_split, 5)
                for n in range(3):
                    sp.dma_start(r.bias_dram[n, 0:E * U].rearrange("(p c) -> p c", p=P), parts[:, n, 0:nu])\
                        .then_inc(bias_stored, 16)
                    sp.dma_start(r.bias_dram[n, E * U:].rearrange("(p c) -> p c", p=P), parts[:, n, nu:])\
                        .then_inc(bias_stored, 16)
                sp.wait_ge(bias_stored, 6 * 16)
                sp.dma_start(r.bias[:, :], r.bias_dram[:, :]).then_inc(bias_placed, 16)
                sp.wait_ge(bias_placed, 16)

            @block.gpsimd
            def _(pool):
                def batch(i):
                    wait_reuse(pool, xT_ps, i)
                    nc.gpsimd.tensor_copy(xb[:, :, :].rearrange("p t c -> p (t c)"), batch_of(g.x_all, i))\
                        .then_inc(xb_ready, STEP)

                each_batch(pool, batch)
                pool.wait_ge(bias_loaded, 2 * 16)
                for n in range(3):
                    nc.gpsimd.tensor_copy(parts[:, n, :], bias[:, n, :]).then_inc(bias_split, 1)
                    if n < 2:
                        pool.wait_ge(bias_split, 2 * n + 1)
                        nc.gpsimd.tensor_tensor(bias[:, n + 1, :], bias[:, n, :], parts[:, n, :], ALU.subtract)\
                            .then_inc(bias_split, 1)
                        pool.wait_ge(bias_split, 2 * n + 2)
                pool.wait_ge(g.zeroed, 2 * 16)
                pool.wait_ge(r.slots_ready, 1)
                for k in range(TOPK):
                    for t in range(NT):
                        pool.indirect_dma_start(
                            out=xs[:, :], out_offset=bass.IndirectOffsetOnAxis(
                                ap=r.slots[:, k * NT + t:k * NT + t + 1], axis=0),
                            in_=g.x_all[:, t * D:(t + 1) * D], in_offset=None).then_inc(scattered, 16)
                pool.wait_ge(scattered, TOPK * NT * 16)

            @block.tensor
            def _(pe):
                pe.wait_ge(w.loaded, w.loads)
                def batch(i):
                    pe.wait_ge(xb_ready, i + STEP)
                    wait_reuse(pe, xT_ready, i)
                    for k in range(KC):
                        for t in range(QT):
                            last = nc.tensor.transpose(xT_bank[:, k * S + t * P:k * S + (t + 1) * P],
                                                       xb[:, t, k * P:(k + 1) * P], g.ident[:, :])
                    last.then_inc(xT_ps, STEP)
                    pe.wait_ge(xT_ready, i + STEP)
                    if w.rw1 is not None:
                        wait_reuse(pe, hid_ready, i)
                        for m in range(KC):
                            for k in range(KC):
                                last = nc.tensor.matmul(hid_bank[:, m * S:(m + 1) * S],
                                                        w.rw1[:, k * D + m * P:k * D + (m + 1) * P],
                                                        xT[:, k, :], start=k == 0, stop=k == KC - 1)
                        last.then_inc(hid_ps, STEP)
                        pe.wait_ge(hid_ready, i + STEP)
                    wait_reuse(pe, logit_ready, i)
                    for t in range(QT):
                        for k in range(KC):
                            last = nc.tensor.matmul(logit_bank[:, t * E:(t + 1) * E], hid[:, k, t * P:(t + 1) * P],
                                                    w.router[:, k * E:(k + 1) * E], start=k == 0, stop=k == KC - 1)
                    last.then_inc(logit_ps, STEP)

                each_batch(pe, batch)
                pe.wait_ge(hot_ready, 1)
                nc.tensor.matmul(sum_bank[:, 0:NT * E], g.before16[:, :], hot16[:, :], start=True, stop=True)
                nc.tensor.matmul(sum_bank[:, NT * E:2 * NT * E], g.ones16[:, :], hot16[:, :],
                                 start=True, stop=True).then_inc(count_ps, 1)

            @block.scalar
            def _(act):
                def batch(i):
                    act.wait_ge(xT_ps, i + STEP)
                    wait_reuse(act, logit_ps, i)
                    nc.scalar.activation(xT[:, :, :], fold(xT_bank[:, :], KC), ACT.Copy).then_inc(xT_ready, STEP)
                    if w.rw1 is not None:
                        act.wait_ge(hid_ps, i + STEP)
                        for m in range(KC):
                            last = nc.scalar.activation(hid[:, m, :], hid_bank[:, m * S:(m + 1) * S], ACT.Silu,
                                                        bias=w.rb1[:, m:m + 1])
                        last.then_inc(hid_ready, STEP)

                each_batch(act, batch)
                act.wait_ge(v, 2)
                nc.scalar.activation(gap[:, 1, :], gap[:, 0, :], ACT.Exp).then_inc(exp_ready, 1)

            @block.vector
            def _(dve):
                done = [0]

                def step(instruction):
                    done[0] += 1
                    instruction.then_inc(v, 1)
                    dve.wait_ge(v, done[0])

                def batch(i):
                    dve.wait_ge(logit_ps, i + STEP)
                    step_e = QT * E // STEP
                    out = fold(logits[:, :, :].rearrange("p t e -> p (t e)")[:, bass.ds(i * step_e, QT * E)], QT)
                    src = fold(logit_bank[:, 0:QT * E], QT)
                    if w.rb2 is None:
                        nc.vector.tensor_copy(out, src).then_inc(logit_ready, STEP)
                    else:
                        nc.vector.tensor_tensor(out, src, spread(w.rb2[:, :], QT, 1), ALU.add)\
                            .then_inc(logit_ready, STEP)

                each_batch(dve, batch)
                dve.wait_ge(logit_ready, B * STEP)
                for t in range(NT):
                    last = nc.vector.max(top8[:, t, :], logits[:, t, :])
                step(last)
                step(nc.vector.tensor_tensor(gap[:, 0, :], top8[:, :, 1], top8[:, :, 0], ALU.subtract))
                for t in range(NT):
                    last = nc.vector.max_index(index[:, t, :], top8[:, t, :], logits[:, t, :])
                step(last)
                step(nc.vector.tensor_copy(choice[:, :, :], index[:, :, 0:TOPK]))
                for k in range(TOPK):
                    last = nc.vector.tensor_tensor(hot[:, k, :, :], spread(choice[:, :, k], E, 2),
                                                   spread(g.iota[:, 0:E], NT, 1), ALU.is_equal)
                step(last)
                nc.vector.tensor_tensor(hot16[:, :], hot[:, 0, :, :].rearrange("p t e -> p (t e)"),
                                        hot[:, 1, :, :].rearrange("p t e -> p (t e)"), ALU.add)\
                    .then_inc(hot_ready, 1)
                dve.wait_ge(exp_ready, 1)
                step(nc.vector.tensor_scalar(gap[:, 2, :], gap[:, 1, :], 1.0, None, ALU.add))
                step(nc.vector.reciprocal(r.weights[:, 0:NT], gap[:, 2, :]))
                nc.vector.tensor_tensor(r.weights[:, NT:2 * NT], gap[:, 1, :], r.weights[:, 0:NT], ALU.mult)
                dve.wait_ge(count_ps, 1)
                nc.vector.tensor_copy(place[:, :, :], fold(sum_bank[:, 0:NT * E], NT))
                nc.vector.tensor_copy(count[:, :, :], fold(sum_bank[:, NT * E:2 * NT * E], NT))
                step(nc.vector.tensor_copy(total[:, 0, :, :], fold(sum_bank[:, NT * E:2 * NT * E], NT)))
                side, reach = 0, 1
                while reach < NT:
                    nc.vector.tensor_copy(total[:, 1 - side, 0:reach, :], total[:, side, 0:reach, :])
                    step(nc.vector.tensor_tensor(total[:, 1 - side, reach:, :], total[:, side, reach:, :],
                                                 total[:, side, 0:NT - reach, :], ALU.add))
                    side, reach = 1 - side, 2 * reach
                step(nc.vector.tensor_scalar(tiles[:, 0, :], total[:, side, NT - 1, :], 127.0, 1.0 / P,
                                             ALU.add, ALU.mult))
                step(nc.vector.tensor_scalar(tiles[:, 1, :], tiles[:, 0, :], -127.0 / 256, None, ALU.add))
                step(nc.vector.tensor_scalar(tiles[:, 2, :], tiles[:, 1, :], 12582912.0, None, ALU.add))
                step(nc.vector.tensor_scalar(tiles[:, 3, :], tiles[:, 2, :], -12582912.0, None, ALU.add))
                src, other, reach = 3, 4, 1
                while reach < E:
                    nc.vector.tensor_copy(tiles[:, other, 0:reach], tiles[:, src, 0:reach])
                    step(nc.vector.tensor_tensor(tiles[:, other, reach:], tiles[:, src, reach:],
                                                 tiles[:, src, 0:E - reach], ALU.add))
                    src, other, reach = other, (5 if other == 4 else 4), 2 * reach
                end = src
                free = 9 - end
                step(nc.vector.tensor_tensor(total[:, 1 - side, :, :], total[:, side, :, :], count[:, :, :],
                                             ALU.subtract))
                step(nc.vector.tensor_tensor(place[:, :, :], place[:, :, :], total[:, 1 - side, :, :], ALU.add))
                nc.vector.memset(tiles[:, free, 0:1], 0.0)
                step(nc.vector.tensor_scalar(tiles[:, free, 1:E], tiles[:, end, 0:E - 1], float(P), None,
                                             ALU.mult))
                step(nc.vector.tensor_tensor(place[:, :, :], place[:, :, :], spread(tiles[:, free, :], NT, 1),
                                             ALU.add))
                for k in range(TOPK):
                    last = nc.vector.tensor_tensor(placed[:, k, :, :], hot[:, k, :, :], place[:, :, :], ALU.mult)
                step(last)
                for k in range(TOPK):
                    last = nc.vector.tensor_reduce(slot[:, k, :], placed[:, k, :, :], AX.X, ALU.add)
                step(last)
                nc.vector.tensor_copy(r.slots[:, :], slot[:, :, :].rearrange("p k t -> p (k t)"))\
                    .then_inc(r.slots_ready, 1)
                step(nc.vector.tensor_tensor(owner[:, :, :], spread(g.iota[:, 0:ROUTED], E, 2),
                                             spread(tiles[:, end, :], ROUTED, 1), ALU.is_ge))
                step(nc.vector.tensor_reduce(owned[:, 0, :], owner[:, :, :], AX.X, ALU.add))
                step(nc.vector.tensor_scalar(owned[:, 1, :], owned[:, 0, :], float(E - 1), None, ALU.min))
                nc.vector.tensor_copy(r.expert[:, 0:ROUTED], owned[:, 1, :])


def each_tile(engine, body, n):
    body(0)
    with engine.Fori(1, n) as j:
        body(j)


def expert_phase(nc, a, g, tag, r, xs, ys, func):
    with ExitStack() as stack:
        core = Core(nc, stack)
        xg = core.sb(f"{tag}_xg", [P, D])
        xgT = core.sb(f"{tag}_xgT", [P, KC, P])
        hid = core.sb(f"{tag}_hid", [P, U])
        hidT = core.sb(f"{tag}_hidT", [P, UC, P])
        y = core.sb(f"{tag}_y", [P, D])
        up_bank = [core.ps(f"{tag}_u{n}") for n in range(2)]
        t_bank = [core.ps(f"{tag}_t{n}") for n in range(2)]
        x_bank = core.ps(f"{tag}_x")
        y_bank = core.ps(f"{tag}_yb")
        xg_loaded, xgT_ps, xgT_ready, up_ps, hid_ready, hidT_ps, hidT_ready, down_ps, y_ready, y_stored = (
            core.sem(f"{tag}_{n}") for n in ("xg_loaded", "xgT_ps", "xgT_ready", "up_ps", "hid_ready", "hidT_ps",
                                             "hidT_ready", "down_ps", "y_ready", "y_stored"))
        CH = U // 512
        last_tile = ROUTED - 1

        with nc.Block() as block:

            @block.sync
            def _(sp):
                def load(j):
                    wait_reuse(sp, xgT_ps, j)
                    sp.dma_start(xg[:, :], xs[bass.ds(j * P, P), :]).then_inc(xg_loaded, 16)

                each_tile(sp, load, ROUTED)

            @block.gpsimd
            def _(pool):
                with pool.Fori(0, ROUTED) as j:
                    pool.wait_ge(y_ready, j + 1)
                    pool.dma_start(ys[bass.ds(j * P, P), :], y[:, :]).then_inc(y_stored, 16)
                pool.wait_ge(y_stored, ROUTED * 16)

            @block.tensor
            def _(pe):
                def take(j):
                    pe.wait_ge(xg_loaded, (j + 1) * 16)
                    wait_reuse(pe, xgT_ready, j)
                    for k in range(KC):
                        last = nc.tensor.transpose(x_bank[:, k * P:(k + 1) * P], xg[:, k * P:(k + 1) * P],
                                                   g.ident[:, :])
                    last.then_inc(xgT_ps, 1)

                def up(j):
                    e = pe.value_load(r.expert[0:1, bass.ds(j, 1)], min_val=0, max_val=E - 1)
                    pe.wait_ge(xgT_ready, j + 1)
                    wait_reuse(pe, hid_ready, j * CH)
                    for c in range(CH):
                        for k in range(KC):
                            at = e * (KC * U) + (k * U + c * 512)
                            nc.tensor.matmul(up_bank[c][:, :], xgT[:, k, :], g.w_up[:, bass.ds(at, 512)],
                                             start=k == 0, stop=False)
                        at = e * U + c * 512
                        nc.tensor.matmul(up_bank[c][:, :], g.ones16[0:3, :], r.bias[:, bass.ds(at, 512)],
                                         start=False, stop=True).then_inc(up_ps, 1)

                def turn(j):
                    for c in range(CH):
                        pe.wait_ge(hid_ready, j * CH + c + 1)
                        if c == 0:
                            wait_reuse(pe, hidT_ready, j * CH)
                        for n in range(UC // CH):
                            last = nc.tensor.transpose(t_bank[c][:, n * P:(n + 1) * P],
                                                       hid[:, c * 512 + n * P:c * 512 + (n + 1) * P], g.ident[:, :])
                        last.then_inc(hidT_ps, 1)

                def down(j):
                    e = pe.value_load(r.expert[0:1, bass.ds(j, 1)], min_val=0, max_val=E - 1)
                    wait_reuse(pe, y_ready, j)
                    for c in range(CH):
                        pe.wait_ge(hidT_ready, j * CH + c + 1)
                        for n in range(c * UC // CH, (c + 1) * UC // CH):
                            at = e * (UC * D) + n * D
                            nc.tensor.matmul(y_bank[:, 0:D], hidT[:, n, :], g.w_down[:, bass.ds(at, D)],
                                             start=n == 0, stop=False)
                    at = e * D + E * U
                    nc.tensor.matmul(y_bank[:, 0:D], g.ones16[0:3, :], r.bias[:, bass.ds(at, D)],
                                     start=False, stop=True).then_inc(down_ps, 1)

                pe.wait_ge(g.experts_loaded, (r.layer + 1) * 2 * E * 16)
                take(0)
                up(0)
                take(1)

                def tile(j):
                    turn(j)
                    up(j + 1)
                    take(j + 2)
                    down(j)

                each_tile(pe, tile, last_tile - 1)
                turn(last_tile - 1)
                up(last_tile)
                down(last_tile - 1)
                turn(last_tile)
                down(last_tile)

            @block.scalar
            def _(act):
                def activate(j):
                    for c in range(CH):
                        act.wait_ge(up_ps, j * CH + c + 1)
                        if c == 0:
                            wait_reuse(act, hidT_ps, j * CH)
                        nc.scalar.activation(hid[:, c * 512:(c + 1) * 512], up_bank[c][:, :], func)\
                            .then_inc(hid_ready, 1)

                def result(j):
                    act.wait_ge(down_ps, j + 1)
                    wait_reuse(act, y_stored, j * 16)
                    nc.scalar.activation(y[:, :], y_bank[:, 0:D], ACT.Copy).then_inc(y_ready, 1)

                activate(0)

                def tile(j):
                    activate(j + 1)
                    result(j)

                each_tile(act, tile, last_tile)
                result(last_tile)

            @block.vector
            def _(dve):
                def take(j):
                    dve.wait_ge(xgT_ps, j + 1)
                    wait_reuse(dve, up_ps, j * CH)
                    nc.vector.tensor_copy(xgT[:, :, :], fold(x_bank[:, 0:KC * P], KC)).then_inc(xgT_ready, 1)

                def turned(j):
                    for c in range(CH):
                        dve.wait_ge(hidT_ps, j * CH + c + 1)
                        if c == 0:
                            wait_reuse(dve, down_ps, j)
                        half = UC // CH
                        nc.vector.tensor_copy(hidT[:, c * half:(c + 1) * half, :], fold(t_bank[c][:, :], half))\
                            .then_inc(hidT_ready, 1)

                take(0)
                take(1)

                def tile(j):
                    turned(j)
                    take(j + 2)

                each_tile(dve, tile, last_tile - 1)
                turned(last_tile - 1)
                turned(last_tile)


def combine_phase(nc, a, g, tag, r, ys, twice, out, extra):
    with ExitStack() as stack:
        core = Core(nc, stack)
        rows = core.sb(f"{tag}_rows", [P, 2, TOPK, QT, D])
        index = core.sb(f"{tag}_index", [P, 2, TOPK, QT], U32)
        part = core.sb(f"{tag}_part", [P, 2, QT, D])
        norm = Norm(core, tag)
        index_ready = core.sem(f"{tag}_index_ready")
        part_ready = core.sem(f"{tag}_part_ready")
        both_ready = core.sem(f"{tag}_both_ready")
        carrier = core.sem(f"{tag}_carrier")
        gathered = [core.sem(f"{tag}_gathered{n}") for n in range(2)]
        stored = core.sem(f"{tag}_stored")
        per_pair = TOPK * QT * 16

        with nc.Block() as block:

            @block.gpsimd
            def _(pool):
                def gather(j, s):
                    for k in range(TOPK):
                        col = j // (STEP // QT) + k * NT
                        last = nc.gpsimd.tensor_copy(index[:, s, k, :], r.slots[:, bass.ds(col, QT)])
                    last.then_inc(index_ready, STEP)
                    pool.wait_ge(index_ready, j + STEP)
                    pool.sem_inc(carrier, 1)
                    for k in range(TOPK):
                        for qt in range(QT):
                            pool.indirect_dma_start(
                                out=rows[:, s, k, qt, :], out_offset=None, in_=ys[:, :],
                                in_offset=bass.IndirectOffsetOnAxis(ap=index[:, s, k, qt:qt + 1], axis=0))\
                                .then_inc(gathered[s], 16)

                gather(0, 0)
                gather(STEP, 1)
                with pool.Fori(0, (B - 4) * STEP + 1, 2 * STEP) as i:
                    for s in range(2):
                        norm.pool_rstd(nc, pool, i + s * STEP, g.minus_half)
                        gather(i + (2 + s) * STEP, s)
                for s in range(2):
                    norm.pool_rstd(nc, pool, (B - 2 + s) * STEP, g.minus_half)

            @block.vector
            def _(dve):
                def pair(p):
                    for s in range(2):
                        i = p + s * STEP
                        dve.wait_ge(gathered[s], p * (per_pair // (2 * STEP)) + per_pair)
                        col = i // (STEP // QT)
                        wait_reuse(dve, norm.done, i)
                        for qt in range(QT):
                            last = nc.vector.scalar_tensor_tensor(
                                part[:, 0, qt, :], rows[:, s, 0, qt, :], r.weights[:, bass.ds(col + qt, 1)],
                                tile_of(g.x_all, i, qt), ALU.mult, ALU.add)
                        last.then_inc(part_ready, STEP)
                        dve.wait_ge(part_ready, i + STEP)
                        for qt in range(QT):
                            last = nc.vector.scalar_tensor_tensor(
                                (part[:, 1, qt, :] if twice else norm.y[:, qt, :]), rows[:, s, 1, qt, :],
                                r.weights[:, bass.ds(NT + col + qt, 1)], part[:, 0, qt, :],
                                ALU.mult, ALU.add)
                        if twice:
                            last.then_inc(both_ready, STEP)
                            dve.wait_ge(both_ready, i + STEP)
                            last = nc.vector.tensor_tensor(norm.y[:, :, :], part[:, 1, :, :],
                                                           fold(batch_of(g.x_all, i), QT), ALU.add)
                        last.then_inc(norm.summed, STEP)
                        norm.vector_moments(nc, dve, i)
                        norm.vector_scale(nc, dve, i, g.x_all)

                pair(0)
                with dve.Fori(2 * STEP, (B - 2) * STEP + 1, 2 * STEP) as p:
                    pair(p)

            @block.sync
            def _(sp):
                if extra is not None:
                    extra(sp)
                if out is not None:
                    def batch(i):
                        sp.wait_ge(norm.done, i + STEP)
                        sp.dma_start(out[bass.ds(i * (S // STEP), S), :]
                                     .rearrange("(t p) c -> p t c", p=P),
                                     fold(batch_of(g.x_all, i), QT)).then_inc(stored, 16)

                    each_batch(sp, batch)
                    sp.wait_ge(stored, B * 16)


class Weights:
    wq = wk = wv = wo = bq = bk = bv = bo = rw1 = rb1 = rb2 = router = None

    def __init__(self, core, a, tag, mats=(), cols=(), rows=(), narrow=()):
        self.loaded = core.sem(f"{tag}_loaded")
        self.parts = []
        for attribute, name in mats:
            self.add(attribute, core.sb(f"{tag}_{attribute}", [P, KC * D]),
                     a[name].rearrange("(k p) c -> p k c", p=P), KC)
        for attribute, name in narrow:
            self.add(attribute, core.sb(f"{tag}_{attribute}", [P, KC * E]),
                     a[name].rearrange("(k p) c -> p k c", p=P), KC)
        for attribute, name in cols:
            self.add(attribute, core.sb(f"{tag}_{attribute}", [P, KC]), a[name], 0)
        for attribute, name in rows:
            n = a[name].shape[1]
            self.add(attribute, core.sb(f"{tag}_{attribute}", [P, n]), a[name].broadcast_to([P, n]), 0)
        self.loads = 16 * len(self.parts)

    def add(self, attribute, tile, source, n):
        if attribute == "wq":
            self.wq = tile
        elif attribute == "wk":
            self.wk = tile
        elif attribute == "wv":
            self.wv = tile
        elif attribute == "wo":
            self.wo = tile
        elif attribute == "bq":
            self.bq = tile
        elif attribute == "bk":
            self.bk = tile
        elif attribute == "bv":
            self.bv = tile
        elif attribute == "bo":
            self.bo = tile
        elif attribute == "rw1":
            self.rw1 = tile
        elif attribute == "rb1":
            self.rb1 = tile
        elif attribute == "rb2":
            self.rb2 = tile
        elif attribute == "router":
            self.router = tile
        self.parts.append((fold(tile[:, :], n) if n else tile[:, :], source))

    def load(self, queue):
        for tile, source in self.parts:
            queue.dma_start(tile, source).then_inc(self.loaded, 16)


class Routing:

    def __init__(self, nc, core, tag):
        self.slots = core.sb(f"{tag}_slots", [P, TOPK * NT], U32)
        self.weights = core.sb(f"{tag}_weights", [P, TOPK * NT])
        self.expert = core.sb(f"{tag}_expert", [P, ROUTED + 1], I32)
        self.slots_ready = core.sem(f"{tag}_slots_ready")
        self.bias = core.sb(f"{tag}_bias3", [3, E * (U + D)], BF16)
        self.bias_dram = nc.dram_tensor(f"{tag}_bias_dram", (3, E * (U + D)), BF16)


class Shared:

    def __init__(self, nc, core, a):
        self.nc, self.a = nc, a
        self.x_all = core.sb("x_all", [P, NT * D])
        self.w_up = core.sb("w_up", [P, E * KC * U])
        self.w_down = core.sb("w_down", [P, E * UC * D])
        self.ident = core.sb("ident", [P, P])
        self.ident16 = core.sb("ident16", [P, P], BF16)
        self.before16 = core.sb("before16", [P, P], BF16)
        self.ones16 = core.sb("ones16", [P, P], BF16)
        self.causal16 = core.sb("causal16", [P, 2, P], BF16)
        self.pair_mask = core.sb("pair_mask", [P, 2])
        self.head_mask = core.sb("head_mask", [P, NH // KC])
        self.iota = core.sb("iota", [P, ROUTED])
        self.minus_half = core.sb("minus_half", [P, QT])
        self.minus_one = core.sb("minus_one", [P, 2])
        self.zeros = core.sb("zeros", [P, D])
        self.x_loaded = core.sem("x_loaded")
        self.const_loaded = core.sem("const_loaded")
        self.experts_loaded = core.sem("experts_loaded")
        self.zeroed = core.sem("zeroed")
        self.zero_ready = core.sem("zero_ready")

    def load_experts(self, queue, up, down):
        for e in range(E):
            queue.dma_start(fold(self.w_up[:, e * KC * U:(e + 1) * KC * U], KC),
                            up[e].rearrange("(k p) u -> p k u", p=P)).then_inc(self.experts_loaded, 16)
            queue.dma_start(fold(self.w_down[:, e * UC * D:(e + 1) * UC * D], UC),
                            down[e].rearrange("(n p) c -> p n c", p=P)).then_inc(self.experts_loaded, 16)


class Mixer:

    def __init__(self, core):
        self.dft = core.sb("dft", [P, QT * FFT])
        self.idft = core.sb("idft", [P, NF * S])
        self.spec_re = core.sb("spec_re", [P, KC * D])
        self.spec_re2 = core.sb("spec_re2", [P, KC * D])
        self.spec_im = core.sb("spec_im", [P, KC * D])
        self.ss_w = core.sb("ss_w", [P, KC * D])
        self.gate_w = core.sb("gate_w", [P, KC * D])
        self.fin_w = core.sb("fin_w", [P, KC * D])
        self.ss_b = core.sb("ss_b", [P, KC])
        self.gate_b = core.sb("gate_b", [P, KC])
        self.fin_b = core.sb("fin_b", [P, D])
        self.dft_loaded = core.sem("dft_loaded")
        self.loaded = core.sem("mixer_loaded")
        self.loads = 7 * 16

    def load(self, queue, a):
        queue.dma_start(fold(self.dft[:, :], QT), a["dft"].rearrange("(t p) f -> p t f", p=P))\
            .then_inc(self.dft_loaded, 16)
        for tile, name, n in ((self.idft, "idft", NF), (self.ss_w, "ss_wT", KC), (self.gate_w, "gate_wT", KC),
                              (self.fin_w, "fin_wT", KC)):
            queue.dma_start(fold(tile[:, :], n), a[name].rearrange("(t p) f -> p t f", p=P))\
                .then_inc(self.loaded, 16)
        queue.dma_start(self.ss_b[:, :], a["ss_b"]).then_inc(self.loaded, 16)
        queue.dma_start(self.gate_b[:, :], a["gate_b"]).then_inc(self.loaded, 16)
        queue.dma_start(self.fin_b[:, :], a["fin_b"].broadcast_to([P, D])).then_inc(self.loaded, 16)


def decoder(nc, a, out):
    xs = [nc.dram_tensor(f"xs{n}", (ROUTED * P, D), F32) for n in range(2)]
    ys = [nc.dram_tensor(f"ys{n}", (ROUTED * P, D), F32) for n in range(2)]
    with ExitStack() as stack:
        core = Core(nc, stack)
        g = Shared(nc, core, a)

        with ExitStack() as first:
            w0 = Weights(Core(nc, first), a, "c0", mats=(("wq", "L0_wqT"), ("wk", "L0_wkT"),
                                                         ("wv", "L0_wvT"), ("wo", "L0_woT")))
            with ExitStack() as early:
                mx = Mixer(Core(nc, early))

                def load_first(sp):
                    mx.load(sp, a)
                    w0.load(sp)
                    sp.wait_ge(g.zero_ready, 1)
                    for n in range(2):
                        sp.dma_start(xs[n].rearrange("(t p) c -> p t c", p=P),
                                     spread(g.zeros[:, :], ROUTED, 1)).then_inc(g.zeroed, 16)
                    g.load_experts(sp, a["L0_up"], a["L0_down"])

                kernel_spectrum(nc, a, g, mx, load_first)
                mixer_phase(nc, a, g, mx)
            attention_phase(nc, a, g, "c0", w0, cross=True, causal=True, top=False, project=True,
                            scale=DK ** -0.5)
        experts(nc, a, g, 0, xs[0], ys[0], out)
        with ExitStack() as second:
            ws = Weights(Core(nc, second), a, "s1", mats=(("wq", "L1_wq"), ("wk", "L1_wk"), ("wv", "L1_wv")))

            def prefetch(sp):
                g.load_experts(sp, a["L1_up"], a["L1_down"])

            attention_phase(nc, a, g, "s1", ws, cross=False, causal=False, top=False, project=False,
                            scale=D ** -0.5, loads=(ws.load, prefetch))
        with ExitStack() as third:
            wc = Weights(Core(nc, third), a, "c1", mats=(("wq", "L1_wqT"), ("wk", "L1_wkT"),
                                                         ("wv", "L1_wvT"), ("wo", "L1_woT")),
                         cols=(("bq", "L1_bq"), ("bk", "L1_bk")), rows=(("bv", "L1_bv"), ("bo", "L1_bo")))
            attention_phase(nc, a, g, "c1", wc, cross=True, causal=False, top=True,
                            project=True, scale=DK ** -0.5, loads=(wc.load,))
        experts(nc, a, g, 1, xs[1], ys[1], out)


def experts(nc, a, g, layer, xs, ys, out):
    with ExitStack() as stack:
        core = Core(nc, stack)
        r = Routing(nc, core, f"r{layer}")
        r.layer = layer
        if layer == 0:
            w = Weights(core, a, "t0", narrow=(("router", "L0_router"),))
            w.b_up, w.b_down, func = a["L0_b_up"], a["L0_b_down"], ACT.Gelu
        else:
            w = Weights(core, a, "t1", mats=(("rw1", "L1_rw1"),), narrow=(("router", "L1_rw2"),),
                        cols=(("rb1", "L1_rb1"),), rows=(("rb2", "L1_rb2"),))
            w.b_up, w.b_down, func = a["L1_b_up"], a["L1_b_down"], ACT.Silu
        route_phase(nc, a, g, f"t{layer}", w, r, xs)
        expert_phase(nc, a, g, f"e{layer}", r, xs, ys, func)
        combine_phase(nc, a, g, f"k{layer}", r, ys, layer == 1, out if layer == 1 else None, None)



def _laid_out(i):
    c = np.ascontiguousarray

    def col(v):
        return c(v.reshape(KC, P).T)

    f = np.arange(FFT // 2)
    t = np.arange(S)
    turn = 2 * np.pi * np.outer(t, f) / FFT
    nyquist = (-1.0) ** t
    dft = np.concatenate([np.cos(turn), -np.sin(turn)], axis=1)
    dft[:, FFT // 2] = nyquist
    idft = 2 * np.concatenate([np.cos(turn.T), -np.sin(turn.T)], axis=0) / FFT
    idft[0] = 1 / FFT
    idft[FFT // 2] = nyquist / FFT
    p = np.arange(P)
    const = np.zeros((P, 3 * P + 2 + NH // KC + ROUTED), np.float32)
    const[:, 0:P] = np.eye(P)
    const[:, P:2 * P] = p[:, None] < p[None, :]
    const[:, 2 * P:3 * P] = np.where(p[None, :] > p[:, None], -1e30, 0)
    const[:, 3 * P] = (p // DK) % 2 == 0
    const[:, 3 * P + 1] = (p // DK) % 2 == 1
    const[:, 3 * P + 2:3 * P + 2 + NH // KC] = p[:, None] // DK == np.arange(NH // KC)
    const[:, 3 * P + 2 + NH // KC:] = np.arange(ROUTED)
    qkv = i["L1_attn_w_qkv"]
    return {
        "x": i["x"].reshape(N, D),
        "ctxT": c(i["ctx_1024"].transpose(0, 2, 1)).reshape(B * D, S),
        "decays": i["L0_attn_decays"].reshape(STATES, 1),
        "frequencies": i["L0_attn_frequencies"].reshape(STATES, 1),
        "in_projT": c(i["L0_attn_in_proj"].T),
        "out_proj": i["L0_attn_out_proj"],
        "lag": np.tile(np.arange(S, dtype=np.float32), (STATES, 1)),
        "dft": dft.astype(np.float32), "idft": idft.astype(np.float32), "const": const,
        "ss_wT": c(i["L0_attn_ss_W"].T), "gate_wT": c(i["L0_attn_gate_W"].T), "fin_wT": c(i["L0_attn_fin_W"].T),
        "ss_b": col(i["L0_attn_ss_b"]), "gate_b": col(i["L0_attn_gate_b"]),
        "fin_b": i["L0_attn_fin_b"].reshape(1, D),
        "L0_wqT": c(i["L0_xattn_Wq"].T), "L0_wkT": c(i["L0_xattn_Wk"].T), "L0_wvT": c(i["L0_xattn_Wv"].T),
        "L0_woT": c(i["L0_xattn_Wo"].T),
        "L0_up": c(i["L0_ffn_w_up"].transpose(0, 2, 1)), "L0_down": c(i["L0_ffn_w_down"].transpose(0, 2, 1)),
        "L0_b_up": i["L0_ffn_b_up"].reshape(P, -1), "L0_b_down": i["L0_ffn_b_down"].reshape(P, -1),
        "L0_router": c(i["L0_ffn_w_router"].T),
        "L1_wq": c(qkv[:, 0:D]), "L1_wk": c(qkv[:, D:2 * D]), "L1_wv": c(qkv[:, 2 * D:]),
        "L1_wqT": c(i["L1_xattn_Wq"].T), "L1_wkT": c(i["L1_xattn_Wk"].T), "L1_wvT": c(i["L1_xattn_Wv"].T),
        "L1_woT": c(i["L1_xattn_Wo"].T),
        "L1_bq": col(i["L1_xattn_bq"]), "L1_bk": col(i["L1_xattn_bk"]),
        "L1_bv": i["L1_xattn_bv"].reshape(1, D), "L1_bo": i["L1_xattn_bo"].reshape(1, D),
        "L1_rw1": i["L1_ffn_rw1"], "L1_rb1": col(i["L1_ffn_rb1"]), "L1_rw2": i["L1_ffn_rw2"],
        "L1_rb2": i["L1_ffn_rb2"].reshape(1, E),
        "L1_up": i["L1_ffn_we1"], "L1_down": i["L1_ffn_we2"],
        "L1_b_up": i["L1_ffn_be1"].reshape(P, -1), "L1_b_down": i["L1_ffn_be2"].reshape(P, -1),
    }


def kernel(**inputs):
    import concourse.bacc as bacc
    from concourse.bass_utils import run_bass_kernel_spmd

    arrays = {n: np.ascontiguousarray(v) for n, v in
              _laid_out({n: np.asarray(v) for n, v in inputs.items()}).items()}
    nc = bacc.Bacc("TRN2", target_bir_lowering=False, num_devices=1)
    a = {n: nc.dram_tensor(f"in_{n}", v.shape, F32, kind="ExternalInput").ap() for n, v in arrays.items()}
    out = nc.dram_tensor("out", (N, D), F32, kind="ExternalOutput").ap()
    decoder(nc, a, out)
    result = run_bass_kernel_spmd(nc, [{f"in_{n}": v for n, v in arrays.items()}], core_ids=[0])
    return result.results[0]["out"].reshape(B, S, D)
```

```python
from contextlib import ExitStack

import numpy as np

import concourse.bass as bass
from concourse import mybir

F32 = mybir.dt.float32
BF16 = mybir.dt.bfloat16
I32 = mybir.dt.int32
U32 = mybir.dt.uint32
ALU = mybir.AluOpType
ACT = mybir.ActivationFunctionType
AX = mybir.AxisListType

P = 128
B, S, D = 8, 256, 256
N = B * S
NT = N // P
QT = S // P
KC = D // P
NH, DK = 16, 16
HP = NH // 2
STATES = 64
FFT = 2 * S
NF = FFT // P
E, U, TOPK = 8, 1024, 2
UC = U // P
ROUTED = N * TOPK // P + E - 1
KEPT = 32
EPS = 1e-5
NEG = -3.0e38
STEP = 16


class Core:

    def __init__(self, nc, stack):
        self.nc = nc
        self.stack = stack
        self.sems = []
        stack.callback(self.clear)

    def clear(self):
        if self.sems:
            self.nc.clear_and_free_semaphores(self.sems)
            self.nc.all_engine_barrier()

    def sb(self, name, shape, dtype=F32):
        return self.stack.enter_context(self.nc.sbuf_tensor(name, shape, dtype))

    def ps(self, name, shape=(P, 512), dtype=F32):
        return self.stack.enter_context(self.nc.psum_tensor(name, list(shape), dtype))

    def sem(self, name):
        self.sems.append(self.nc.alloc_semaphore(name))
        return self.sems[-1]


def fold(ap, n):
    return ap.rearrange("p (n c) -> p n c", n=n)


def spread(ap, n, axis):
    shape = list(ap.shape)
    shape.insert(axis, n)
    return ap.unsqueeze(axis).broadcast_to(shape)


def batch_of(x_all, i):
    step = QT * D // STEP
    return x_all[:, bass.ds(i * step, QT * D)]


def tile_of(x_all, i, qt):
    step = QT * D // STEP
    return x_all[:, bass.ds(i * step + qt * D, D)]


def wait_reuse(engine, sem, value):
    if not (isinstance(value, int) and value <= 0):
        engine.wait_ge(sem, value)


def each_batch(engine, body, last=(B - 1) * STEP):
    body(0)
    with engine.Fori(STEP, last + 1, STEP) as i:
        body(i)


class Norm:

    def __init__(self, core, tag):
        self.y = core.sb(f"{tag}_y", [P, QT, D])
        self.stats = core.sb(f"{tag}_stats", [P, QT, 6])
        self.moments = core.sb(f"{tag}_moments", [P, QT, 2])
        self.var = core.sb(f"{tag}_var", [P, QT])
        self.rstd = core.sb(f"{tag}_rstd", [P, QT])
        self.summed = core.sem(f"{tag}_summed")
        self.stats_ready = core.sem(f"{tag}_stats_ready")
        self.moments_ready = core.sem(f"{tag}_moments_ready")
        self.var_ready = core.sem(f"{tag}_var_ready")
        self.rstd_ready = core.sem(f"{tag}_rstd_ready")
        self.done = core.sem(f"{tag}_done")
        self.carrier = core.sem(f"{tag}_norm_carrier")

    def vector_moments(self, nc, dve, i):
        dve.wait_ge(self.summed, i + STEP)
        for qt in range(QT):
            last = nc.vector.bn_stats(self.stats[:, qt, :], self.y[:, qt, :])
        last.then_inc(self.stats_ready, STEP)
        dve.wait_ge(self.stats_ready, i + STEP)
        dve.sem_inc(self.carrier, 1)
        for qt in range(QT):
            last = nc.vector.bn_aggr(self.moments[:, qt, :], self.stats[:, qt, :])
        last.then_inc(self.moments_ready, STEP)

    def pool_rstd(self, nc, pool, i, minus_half):
        pool.wait_ge(self.moments_ready, i + STEP)
        nc.gpsimd.tensor_scalar(self.var[:, :], self.moments[:, :, 1], EPS, None, ALU.add)\
            .then_inc(self.var_ready, STEP)
        pool.wait_ge(self.var_ready, i + STEP)
        nc.gpsimd.tensor_tensor(self.rstd[:, :], self.var[:, :], minus_half[:, 0:QT], ALU.pow)\
            .then_inc(self.rstd_ready, STEP)

    def vector_scale(self, nc, dve, i, x_all, batch=None):
        dve.wait_ge(self.rstd_ready, i + STEP)
        for qt in range(QT):
            last = nc.vector.tensor_scalar(tile_of(x_all, i if batch is None else batch, qt),
                                           self.y[:, qt, :], self.moments[:, qt, 0:1],
                                           self.rstd[:, qt:qt + 1],
                                           ALU.subtract, ALU.mult)
        last.then_inc(self.done, STEP)


def kernel_spectrum(nc, a, g, mx, load_rest):
    with ExitStack() as stack:
        core = Core(nc, stack)
        lag = core.sb("lag", [STATES, S])
        mode = core.sb("mode", [STATES, 6])
        w_in = core.sb("w_in", [STATES, D])
        w_out = core.sb("w_out", [STATES, D])
        w = core.sb("w", [STATES, D])
        damp = core.sb("damp", [STATES, S])
        phase = core.sb("phase", [STATES, S])
        turns = core.sb("turns", [STATES, 2, S])
        rest = core.sb("rest", [STATES, 3, S])
        mag = core.sb("mag", [STATES, 2, S])
        half_pi = core.sb("half_pi", [STATES, 1])
        wave = core.sb("wave", [STATES, S])
        decay_env = core.sb("decay_env", [STATES, S])
        modes = core.sb("modes", [STATES, S])
        k_time = core.sb("k_time", [P, QT, D])
        const = core.sb("const", [P, 4 * P + 3 + NH // KC])
        k_ps = core.ps("k_ps")
        re_ps = core.ps("re_ps")
        im_ps = core.ps("im_ps")
        loaded = core.sem("p0_loaded")
        decayed = core.sem("p0_decayed")
        v = core.sem("p0_vector_step")
        waved = core.sem("p0_waved")
        k_done = core.sem("p0_k_done")
        k_copied = core.sem("p0_k_copied")
        spec_done = core.sem("p0_spec_done")

        with nc.Block() as block:

            @block.sync
            def _(sp):
                sp.dma_start(mode[:, 0:1], a["decays"]).then_inc(loaded, 16)
                sp.dma_start(mode[:, 1:2], a["frequencies"]).then_inc(loaded, 16)
                sp.dma_start(lag[:, :], a["lag"]).then_inc(loaded, 16)
                sp.dma_start(w_in[:, :], a["in_projT"]).then_inc(loaded, 16)
                sp.dma_start(w_out[:, :], a["out_proj"]).then_inc(loaded, 16)
                sp.dma_start(const[:, :], a["const"]).then_inc(g.const_loaded, 16)
                sp.dma_start(fold(g.x_all[:, :], NT), a["x"].rearrange("(t p) c -> p t c", p=P))\
                    .then_inc(g.x_loaded, 16)
                load_rest(sp)

            @block.scalar
            def _(act):
                act.wait_ge(loaded, 5 * 16)
                nc.scalar.activation(mode[:, 2:3], mode[:, 0:1], ACT.Exp).then_inc(decayed, 1)
                act.wait_ge(v, 2)
                nc.scalar.activation(decay_env[:, :], damp[:, :], ACT.Exp, scale=-1.0)\
                    .then_inc(decayed, 1)
                act.wait_ge(v, 12)
                nc.scalar.activation(wave[:, :], mag[:, 1, :], ACT.Sin, bias=half_pi[:, 0:1], scale=-1.0)\
                    .then_inc(waved, 1)
                for t in range(QT):
                    act.wait_ge(k_done, QT)
                    nc.scalar.activation(k_time[:, t, :], k_ps[:, t * D:(t + 1) * D], ACT.Copy)\
                        .then_inc(k_copied, 1)

            @block.vector
            def _(dve):
                def step(instruction, n):
                    instruction.then_inc(v, 1)
                    dve.wait_ge(v, n)

                nc.vector.memset(half_pi[:, :], float(np.pi / 2)).then_inc(v, 1)
                dve.wait_ge(decayed, 1)
                nc.vector.tensor_scalar(damp[:, :], lag[:, :], mode[:, 2:3], None, ALU.mult)\
                    .then_inc(v, 1)
                step(nc.vector.tensor_scalar(mode[:, 3:4], mode[:, 1:2], float(np.float32(2 * np.pi)),
                                             None, ALU.mult), 3)
                step(nc.vector.tensor_scalar(phase[:, :], lag[:, :], mode[:, 3:4], None, ALU.mult), 4)
                step(nc.vector.tensor_scalar(turns[:, 0, :], phase[:, :], float(1 / (2 * np.pi)),
                                             None, ALU.mult), 5)
                step(nc.vector.tensor_scalar(turns[:, 1, :], turns[:, 0, :], 12582912.0, None, ALU.add), 6)
                step(nc.vector.tensor_scalar(turns[:, 0, :], turns[:, 1, :], -12582912.0, None, ALU.add), 7)
                part1 = 6.28125
                part2 = float(np.round((2 * np.pi - part1) * 2.0**17) / 2.0**17)
                part3 = float(2 * np.pi - part1 - part2)
                step(nc.vector.scalar_tensor_tensor(rest[:, 0, :], turns[:, 0, :], -part1, phase[:, :],
                                                    ALU.mult, ALU.add), 8)
                step(nc.vector.scalar_tensor_tensor(rest[:, 1, :], turns[:, 0, :], -part2, rest[:, 0, :],
                                                    ALU.mult, ALU.add), 9)
                step(nc.vector.scalar_tensor_tensor(rest[:, 2, :], turns[:, 0, :], -part3, rest[:, 1, :],
                                                    ALU.mult, ALU.add), 10)
                step(nc.vector.tensor_scalar(mag[:, 0, :], rest[:, 2, :], -1.0, None, ALU.mult), 11)
                nc.vector.tensor_tensor(mag[:, 1, :], rest[:, 2, :], mag[:, 0, :], ALU.max).then_inc(v, 1)
                nc.vector.tensor_tensor(w[:, :], w_in[:, :], w_out[:, :], ALU.mult)
                dve.wait_ge(waved, 1)
                dve.wait_ge(decayed, 2)
                nc.vector.tensor_tensor(modes[:, :], wave[:, :], decay_env[:, :], ALU.mult).then_inc(v, 1)
                dve.wait_ge(spec_done, 1)
                half = KC * D
                nc.vector.tensor_copy(mx.spec_re[:, :], re_ps[:, 0:half])
                nc.vector.tensor_copy(mx.spec_re2[:, :], re_ps[:, 0:half])
                nc.vector.tensor_copy(mx.spec_im[:, :], im_ps[:, 0:half]).then_inc(v, 1)
                dve.wait_ge(v, 14)
                nc.vector.tensor_copy(mx.spec_re2[0:1, 0:D], im_ps[0:1, 0:D])
                nc.vector.memset(mx.spec_im[0:1, 0:D], 0.0)

            @block.tensor
            def _(pe):
                pe.wait_ge(v, 13)
                for t in range(QT):
                    nc.tensor.matmul(k_ps[:, t * D:(t + 1) * D], modes[:, t * P:(t + 1) * P], w[:, :],
                                     start=True, stop=True).then_inc(k_done, 1)
                pe.wait_ge(k_copied, QT)
                pe.wait_ge(mx.dft_loaded, 16)
                for f in range(NF):
                    out = (re_ps, im_ps)[f // 2][:, (f % 2) * D:(f % 2 + 1) * D]
                    for t in range(QT):
                        last = nc.tensor.matmul(out, mx.dft[:, t * FFT + f * P:t * FFT + (f + 1) * P],
                                                k_time[:, t, :], start=t == 0, stop=t == QT - 1)
                last.then_inc(spec_done, 1)

            @block.gpsimd
            def _(pool):
                nc.gpsimd.memset(g.minus_half[:, :], -0.5)
                nc.gpsimd.memset(g.minus_one[:, :], -1.0)
                nc.gpsimd.memset(g.ones16[:, :], 1.0)
                nc.gpsimd.memset(g.ones_row[:, :], 1.0)
                pool.wait_ge(g.const_loaded, 16)
                nc.gpsimd.tensor_copy(g.ident[:, :], const[:, 0:P])
                nc.gpsimd.tensor_copy(g.ident16[:, :], const[:, 0:P])
                nc.gpsimd.tensor_copy(g.before16[:, :], const[:, P:2 * P])
                for h in range(2):
                    nc.gpsimd.tensor_copy(g.causal16[:, h, :], const[:, 2 * P:3 * P])
                nc.gpsimd.tensor_copy(g.pair_mask[:, :], const[:, 3 * P:3 * P + 2])
                nc.gpsimd.tensor_copy(g.head_mask[:, :], const[:, 3 * P + 2:3 * P + 2 + NH // KC])
                nc.gpsimd.tensor_copy(g.iota[:, :], const[:, 3 * P + 2 + NH // KC:-1])
                nc.gpsimd.tensor_copy(g.row[:, :], const[:, 4 * P + 2 + NH // KC:])


def mixer_phase(nc, a, g, mx):
    with ExitStack() as stack:
        core = Core(nc, stack)
        xb = core.sb("m_xb", [P, QT, D])
        xT = core.sb("m_xT", [P, KC, S])
        prod = core.sb("m_prod", [P, 4, KC * D])
        yf = core.sb("m_yf", [P, NF, D])
        yT = core.sb("m_yT", [P, KC, S])
        ssT = core.sb("m_ssT", [P, KC, S])
        gateT = core.sb("m_gateT", [P, KC, S])
        mixT = core.sb("m_mixT", [P, KC, S])
        xr = core.sb("m_xr", [P, QT, D])
        norm = Norm(core, "m")
        ps_xT, ps_re, ps_im, ps_gate, ps_y, ps_ss, ps_out = (core.ps(f"m_ps{n}") for n in range(7))
        xb_ready, xT_ps, xT_ready, u_ps, prod_ready, yf_ready = (
            core.sem(f"m_{n}") for n in ("xb_ready", "xT_ps", "xT_ready", "u_ps", "prod_ready", "yf_ready"))
        gate_ps, gate_ready, y_ps, yT_ready, ss_ps, ss_ready, mix_ready, out_ps, xr_ready = (
            core.sem(f"m_{n}") for n in ("gate_ps", "gate_ready", "y_ps", "yT_ready", "ss_ps", "ss_ready",
                                         "mix_ready", "out_ps", "xr_ready"))
        last_base = (B - 1) * STEP

        with nc.Block() as block:

            @block.gpsimd
            def _(pool):
                def spectrum(j):
                    pool.wait_ge(prod_ready, j + STEP)
                    wait_reuse(pool, y_ps, j)
                    nc.gpsimd.tensor_tensor(yf[:, 0:KC, :], fold(prod[:, 0, :], KC), fold(prod[:, 1, :], KC),
                                            ALU.subtract)
                    nc.gpsimd.tensor_tensor(yf[:, KC:NF, :], fold(prod[:, 2, :], KC), fold(prod[:, 3, :], KC),
                                            ALU.add).then_inc(yf_ready, STEP)

                def back(i):
                    wait_reuse(pool, norm.summed, i)
                    nc.gpsimd.tensor_tensor(xr[:, :, :], fold(batch_of(g.x_all, i), QT),
                                            spread(mx.fin_b[:, :], QT, 1), ALU.add).then_inc(xr_ready, STEP)

                pool.wait_ge(g.x_loaded, 16)
                pool.wait_ge(mx.loaded, mx.loads)
                spectrum(0)

                def batch(i):
                    back(i)
                    spectrum(i + STEP)
                    norm.pool_rstd(nc, pool, i, g.minus_half)

                each_batch(pool, batch, last_base - STEP)
                back(last_base)
                norm.pool_rstd(nc, pool, last_base, g.minus_half)

            @block.tensor
            def _(pe):
                def front(j):
                    pe.wait_ge(xb_ready, j + STEP)
                    wait_reuse(pe, xT_ready, j)
                    for k in range(KC):
                        for t in range(QT):
                            last = nc.tensor.transpose(ps_xT[:, k * S + t * P:k * S + (t + 1) * P],
                                                       xb[:, t, k * P:(k + 1) * P], g.ident[:, :])
                    last.then_inc(xT_ps, STEP)
                    wait_reuse(pe, prod_ready, j)
                    for f in range(NF):
                        out = (ps_re, ps_im)[f // 2][:, (f % 2) * D:(f % 2 + 1) * D]
                        for t in range(QT):
                            last = nc.tensor.matmul(out, mx.dft[:, t * FFT + f * P:t * FFT + (f + 1) * P],
                                                    xb[:, t, :], start=t == 0, stop=t == QT - 1)
                    last.then_inc(u_ps, STEP)

                def gate(j):
                    pe.wait_ge(xT_ready, j + STEP)
                    wait_reuse(pe, gate_ready, j)
                    for m in range(KC):
                        for k in range(KC):
                            last = nc.tensor.matmul(ps_gate[:, m * S:(m + 1) * S],
                                                    mx.gate_w[:, k * D + m * P:k * D + (m + 1) * P],
                                                    xT[:, k, :], start=k == 0, stop=k == KC - 1)
                    last.then_inc(gate_ps, STEP)

                def inverse(i):
                    pe.wait_ge(yf_ready, i + STEP)
                    wait_reuse(pe, yT_ready, i)
                    for m in range(KC):
                        for f in range(NF):
                            last = nc.tensor.matmul(ps_y[:, m * S:(m + 1) * S], yf[:, f, m * P:(m + 1) * P],
                                                    mx.idft[:, f * S:(f + 1) * S], start=f == 0, stop=f == NF - 1)
                    last.then_inc(y_ps, STEP)

                def state(i):
                    pe.wait_ge(yT_ready, i + STEP)
                    wait_reuse(pe, ss_ready, i)
                    for m in range(KC):
                        for k in range(KC):
                            last = nc.tensor.matmul(ps_ss[:, m * S:(m + 1) * S],
                                                    mx.ss_w[:, k * D + m * P:k * D + (m + 1) * P],
                                                    yT[:, k, :], start=k == 0, stop=k == KC - 1)
                    last.then_inc(ss_ps, STEP)

                def project(i):
                    pe.wait_ge(mix_ready, i + STEP)
                    wait_reuse(pe, norm.summed, i)
                    for t in range(QT):
                        for k in range(KC):
                            last = nc.tensor.matmul(ps_out[:, t * D:(t + 1) * D], mixT[:, k, t * P:(t + 1) * P],
                                                    mx.fin_w[:, k * D:(k + 1) * D], start=k == 0, stop=k == KC - 1)
                    last.then_inc(out_ps, STEP)

                pe.wait_ge(mx.loaded, mx.loads)
                front(0)
                gate(0)
                def batch(i):
                    inverse(i)
                    front(i + STEP)
                    state(i)
                    gate(i + STEP)
                    project(i)

                each_batch(pe, batch, last_base - STEP)
                inverse(last_base)
                state(last_base)
                project(last_base)

            @block.scalar
            def _(act):
                def take(j):
                    act.wait_ge(xT_ps, j + STEP)
                    wait_reuse(act, gate_ps, j)
                    nc.scalar.activation(xT[:, :, :], fold(ps_xT[:, :], KC), ACT.Copy).then_inc(xT_ready, STEP)

                def gate(j):
                    act.wait_ge(gate_ps, j + STEP)
                    wait_reuse(act, mix_ready, j)
                    for m in range(KC):
                        last = nc.scalar.activation(gateT[:, m, :], ps_gate[:, m * S:(m + 1) * S], ACT.Gelu,
                                                    bias=mx.gate_b[:, m:m + 1])
                    last.then_inc(gate_ready, STEP)

                def back(i):
                    act.wait_ge(y_ps, i + STEP)
                    wait_reuse(act, ss_ps, i)
                    nc.scalar.activation(yT[:, :, :], fold(ps_y[:, :], KC), ACT.Copy).then_inc(yT_ready, STEP)

                def state(i):
                    act.wait_ge(ss_ps, i + STEP)
                    wait_reuse(act, mix_ready, i)
                    for m in range(KC):
                        last = nc.scalar.activation(ssT[:, m, :], ps_ss[:, m * S:(m + 1) * S], ACT.Gelu,
                                                    bias=mx.ss_b[:, m:m + 1])
                    last.then_inc(ss_ready, STEP)

                take(0)
                gate(0)
                def batch(i):
                    back(i)
                    take(i + STEP)
                    state(i)
                    gate(i + STEP)

                each_batch(act, batch, last_base - STEP)
                back(last_base)
                state(last_base)

            @block.vector
            def _(dve):
                def take(j):
                    wait_reuse(dve, u_ps, j)
                    nc.vector.tensor_copy(xb[:, :, :].rearrange("p t c -> p (t c)"), batch_of(g.x_all, j))\
                        .then_inc(xb_ready, STEP)

                def mix(i):
                    dve.wait_ge(ss_ready, i + STEP)
                    dve.wait_ge(gate_ready, i + STEP)
                    wait_reuse(dve, out_ps, i)
                    nc.vector.tensor_tensor(mixT[:, :, :], ssT[:, :, :], gateT[:, :, :], ALU.mult)\
                        .then_inc(mix_ready, STEP)

                def spectrum(j):
                    dve.wait_ge(u_ps, j + STEP)
                    wait_reuse(dve, yf_ready, j)
                    nc.vector.tensor_tensor(prod[:, 0, :], ps_re[:, :], mx.spec_re[:, :], ALU.mult)
                    nc.vector.tensor_tensor(prod[:, 1, :], ps_im[:, :], mx.spec_im[:, :], ALU.mult)
                    nc.vector.tensor_tensor(prod[:, 2, :], ps_re[:, :], mx.spec_im[:, :], ALU.mult)
                    nc.vector.tensor_tensor(prod[:, 3, :], ps_im[:, :], mx.spec_re2[:, :], ALU.mult)\
                        .then_inc(prod_ready, STEP)

                def back(i, following=None):
                    dve.wait_ge(out_ps, i + STEP)
                    dve.wait_ge(xr_ready, i + STEP)
                    wait_reuse(dve, norm.done, i)
                    nc.vector.tensor_tensor(norm.y[:, :, :], fold(ps_out[:, :], QT), xr[:, :, :], ALU.add)\
                        .then_inc(norm.summed, STEP)
                    norm.vector_moments(nc, dve, i)
                    if following is not None:
                        take(following)
                    norm.vector_scale(nc, dve, i, g.x_all)

                dve.wait_ge(g.x_loaded, 16)
                dve.wait_ge(mx.loaded, mx.loads)
                take(0)
                spectrum(0)
                take(STEP)

                def batch(i):
                    spectrum(i + STEP)
                    mix(i)
                    back(i, i + 2 * STEP)

                each_batch(dve, batch, last_base - 2 * STEP)
                spectrum(last_base)
                mix(last_base - STEP)
                back(last_base - STEP)
                mix(last_base)
                back(last_base)


def attention_phase(nc, a, g, tag, w, *, cross, causal, top, project, scale,
                    load_own=False, prefetch=None):
    UNITS = QT * HP
    HALF = UNITS // KC
    PAIRS = HP // KC
    GROUP = 1 if top else PAIRS
    PROBS = 2 if top else 4
    TURNED = 2 * GROUP
    LAG = 1 if top else 2
    AHEAD = 2 if top else 3

    def unit(u):
        u %= UNITS
        return u // HALF, u // PAIRS % QT, u % PAIRS

    def keys(qt):
        return qt + 1 if causal else QT

    with ExitStack() as stack:
        core = Core(nc, stack)
        xb = core.sb(f"{tag}_xb", [P, QT, D])
        xT = core.sb(f"{tag}_xT", [P, KC, S])
        cT = core.sb(f"{tag}_cT", [P, KC, S]) if cross else xT
        qT = core.sb(f"{tag}_qT", [P, KC, S])
        kz = core.sb(f"{tag}_kz", [P, KC, 2 if top else NH // KC, S])
        val = core.sb(f"{tag}_val", [P, QT, HP * 4 * DK])
        prob = core.sb(f"{tag}_prob", [P, PROBS, 2, S])
        if top:
            turned_weights = core.sb(f"{tag}_probT", [P, TURNED, 2, QT, P])
        else:
            group_weights = [core.sb(f"{tag}_probT{qt}", [P, GROUP, 2, keys(qt), P]) for qt in range(QT)]
        sums = core.sb(f"{tag}_sums", [P, PROBS, 2])
        inverse = core.sb(f"{tag}_inverse", [P, PROBS, 2])
        neg_max = core.sb(f"{tag}_neg_max", [P, 4, 2])
        ctxT = core.sb(f"{tag}_ctxT", [P, KC, S])
        if top:
            top8 = core.sb(f"{tag}_top8", [P, 2, 2, KEPT // 8, 8])
            top_exp = core.sb(f"{tag}_top_exp", [P, 2, KEPT])
            scores = core.sb(f"{tag}_scores", [P, 2, 2, S])
            rest = core.sb(f"{tag}_rest", [P, 2, 2, 2, S])
            kept = core.sb(f"{tag}_kept", [P, 2, 2, S])
            bk = core.sb(f"{tag}_bk_masked", [P, KC, 2])
        bq = core.sb(f"{tag}_bq_scaled", [P, KC]) if w.bq is not None else None
        carrier = core.sem(f"{tag}_carrier")
        bq_ready = core.sem(f"{tag}_bq_ready")
        norm = Norm(core, tag)
        s_banks = [core.ps(f"{tag}_s{n}") for n in range(AHEAD)]
        t_bank = [core.ps(f"{tag}_t{n}") for n in range(2)]
        o_banks = [core.ps(f"{tag}_o{n}") for n in range(KC if top else 1)]
        j_bank = [core.ps(f"{tag}_j{n}") for n in range(2)]
        (xb_ready, cT_loaded, xT_ps, xT_ready, q_ready, qk_ps, k_ready, v_ps, v_ready, s_ps, s_read, max_ready,
         topk_ready, top_step, neg_ready, kept_ready, dropped_ready, subtracted, inverse_ready, p_ready, tp_ps,
         pt_ready, av_ps, ctx_ready, o_ps, residual_ready, val_zeroed, bk_ready) = (
            core.sem(f"{tag}_{n}") for n in (
                "xb_ready", "cT_loaded", "xT_ps", "xT_ready", "q_ready", "qk_ps", "k_ready", "v_ps", "v_ready",
                "s_ps", "s_read", "max_ready", "topk_ready", "top_step", "neg_ready", "kept_ready",
                "dropped_ready", "subtracted", "inverse_ready", "p_ready", "tp_ps", "pt_ready", "av_ps",
                "ctx_ready", "o_ps", "residual_ready", "val_zeroed", "bk_ready"))
        last_base = (B - 1) * STEP

        def probT(u):
            if top:
                return turned_weights[:, u % TURNED, :, :, :]
            _, qt, j = unit(u)
            return group_weights[qt][:, j, :, :, :]

        def s_bank(n, u):
            return s_banks[(UNITS * n + u) % AHEAD]

        def o_bank(m):
            return o_banks[m][:, 0:S] if len(o_banks) == KC else o_banks[0][:, m * S:(m + 1) * S]

        def batches(engine, body):
            body(0, 0, True, False)
            assert (B - 2) % AHEAD == 0
            with engine.Fori(STEP, last_base - AHEAD * STEP + 1, AHEAD * STEP) as i:
                for n in range(AHEAD):
                    body(i + n * STEP if n else i, (n + 1) % AHEAD, False, False)
            body(last_base, (B - 1) % AHEAD, False, True)

        with nc.Block() as block:

            @block.sync
            def _(sp):
                def load(j):
                    wait_reuse(sp, v_ps, j)
                    b_rows = KC * P // STEP
                    src = a["ctxT"][bass.ds(j * b_rows, KC * P), :]
                    sp.dma_start(cT[:, :, :], src.rearrange("(k p) s -> p k s", p=P)).then_inc(cT_loaded, 16)

                if cross:
                    each_batch(sp, load)
                if prefetch is not None:
                    sp.wait_ge(w.loaded, w.loads)
                    prefetch(sp)

            @block.gpsimd
            def _(pool):
                def take(j):
                    wait_reuse(pool, xT_ps, j)
                    nc.gpsimd.tensor_copy(xb[:, :, :].rearrange("p t c -> p (t c)"), batch_of(g.x_all, j))\
                        .then_inc(xb_ready, STEP)

                def residual(i):
                    wait_reuse(pool, norm.done, i)
                    if w.bo is None:
                        nc.gpsimd.tensor_copy(norm.y[:, :, :].rearrange("p t c -> p (t c)"),
                                              batch_of(g.x_all, i)).then_inc(residual_ready, STEP)
                    else:
                        nc.gpsimd.tensor_tensor(norm.y[:, :, :], fold(batch_of(g.x_all, i), QT),
                                                spread(w.bo[:, :], QT, 1), ALU.add).then_inc(residual_ready, STEP)

                def weights(i, u):
                    slot = prob[:, u % PROBS, :, :]
                    if top:
                        pool.wait_ge(dropped_ready, i + u + 1)
                        nc.gpsimd.tensor_tensor(inverse[:, u % PROBS, :], sums[:, u % PROBS, :],
                                                g.minus_one[:, :], ALU.pow).then_inc(inverse_ready, 1)
                        nc.gpsimd.tensor_tensor(slot, kept[:, u % 2, :, :], slot, ALU.subtract)\
                            .then_inc(subtracted, 1)
                        pool.wait_ge(subtracted, i + u + 1)
                        n = S
                    else:
                        n = keys(unit(u)[1]) * P
                    pool.wait_ge(inverse_ready, i + u + 1)
                    nc.gpsimd.tensor_tensor(slot[:, :, 0:n], slot[:, :, 0:n],
                                            spread(inverse[:, u % PROBS, :], n, 2), ALU.mult)\
                        .then_inc(p_ready, 1)

                take(0)
                nc.gpsimd.memset(val[:, :, :], 0.0).then_inc(val_zeroed, 1)
                pool.wait_ge(w.loaded, w.loads)

                def body(i, n, first, last):
                    for u in range(UNITS):
                        weights(i, u)
                        if u == 3 and not last:
                            take(i + STEP)
                        if u == 8 and not first:
                            norm.pool_rstd(nc, pool, i - STEP, g.minus_half)
                        if u == 12:
                            residual(i)

                batches(pool, body)
                norm.pool_rstd(nc, pool, last_base, g.minus_half)

            @block.tensor
            def _(pe):
                def turn_x(j):
                    pe.wait_ge(xb_ready, j + STEP)
                    wait_reuse(pe, v_ready, j)
                    for k in range(KC):
                        for t in range(QT):
                            last = nc.tensor.transpose(j_bank[1][:, k * S + t * P:k * S + (t + 1) * P],
                                                       xb[:, t, k * P:(k + 1) * P], g.ident[:, :])
                    last.then_inc(xT_ps, STEP)

                def project_q(j, m):
                    if m == 0:
                        pe.wait_ge(xT_ready, j + STEP)
                        if cross:
                            pe.wait_ge(cT_loaded, j + STEP)
                        wait_reuse(pe, norm.summed, j - STEP)
                    else:
                        pe.wait_ge(v_ready, j + HALF)
                    for k in range(KC):
                        nc.tensor.matmul(j_bank[m][:, 0:S], w.wq[:, k * D + m * P:k * D + (m + 1) * P],
                                         xT[:, k, :], start=k == 0, stop=k == KC - 1)

                def project_k(j, m):
                    for k in range(KC):
                        last = nc.tensor.matmul(j_bank[m][:, S:2 * S], w.wk[:, k * D + m * P:k * D + (m + 1) * P],
                                                cT[:, k, :], start=k == 0, stop=k == KC - 1)
                    last.then_inc(qk_ps, HALF)

                def project_v(j, m, t):
                    if m == 1 and t == 0:
                        pe.wait_ge(q_ready, j + STEP)
                        pe.wait_ge(k_ready, j + STEP)
                    for k in range(KC):
                        last = nc.tensor.matmul(j_bank[1][:, t * P:(t + 1) * P], cT[:, k, t * P:(t + 1) * P],
                                                w.wv[:, k * D + m * P:k * D + (m + 1) * P],
                                                start=k == 0, stop=k == KC - 1 and w.bv is None)
                    if w.bv is not None:
                        last = nc.tensor.matmul(j_bank[1][:, t * P:(t + 1) * P], g.ones_row[:, :],
                                                w.bv[0:1, m * P:(m + 1) * P], start=False, stop=True)
                    if t == QT - 1:
                        last.then_inc(v_ps, HALF)

                def score(i, n, u):
                    m, qt, j = unit(u)
                    if u % HALF == 0:
                        pe.wait_ge(q_ready, i + u + HALF)
                    if qt == 0 and (not top or j == 0):
                        pe.wait_ge(k_ready, i + u // HALF * HALF + (HALF if top else 2 * j + 2))
                    wait_reuse(pe, s_read, i + u + 1 - AHEAD)
                    seen = keys(qt) * P
                    out = fold(s_bank(n, u)[:, :], 2)[:, :, 0:seen]
                    if top:
                        rows = slice(32 * j, 32 * j + 32)
                        moving = kz[rows, m, :, 0:seen]
                    else:
                        rows = slice(0, P)
                        moving = kz[:, m, 2 * j:2 * j + 2, 0:seen]
                    last = nc.tensor.matmul(out, qT[rows, m, qt * P:(qt + 1) * P], moving,
                                            start=True, stop=not causal)
                    if causal:
                        last = nc.tensor.matmul(out[:, :, qt * P:(qt + 1) * P], g.ident16[:, :],
                                                g.causal16[:, :, :], start=False, stop=True)
                    last.then_inc(s_ps, 1)

                def turn(i, u):
                    n_keys = keys(unit(u)[1])
                    pe.wait_ge(p_ready, i + u + 1)
                    wait_reuse(pe, pt_ready, i + u - 1)
                    for h in range(2):
                        for kt in range(n_keys):
                            c = (h * QT + kt) * P
                            last = nc.tensor.transpose(t_bank[u % 2][:, c:c + P],
                                                       prob[:, u % PROBS, h, kt * P:(kt + 1) * P], g.ident[:, :])
                    last.then_inc(tp_ps, 1)

                def gather(i, u):
                    m, qt, j = unit(u)
                    pe.wait_ge(pt_ready, i + u + 1)
                    if (u + 1) % HALF == GROUP % HALF:
                        pe.wait_ge(v_ready, i + (u // HALF + 1) * HALF)
                        wait_reuse(pe, ctx_ready, i + (u // HALF + 1 - len(o_banks)) * HALF)
                    steps = [(h, kt) for h in range(2) for kt in range(keys(qt))]
                    for h, kt in steps:
                        for member in range(u - GROUP + 1, u + 1):
                            pair = unit(member)[2]
                            at = ((m * PAIRS + pair) * 2 + h) * 2 * DK
                            last = nc.tensor.matmul(
                                o_bank(m)[32 * pair:32 * pair + 32, qt * P:(qt + 1) * P],
                                val[:, kt, at:at + 2 * DK], probT(member)[:, h, kt, :],
                                start=(h, kt) == steps[0], stop=(h, kt) == steps[-1])
                    last.then_inc(av_ps, GROUP)

                def tail(i, qt):
                    if qt == 0:
                        pe.wait_ge(ctx_ready, i + STEP)
                    for k in range(KC):
                        piece = ctxT[:, k, qt * P:(qt + 1) * P]
                        if project:
                            last = nc.tensor.matmul(j_bank[0][:, qt * D:(qt + 1) * D], piece,
                                                    w.wo[:, k * D:(k + 1) * D], start=k == 0, stop=k == KC - 1)
                        else:
                            last = nc.tensor.transpose(j_bank[0][:, qt * D + k * P:qt * D + (k + 1) * P],
                                                       piece, g.ident[:, :])
                    if qt == QT - 1:
                        last.then_inc(o_ps, STEP)

                def behind(i, first, u):
                    if u >= LAG or not first:
                        turn(i, u - LAG)
                    if (u - LAG) % GROUP == 0 and (u > LAG or not first):
                        gather(i, u - LAG - 1)

                turn_x(0)
                pe.wait_ge(w.loaded, w.loads)
                pe.wait_ge(val_zeroed, 1)
                project_q(0, 0)
                project_k(0, 0)
                project_v(0, 0, 0)
                project_v(0, 0, 1)
                for u in range(AHEAD):
                    score(0, 0, u)

                def body(i, n, first, last):
                    for u in range(UNITS):
                        if u + AHEAD < UNITS or not last:
                            score(i, n, u + AHEAD)
                        behind(i, first, u)
                        if u == 1:
                            project_q(i, 1)
                        if u == 2:
                            project_k(i, 1)
                        if u in (4, 5) and not first:
                            tail(i - STEP, u - 4)
                        if u in (7, 8):
                            project_v(i, 1, u - 7)
                        if u == 9 and not last:
                            turn_x(i + STEP)
                        if u == 10 and not last:
                            project_q(i + STEP, 0)
                        if u == 11 and not last:
                            project_k(i + STEP, 0)
                        if u in (12, 13) and not last:
                            project_v(i + STEP, 0, u - 12)

                batches(pe, body)
                for u in range(UNITS, UNITS + LAG):
                    behind(last_base, False, u)
                gather(last_base, UNITS - 1)
                for qt in range(QT):
                    tail(last_base, qt)

            @block.scalar
            def _(act):
                if load_own:
                    w.load(act)
                if w.bq is not None:
                    act.wait_ge(w.loaded, w.loads)
                    nc.scalar.mul(bq[:, :], w.bq[:, :], scale).then_inc(bq_ready, 1)
                    act.wait_ge(bq_ready, 1)
                if top:
                    act.wait_ge(bk_ready, 1)
                act.wait_ge(val_zeroed, 1)

                def take_x(j):
                    act.wait_ge(xT_ps, j + STEP)
                    wait_reuse(act, v_ps, j)
                    nc.scalar.activation(xT[:, :, :], fold(j_bank[1][:, :], KC), ACT.Copy)\
                        .then_inc(xT_ready, STEP)

                def queries(j, m):
                    act.wait_ge(qk_ps, j + (m + 1) * HALF)
                    wait_reuse(act, s_ps, j + (m - 1) * HALF)
                    if w.bq is None:
                        last = nc.scalar.activation(qT[:, m, :], j_bank[m][:, 0:S], ACT.Copy, scale=scale)
                    else:
                        last = nc.scalar.activation(qT[:, m, :], j_bank[m][:, 0:S], ACT.Identity,
                                                    bias=bq[:, m:m + 1], scale=scale)
                    last.then_inc(q_ready, HALF)
                    if top:
                        for h in range(2):
                            last = nc.scalar.activation(kz[:, m, h, :], j_bank[m][:, S:2 * S], ACT.Identity,
                                                        bias=bk[:, m, h:h + 1], scale=g.pair_mask[:, h:h + 1])
                        last.then_inc(k_ready, HALF)

                def key_rows(j, m, pair):
                    if pair == 0:
                        act.wait_ge(qk_ps, j + (m + 1) * HALF)
                        wait_reuse(act, s_ps, j + (m - 1) * HALF)
                    for h in (2 * pair, 2 * pair + 1):
                        nc.scalar.activation(kz[:, m, h, :], j_bank[m][:, S:2 * S], ACT.Copy,
                                             scale=g.head_mask[:, h:h + 1]).then_inc(k_ready, 1)

                def values(j, m):
                    act.wait_ge(v_ps, j + (m + 1) * HALF)
                    wait_reuse(act, av_ps, j + (m - 1) * HALF)
                    for t in range(QT):
                        width = PAIRS * 4 * DK
                        out = val[:, t, m * width:(m + 1) * width].rearrange(
                            "p (pair group c) -> p pair group c", pair=PAIRS, c=DK)[:, :, 0:4:3, :]
                        src = j_bank[1][:, t * P:(t + 1) * P].rearrange(
                            "p (pair head c) -> p pair head c", pair=PAIRS, c=DK)
                        last = nc.scalar.activation(out, src, ACT.Copy)
                    last.then_inc(v_ready, HALF)

                def exponentials(i, n, u):
                    seen = keys(unit(u)[1]) * P
                    act.wait_ge(max_ready, i + u + 1)
                    wait_reuse(act, tp_ps, i + u + 1 - PROBS)
                    for h in range(2):
                        last = nc.scalar.activation(prob[:, u % PROBS, h, 0:seen],
                                                    s_bank(n, u)[:, h * S:h * S + seen], ACT.Exp,
                                                    bias=neg_max[:, u % 4, h:h + 1],
                                                    accum_out=sums[:, u % PROBS, h:h + 1])
                    last.then_inc(s_read, 1)

                def copy_scores(i, n, u):
                    act.wait_ge(s_ps, i + u + 1)
                    wait_reuse(act, kept_ready, i + u - 1)
                    nc.scalar.activation(scores[:, u % 2, :, :], fold(s_bank(n, u)[:, :], 2), ACT.Copy)\
                        .then_inc(s_read, 1)

                def top_exponentials(i, u):
                    act.wait_ge(topk_ready, i + u + 1)
                    wait_reuse(act, subtracted, i + u - 1)
                    wait_reuse(act, tp_ps, i + u - 1)
                    nc.scalar.mul(neg_max[:, u % 4, :], top8[:, u % 2, :, 0, 0], -1.0).then_inc(neg_ready, 1)
                    act.wait_ge(neg_ready, i + u + 1)
                    for h in range(2):
                        last = nc.scalar.activation(kept[:, u % 2, h, :], scores[:, u % 2, h, :], ACT.Exp,
                                                    bias=neg_max[:, u % 4, h:h + 1])
                    last.then_inc(kept_ready, 1)
                    for h in range(2):
                        nc.scalar.activation(top_exp[:, h, :], top8[:, u % 2, h, :, :].rearrange("p r c -> p (r c)"),
                                             ACT.Exp, bias=neg_max[:, u % 4, h:h + 1],
                                             accum_out=sums[:, u % PROBS, h:h + 1])
                    for h in range(2):
                        last = nc.scalar.activation(prob[:, u % 2, h, :], rest[:, u % 2, 1, h, :], ACT.Exp,
                                                    bias=neg_max[:, u % 4, h:h + 1])
                    last.then_inc(dropped_ready, 1)

                def turned(i, u):
                    act.wait_ge(tp_ps, i + u + 1)
                    wait_reuse(act, av_ps, i + u + 1 - TURNED)
                    nc.scalar.activation(probT(u).rearrange("p h k c -> p (h k c)"),
                                         t_bank[u % 2][:, :], ACT.Copy).then_inc(pt_ready, 1)

                def context(i, m):
                    act.wait_ge(av_ps, i + (m + 1) * HALF)
                    if m == 0:
                        wait_reuse(act, o_ps, i)
                    nc.scalar.activation(ctxT[:, m, :], o_bank(m), ACT.Copy).then_inc(ctx_ready, HALF)

                take_x(0)
                queries(0, 0)
                if not top:
                    for pair in range(PAIRS):
                        key_rows(0, 0, pair)
                values(0, 0)
                if top:
                    copy_scores(0, 0, 0)

                def body(i, n, first, last):
                    for u in range(UNITS):
                        if top:
                            if u + 1 < UNITS or not last:
                                copy_scores(i, n, u + 1)
                            top_exponentials(i, u)
                            if u >= 1 or not first:
                                turned(i, u - 1)
                        else:
                            exponentials(i, n, u)
                        if u == 3:
                            if not first:
                                context(i - STEP, 1)
                            queries(i, 1)
                        if not top and u in (3, 4, 5, 6):
                            key_rows(i, 1, u - 3)
                        if u == 9:
                            values(i, 1)
                        if u == 10 and not last:
                            take_x(i + STEP)
                        if u == 11:
                            context(i, 0)
                        if u == 12 and not last:
                            queries(i + STEP, 0)
                        if not top and u in (12, 13, 14, 15) and not last:
                            key_rows(i + STEP, 0, u - 12)
                        if u == 14 and not last:
                            values(i + STEP, 0)

                batches(act, body)
                if top:
                    turned(last_base, UNITS - 1)
                context(last_base, 1)

            @block.vector
            def _(dve):
                def maxima(i, n, u):
                    seen = keys(unit(u)[1]) * P
                    dve.wait_ge(s_ps, i + u + 1)
                    nc.vector.tensor_reduce(neg_max[:, u % 4, :], fold(s_bank(n, u)[:, :], 2)[:, :, 0:seen],
                                            AX.X, ALU.max, negate=True).then_inc(max_ready, 1)

                def invert(i, u):
                    dve.wait_ge(s_read, i + u + 1)
                    nc.vector.reciprocal(inverse[:, u % PROBS, :], sums[:, u % PROBS, :])\
                        .then_inc(inverse_ready, 1)

                def turned(i, u):
                    n_keys = keys(unit(u)[1])
                    dve.wait_ge(tp_ps, i + u + 1)
                    wait_reuse(dve, av_ps, i + GROUP * ((u - TURNED) // GROUP + 1))
                    src = t_bank[u % 2][:, :].rearrange("p (h k c) -> p h k c", h=2, k=QT)
                    nc.vector.tensor_copy(probT(u), src[:, :, 0:n_keys, :])\
                        .then_inc(pt_ready, 1)

                def select(i, u):
                    dve.wait_ge(s_read, i + u + 1)
                    wait_reuse(dve, dropped_ready, i + u - 1)
                    dve.sem_inc(carrier, 1)
                    rounds = KEPT // 8
                    steps = 4 * rounds - 1
                    base = (i + u) * steps
                    for r in range(rounds):
                        src = [scores[:, u % 2, h, :] if r == 0 else rest[:, u % 2, (r - 1) % 2, h, :]
                               for h in range(2)]
                        for h in range(2):
                            if r > 0:
                                dve.wait_ge(top_step, base + 4 * r - 1 + h)
                                dve.sem_inc(carrier, 1)
                            nc.vector.max(top8[:, u % 2, h, r, :], src[h]).then_inc(top_step, 1)
                        for h in range(2):
                            dve.wait_ge(top_step, base + 4 * r + 1 + h)
                            dve.sem_inc(carrier, 1)
                            last = nc.vector.match_replace(rest[:, u % 2, r % 2, h, :],
                                                           top8[:, u % 2, h, r, :], src[h], NEG)
                            last.then_inc(*((top_step, 1) if (r, h) != (rounds - 1, 1) else (topk_ready, 1)))

                def add(i):
                    dve.wait_ge(o_ps, i + STEP)
                    dve.wait_ge(residual_ready, i + STEP)
                    nc.vector.tensor_tensor(norm.y[:, :, :], fold(j_bank[0][:, :], QT), norm.y[:, :, :], ALU.add)\
                        .then_inc(norm.summed, STEP)

                dve.wait_ge(w.loaded, w.loads)
                if top:
                    for m in range(KC):
                        last = nc.vector.tensor_scalar(bk[:, m, :], g.pair_mask[:, :], w.bk[:, m:m + 1], None,
                                                       ALU.mult)
                    last.then_inc(bk_ready, 1)

                if not top:
                    maxima(0, 0, 0)

                def body(i, n, first, last):
                    for u in range(UNITS):
                        if top:
                            select(i, u)
                        else:
                            if u + 1 < UNITS or not last:
                                maxima(i, n, u + 1)
                            if u >= 1 or not first:
                                invert(i, u - 1)
                            if u > LAG or not first:
                                turned(i, u - LAG - 1)
                        if u == 6 and not first:
                            add(i - STEP)
                        if u == 7 and not first:
                            norm.vector_moments(nc, dve, i - STEP)
                        if u == 10 and not first:
                            norm.vector_scale(nc, dve, i - STEP, g.x_all)

                batches(dve, body)
                if not top:
                    invert(last_base, UNITS - 1)
                    for u in range(UNITS, UNITS + LAG + 1):
                        turned(last_base, u - LAG - 1)
                add(last_base)
                norm.vector_moments(nc, dve, last_base)
                norm.vector_scale(nc, dve, last_base, g.x_all)


def logit_phase(nc, a, g, tag, w, r, x_rows):
    with ExitStack() as stack:
        core = Core(nc, stack)
        xb = core.sb(f"{tag}_xb", [P, 2, QT, D])
        xT = core.sb(f"{tag}_xT", [P, 2, KC, S])
        hid = core.sb(f"{tag}_hid", [P, 2, KC, S]) if w.rw1 is not None else xT
        xT_banks, hid_banks, logit_banks = ([core.ps(f"{tag}_{name}{n}") for n in range(2)]
                                            for name in ("tb", "hb", "lb"))
        xb_ready, xT_ps, xT_ready, hid_ps, hid_ready, logit_ps, logit_ready, x_stored = (
            core.sem(f"{tag}_{n}") for n in ("xb_ready", "xT_ps", "xT_ready", "hid_ps", "hid_ready", "logit_ps",
                                             "logit_ready", "x_stored"))

        with nc.Block() as block:

            @block.sync
            def _(sp):
                w.load(sp)
                sp.dma_start(x_rows.rearrange("(t p) c -> p t c", p=P), fold(g.x_all[:, :], NT))\
                    .then_inc(x_stored, 16)
                sp.dma_start(r.bias_up[:, :], w.b_up.broadcast_to([P, E * U])).then_inc(r.bias_loaded, 16)
                sp.wait_ge(x_stored, 16)

            @block.tensor
            def _(pe):
                def front(i, s):
                    pe.wait_ge(xb_ready, i + STEP)
                    wait_reuse(pe, xT_ready, i - STEP)
                    for k in range(KC):
                        for t in range(QT):
                            last = nc.tensor.transpose(xT_banks[s][:, k * S + t * P:k * S + (t + 1) * P],
                                                       xb[:, s, t, k * P:(k + 1) * P], g.ident[:, :])
                    last.then_inc(xT_ps, STEP)

                def middle(i, s):
                    if w.rw1 is not None:
                        pe.wait_ge(xT_ready, i + STEP)
                        wait_reuse(pe, hid_ready, i - STEP)
                        for m in range(KC):
                            for k in range(KC):
                                last = nc.tensor.matmul(hid_banks[s][:, m * S:(m + 1) * S],
                                                        w.rw1[:, k * D + m * P:k * D + (m + 1) * P],
                                                        xT[:, s, k, :], start=k == 0, stop=k == KC - 1)
                        last.then_inc(hid_ps, STEP)

                def back(i, s):
                    pe.wait_ge(hid_ready if w.rw1 is not None else xT_ready, i + STEP)
                    wait_reuse(pe, logit_ready, i - STEP)
                    for t in range(QT):
                        for k in range(KC):
                            last = nc.tensor.matmul(logit_banks[s][:, t * E:(t + 1) * E],
                                                    hid[:, s, k, t * P:(t + 1) * P],
                                                    w.router[:, k * E:(k + 1) * E], start=k == 0, stop=k == KC - 1)
                    last.then_inc(logit_ps, STEP)

                front(0, 0)
                front(STEP, 1)
                pe.wait_ge(w.loaded, w.loads)
                middle(0, 0)

                def two(i):
                    for s in range(2):
                        front(i + (2 + s) * STEP, s)
                        middle(i + (1 + s) * STEP, 1 - s)
                        back(i + s * STEP, s)

                two(0)
                with pe.Fori(2 * STEP, (B - 4) * STEP + 1, 2 * STEP) as i:
                    two(i)
                middle((B - 1) * STEP, 1)
                for s in range(2):
                    back((B - 2 + s) * STEP, s)

            @block.scalar
            def _(act):
                def front(i, s):
                    act.wait_ge(xT_ps, i + STEP)
                    wait_reuse(act, logit_ps if w.rw1 is None else hid_ps, i - STEP)
                    nc.scalar.activation(xT[:, s, :, :], fold(xT_banks[s][:, :], KC), ACT.Copy)\
                        .then_inc(xT_ready, STEP)

                def back(i, s):
                    if w.rw1 is not None:
                        act.wait_ge(hid_ps, i + STEP)
                        wait_reuse(act, logit_ps, i - STEP)
                        for m in range(KC):
                            last = nc.scalar.activation(hid[:, s, m, :], hid_banks[s][:, m * S:(m + 1) * S],
                                                        ACT.Silu, bias=w.rb1[:, m:m + 1])
                        last.then_inc(hid_ready, STEP)

                front(0, 0)
                front(STEP, 1)
                back(0, 0)

                def two(i):
                    for s in range(2):
                        front(i + (2 + s) * STEP, s)
                        back(i + (1 + s) * STEP, 1 - s)

                two(0)
                with act.Fori(2 * STEP, (B - 4) * STEP + 1, 2 * STEP) as i:
                    two(i)
                back((B - 1) * STEP, 1)

            @block.vector
            def _(dve):
                def take(i, s):
                    wait_reuse(dve, xT_ps, i - STEP)
                    nc.vector.tensor_copy(xb[:, s, :, :].rearrange("p t c -> p (t c)"), batch_of(g.x_all, i))\
                        .then_inc(xb_ready, STEP)

                def result(i, s):
                    dve.wait_ge(logit_ps, i + STEP)
                    step_e = QT * E // STEP
                    out = fold(r.logits[:, :, :].rearrange("p t e -> p (t e)")[:, bass.ds(i * step_e, QT * E)], QT)
                    src = fold(logit_banks[s][:, 0:QT * E], QT)
                    if w.rb2 is None:
                        nc.vector.tensor_copy(out, src).then_inc(logit_ready, STEP)
                    else:
                        nc.vector.tensor_tensor(out, src, spread(w.rb2[:, :], QT, 1), ALU.add)\
                            .then_inc(logit_ready, STEP)

                def two(i):
                    for s in range(2):
                        take(i + (3 + s) * STEP, 1 - s)
                        result(i + s * STEP, s)

                for b in range(3):
                    take(b * STEP, b % 2)
                if w.rb2 is not None:
                    dve.wait_ge(w.loaded, w.loads)
                two(0)
                with dve.Fori(2 * STEP, (B - 6) * STEP + 1, 2 * STEP) as i:
                    two(i)
                take((B - 1) * STEP, 1)
                for b in range(B - 4, B):
                    result(b * STEP, b % 2)


def place_phase(nc, g, tag, r):
    with ExitStack() as stack:
        core = Core(nc, stack)
        top8 = core.sb(f"{tag}_top8", [P, NT, 8])
        index = core.sb(f"{tag}_index", [P, NT, 8], U32)
        choice = core.sb(f"{tag}_choice", [P, NT, TOPK])
        gap = core.sb(f"{tag}_gap", [P, 3, NT])
        hot = core.sb(f"{tag}_hot", [P, TOPK, NT, E])
        hot16 = core.sb(f"{tag}_hot16", [P, NT * E], BF16)
        total = core.sb(f"{tag}_total", [P, 2, NT, E])
        count = core.sb(f"{tag}_count", [P, NT, E])
        tiles = core.sb(f"{tag}_tiles", [P, 6, E])
        place = core.sb(f"{tag}_place", [P, NT, E])
        placed = core.sb(f"{tag}_placed", [P, TOPK, NT, E])
        slot = core.sb(f"{tag}_slot", [P, TOPK, NT])
        owner = core.sb(f"{tag}_owner", [P, ROUTED, E])
        owned = core.sb(f"{tag}_owned", [P, 2, ROUTED])
        at = core.sb(f"{tag}_at", [P, 3, TOPK * NT])
        row_hot = core.sb(f"{tag}_row_hot", [P, TOPK * NT, P], BF16)
        tile_hot = core.sb(f"{tag}_tile_hot", [P, 3, TOPK * NT, ROUTED], BF16)
        found = core.sb(f"{tag}_found", [P, 3, ROUTED])
        copy = core.sb(f"{tag}_copy", [P, 3, ROUTED])
        spare = core.sb(f"{tag}_spare", [P, 1])
        sum_bank, token_bank = core.ps(f"{tag}_sum"), core.ps(f"{tag}_tok")
        v, exp_ready, count_ps, hot_ready, placed_ready, token_ps = (
            core.sem(f"{tag}_{n}") for n in ("vector_step", "exp_ready", "count_ps", "hot_ready",
                                             "placed_ready", "token_ps"))

        with nc.Block() as block:

            @block.tensor
            def _(pe):
                pe.wait_ge(hot_ready, 1)
                nc.tensor.matmul(sum_bank[:, 0:NT * E], g.before16[:, :], hot16[:, :], start=True, stop=True)
                nc.tensor.matmul(sum_bank[:, NT * E:2 * NT * E], g.ones16[:, :], hot16[:, :],
                                 start=True, stop=True).then_inc(count_ps, 1)
                pe.wait_ge(placed_ready, 1)
                for n in range(TOPK * NT):
                    last = nc.tensor.matmul(token_bank[:, 0:3 * ROUTED], row_hot[:, n, :], tile_hot[:, :, n, :],
                                            start=n == 0, stop=n == TOPK * NT - 1)
                last.then_inc(token_ps, 1)

            @block.scalar
            def _(act):
                act.wait_ge(v, 2)
                nc.scalar.activation(gap[:, 1, :], gap[:, 0, :], ACT.Exp).then_inc(exp_ready, 1)

            @block.vector
            def _(dve):
                done = [0]

                def step(instruction):
                    done[0] += 1
                    instruction.then_inc(v, 1)
                    dve.wait_ge(v, done[0])

                for t in range(NT):
                    last = nc.vector.max(top8[:, t, :], r.logits[:, t, :])
                step(last)
                step(nc.vector.tensor_tensor(gap[:, 0, :], top8[:, :, 1], top8[:, :, 0], ALU.subtract))
                for t in range(NT):
                    last = nc.vector.max_index(index[:, t, :], top8[:, t, :], r.logits[:, t, :])
                step(last)
                step(nc.vector.tensor_copy(choice[:, :, :], index[:, :, 0:TOPK]))
                for k in range(TOPK):
                    last = nc.vector.tensor_tensor(hot[:, k, :, :], spread(choice[:, :, k], E, 2),
                                                   spread(g.iota[:, 0:E], NT, 1), ALU.is_equal)
                step(last)
                nc.vector.tensor_tensor(hot16[:, :], hot[:, 0, :, :].rearrange("p t e -> p (t e)"),
                                        hot[:, 1, :, :].rearrange("p t e -> p (t e)"), ALU.add)\
                    .then_inc(hot_ready, 1)
                dve.wait_ge(exp_ready, 1)
                step(nc.vector.tensor_scalar(gap[:, 2, :], gap[:, 1, :], 1.0, None, ALU.add))
                step(nc.vector.reciprocal(r.weights[:, 0:NT], gap[:, 2, :]))
                nc.vector.tensor_tensor(r.weights[:, NT:2 * NT], gap[:, 1, :], r.weights[:, 0:NT], ALU.mult)
                dve.wait_ge(count_ps, 1)
                nc.vector.tensor_copy(place[:, :, :], fold(sum_bank[:, 0:NT * E], NT))
                nc.vector.tensor_copy(count[:, :, :], fold(sum_bank[:, NT * E:2 * NT * E], NT))
                step(nc.vector.tensor_copy(total[:, 0, :, :], fold(sum_bank[:, NT * E:2 * NT * E], NT)))
                side, reach = 0, 1
                while reach < NT:
                    nc.vector.tensor_copy(total[:, 1 - side, 0:reach, :], total[:, side, 0:reach, :])
                    step(nc.vector.tensor_tensor(total[:, 1 - side, reach:, :], total[:, side, reach:, :],
                                                 total[:, side, 0:NT - reach, :], ALU.add))
                    side, reach = 1 - side, 2 * reach
                step(nc.vector.tensor_scalar(tiles[:, 0, :], total[:, side, NT - 1, :], 127.0, 1.0 / P,
                                             ALU.add, ALU.mult))
                step(nc.vector.tensor_scalar(tiles[:, 1, :], tiles[:, 0, :], -127.0 / 256, None, ALU.add))
                step(nc.vector.tensor_scalar(tiles[:, 2, :], tiles[:, 1, :], 12582912.0, None, ALU.add))
                step(nc.vector.tensor_scalar(tiles[:, 3, :], tiles[:, 2, :], -12582912.0, None, ALU.add))
                src, other, reach = 3, 4, 1
                while reach < E:
                    nc.vector.tensor_copy(tiles[:, other, 0:reach], tiles[:, src, 0:reach])
                    step(nc.vector.tensor_tensor(tiles[:, other, reach:], tiles[:, src, reach:],
                                                 tiles[:, src, 0:E - reach], ALU.add))
                    src, other, reach = other, (5 if other == 4 else 4), 2 * reach
                end = src
                free = 9 - end
                step(nc.vector.tensor_tensor(total[:, 1 - side, :, :], total[:, side, :, :], count[:, :, :],
                                             ALU.subtract))
                step(nc.vector.tensor_tensor(place[:, :, :], place[:, :, :], total[:, 1 - side, :, :], ALU.add))
                nc.vector.memset(tiles[:, free, 0:1], 0.0)
                step(nc.vector.tensor_scalar(tiles[:, free, 1:E], tiles[:, end, 0:E - 1], float(P), None,
                                             ALU.mult))
                step(nc.vector.tensor_tensor(place[:, :, :], place[:, :, :], spread(tiles[:, free, :], NT, 1),
                                             ALU.add))
                for k in range(TOPK):
                    last = nc.vector.tensor_tensor(placed[:, k, :, :], hot[:, k, :, :], place[:, :, :], ALU.mult)
                step(last)
                for k in range(TOPK):
                    last = nc.vector.tensor_reduce(slot[:, k, :], placed[:, k, :, :], AX.X, ALU.add)
                step(last)
                flat = slot[:, :, :].rearrange("p k t -> p (k t)")
                step(nc.vector.tensor_scalar(at[:, 0, :], flat, 1.0 / P, -127.0 / 256, ALU.mult, ALU.add))
                step(nc.vector.tensor_scalar(at[:, 2, :], at[:, 0, :], 12582912.0, None, ALU.add))
                step(nc.vector.tensor_scalar(at[:, 1, :], at[:, 2, :], -12582912.0, None, ALU.add))
                step(nc.vector.scalar_tensor_tensor(at[:, 0, :], at[:, 1, :], -float(P), flat,
                                                    ALU.mult, ALU.add))
                nc.vector.tensor_tensor(row_hot[:, :, :], spread(at[:, 0, :], P, 2),
                                        spread(g.iota[:, :], TOPK * NT, 1), ALU.is_equal)
                nc.vector.tensor_scalar(spare[:, :], g.row[:, :], float(TOPK * N), None, ALU.add)
                step(nc.vector.tensor_tensor(tile_hot[:, 2, :, :], spread(at[:, 1, :], ROUTED, 2),
                                             spread(g.iota[:, 0:ROUTED], TOPK * NT, 1), ALU.is_equal))
                nc.vector.tensor_tensor(tile_hot[:, 0, :, :], tile_hot[:, 2, :, :],
                                        spread(g.iota[:, 0:TOPK * NT], ROUTED, 2), ALU.mult)
                nc.vector.tensor_scalar(tile_hot[:, 1, :, :], tile_hot[:, 2, :, :], g.row[:, 0:1], None,
                                        ALU.mult).then_inc(placed_ready, 1)
                step(nc.vector.tensor_tensor(owner[:, :, :], spread(g.iota[:, 0:ROUTED], E, 2),
                                             spread(tiles[:, end, :], ROUTED, 1), ALU.is_ge))
                step(nc.vector.tensor_reduce(owned[:, 0, :], owner[:, :, :], AX.X, ALU.add))
                step(nc.vector.tensor_scalar(owned[:, 1, :], owned[:, 0, :], float(E - 1), None, ALU.min))
                nc.vector.tensor_copy(r.expert[:, 0:ROUTED], owned[:, 1, :])
                dve.wait_ge(token_ps, 1)
                step(nc.vector.tensor_copy(found[:, :, :], fold(token_bank[:, 0:3 * ROUTED], 3)))
                nc.vector.tensor_scalar(copy[:, 2, :], found[:, 2, :], -1.0, 1.0, ALU.mult, ALU.add)
                step(nc.vector.scalar_tensor_tensor(copy[:, 0, :], found[:, 0, :], float(P), found[:, 1, :],
                                                    ALU.mult, ALU.add))
                nc.vector.scalar_tensor_tensor(r.results[:, :], copy[:, 2, :], spare[:, 0:1], copy[:, 0, :],
                                               ALU.mult, ALU.add)
                step(nc.vector.tensor_scalar(copy[:, 1, :], copy[:, 0, :], float(N), -float(N),
                                             ALU.is_ge, ALU.mult))
                nc.vector.tensor_tensor(r.tokens[:, :], copy[:, 0, :], copy[:, 1, :], ALU.add)


def each_tile(engine, body, n):
    body(0)
    with engine.Fori(1, n) as j:
        body(j)


def expert_phase(nc, g, tag, r, b_down, x_rows, ys, func):
    with ExitStack() as stack:
        core = Core(nc, stack)
        xg = core.sb(f"{tag}_xg", [P, D])
        xgT = core.sb(f"{tag}_xgT", [P, KC, P])
        index = core.sb(f"{tag}_index", [P, 1], U32)
        place = core.sb(f"{tag}_place", [P, 1], U32)
        place_ready = core.sem(f"{tag}_place_ready")
        bias_down = core.sb(f"{tag}_bias_down", [P, E * D])
        bias_down_loaded = core.sem(f"{tag}_bias_down_loaded")
        raw = core.sb(f"{tag}_raw", [P, U])
        hid = core.sb(f"{tag}_hid", [P, U])
        hidT = core.sb(f"{tag}_hidT", [P, UC, P])
        y = core.sb(f"{tag}_y", [P, D])
        up_bank = [core.ps(f"{tag}_u{n}") for n in range(2)]
        t_bank = [core.ps(f"{tag}_t{n}") for n in range(2)]
        x_bank = core.ps(f"{tag}_x")
        y_bank = core.ps(f"{tag}_yb")
        carrier, index_ready, raw_ready = (core.sem(f"{tag}_{n}") for n in ("carrier", "index_ready",
                                                                            "raw_ready"))
        xg_loaded, xgT_ps, xgT_ready, up_ps, hid_ready, hidT_ps, hidT_ready, down_ps, y_ready, y_stored = (
            core.sem(f"{tag}_{n}") for n in ("xg_loaded", "xgT_ps", "xgT_ready", "up_ps", "hid_ready", "hidT_ps",
                                             "hidT_ready", "down_ps", "y_ready", "y_stored"))
        CH = U // 512
        last_tile = ROUTED - 1

        with nc.Block() as block:

            @block.gpsimd
            def _(pool):
                def gather(j):
                    wait_reuse(pool, xg_loaded, j * 16)
                    nc.gpsimd.tensor_copy(index[:, 0:1], r.tokens[:, bass.ds(j, 1)]).then_inc(index_ready, 1)
                    pool.wait_ge(index_ready, j + 1)
                    wait_reuse(pool, xgT_ps, j)
                    pool.sem_inc(carrier, 1)
                    pool.indirect_dma_start(out=xg[:, :], out_offset=None, in_=x_rows[:, :],
                                            in_offset=bass.IndirectOffsetOnAxis(ap=index[:, 0:1], axis=0))\
                        .then_inc(xg_loaded, 16)

                def scatter(j):
                    wait_reuse(pool, y_stored, j * 16)
                    nc.gpsimd.tensor_copy(place[:, 0:1], r.results[:, bass.ds(j, 1)]).then_inc(place_ready, 1)
                    pool.wait_ge(place_ready, j + 1)
                    pool.wait_ge(y_ready, j + 1)
                    pool.sem_inc(carrier, 1)
                    pool.indirect_dma_start(out=ys[:, :], in_=y[:, :], in_offset=None,
                                            out_offset=bass.IndirectOffsetOnAxis(ap=place[:, 0:1], axis=0))\
                        .then_inc(y_stored, 16)

                for j in range(3):
                    gather(j)
                gather(3)
                scatter(0)
                with pool.Fori(1, ROUTED - 3) as j:
                    gather(j + 3)
                    scatter(j)
                for j in range(ROUTED - 3, ROUTED):
                    scatter(j)
                pool.wait_ge(y_stored, ROUTED * 16)

            @block.sync
            def _(sp):
                sp.dma_start(bias_down[:, :], b_down.broadcast_to([P, E * D])).then_inc(bias_down_loaded, 16)

            @block.tensor
            def _(pe):
                def take(j):
                    pe.wait_ge(xg_loaded, (j + 1) * 16)
                    wait_reuse(pe, xgT_ready, j)
                    for k in range(KC):
                        last = nc.tensor.transpose(x_bank[:, k * P:(k + 1) * P], xg[:, k * P:(k + 1) * P],
                                                   g.ident[:, :])
                    last.then_inc(xgT_ps, 1)

                def up(j):
                    e = pe.value_load(r.expert[0:1, bass.ds(j, 1)], min_val=0, max_val=E - 1)
                    pe.wait_ge(xgT_ready, j + 1)
                    wait_reuse(pe, raw_ready, j * CH)
                    for c in range(CH):
                        for k in range(KC):
                            at = e * (KC * U) + (k * U + c * 512)
                            last = nc.tensor.matmul(up_bank[c][:, :], xgT[:, k, :],
                                                    g.w_up[:, bass.ds(at, 512)], start=k == 0, stop=k == KC - 1)
                        last.then_inc(up_ps, 1)

                def turn(j):
                    for c in range(CH):
                        pe.wait_ge(hid_ready, j * CH + c + 1)
                        if c == 0:
                            wait_reuse(pe, hidT_ready, j * CH)
                        for n in range(UC // CH):
                            last = nc.tensor.transpose(t_bank[c][:, n * P:(n + 1) * P],
                                                       hid[:, c * 512 + n * P:c * 512 + (n + 1) * P], g.ident[:, :])
                        last.then_inc(hidT_ps, 1)

                def down(j):
                    e = pe.value_load(r.expert[0:1, bass.ds(j, 1)], min_val=0, max_val=E - 1)
                    wait_reuse(pe, y_ready, j)
                    for c in range(CH):
                        pe.wait_ge(hidT_ready, j * CH + c + 1)
                        for n in range(c * UC // CH, (c + 1) * UC // CH):
                            at = e * (UC * D) + n * D
                            last = nc.tensor.matmul(y_bank[:, 0:D], hidT[:, n, :], g.w_down[:, bass.ds(at, D)],
                                                    start=n == 0, stop=n == UC - 1)
                    last.then_inc(down_ps, 1)

                pe.wait_ge(g.experts_loaded, (r.layer + 1) * 2 * E * 16)
                take(0)
                up(0)
                take(1)

                def tile(j):
                    turn(j)
                    up(j + 1)
                    take(j + 2)
                    down(j)

                each_tile(pe, tile, last_tile - 1)
                turn(last_tile - 1)
                up(last_tile)
                down(last_tile - 1)
                turn(last_tile)
                down(last_tile)

            @block.scalar
            def _(act):
                def activate(j):
                    for c in range(CH):
                        act.wait_ge(raw_ready, j * CH + c + 1)
                        if c == 0:
                            wait_reuse(act, hidT_ps, j * CH)
                        nc.scalar.activation(hid[:, c * 512:(c + 1) * 512], raw[:, c * 512:(c + 1) * 512], func)\
                            .then_inc(hid_ready, 1)

                each_tile(act, activate, ROUTED)

            @block.vector
            def _(dve):
                def take(j):
                    dve.wait_ge(xgT_ps, j + 1)
                    wait_reuse(dve, up_ps, j * CH)
                    nc.vector.tensor_copy(xgT[:, :, :], fold(x_bank[:, 0:KC * P], KC)).then_inc(xgT_ready, 1)

                def turned(j):
                    for c in range(CH):
                        dve.wait_ge(hidT_ps, j * CH + c + 1)
                        if c == 0:
                            wait_reuse(dve, down_ps, j)
                        half = UC // CH
                        nc.vector.tensor_copy(hidT[:, c * half:(c + 1) * half, :], fold(t_bank[c][:, :], half))\
                            .then_inc(hidT_ready, 1)

                def expert(j):
                    return dve.value_load(r.expert[0:1, bass.ds(j, 1)], min_val=0, max_val=E - 1)

                def add_bias(j):
                    e = expert(j)
                    for c in range(CH):
                        dve.wait_ge(up_ps, j * CH + c + 1)
                        if c == 0:
                            wait_reuse(dve, hid_ready, j * CH)
                        nc.vector.tensor_tensor(raw[:, c * 512:(c + 1) * 512], up_bank[c][:, :],
                                                r.bias_up[:, bass.ds(e * U + c * 512, 512)], ALU.add)\
                            .then_inc(raw_ready, 1)

                def result(j):
                    e = expert(j)
                    dve.wait_ge(down_ps, j + 1)
                    wait_reuse(dve, y_stored, j * 16)
                    nc.vector.tensor_tensor(y[:, :], y_bank[:, 0:D], bias_down[:, bass.ds(e * D, D)],
                                            ALU.add).then_inc(y_ready, 1)

                dve.wait_ge(r.bias_loaded, 16)
                dve.wait_ge(bias_down_loaded, 16)
                take(0)
                add_bias(0)
                take(1)

                def tile(j):
                    turned(j)
                    add_bias(j + 1)
                    take(j + 2)
                    result(j)

                each_tile(dve, tile, last_tile - 1)
                turned(last_tile - 1)
                add_bias(last_tile)
                result(last_tile - 1)
                turned(last_tile)
                result(last_tile)


def combine_phase(nc, g, tag, r, ys, twice, out):
    with ExitStack() as stack:
        core = Core(nc, stack)
        rows = core.sb(f"{tag}_rows", [P, 2, TOPK, QT, D])
        part = core.sb(f"{tag}_part", [P, 2, QT, D])
        norms = [Norm(core, f"{tag}{n}") for n in range(2)]
        part_ready = core.sem(f"{tag}_part_ready")
        both_ready = core.sem(f"{tag}_both_ready")
        loaded = [core.sem(f"{tag}_loaded{n}") for n in range(2)]
        stored = core.sem(f"{tag}_stored")
        per_batch = TOPK * 16

        with nc.Block() as block:

            @block.scalar
            def _(act):
                def load(j, s):
                    wait_reuse(act, norms[s].summed, (j - s * STEP) // 2)
                    for k in range(TOPK):
                        act.dma_start(rows[:, s, k, :, :], ys[bass.ds(j * (S // STEP) + k * N, S), :]
                                      .rearrange("(t p) c -> p t c", p=P)).then_inc(loaded[s], 16)

                load(0, 0)
                load(STEP, 1)
                with act.Fori(2 * STEP, (B - 2) * STEP + 1, 2 * STEP) as j:
                    for s in range(2):
                        load(j + s * STEP, s)

            @block.gpsimd
            def _(pool):
                with pool.Fori(0, B // 2 * STEP, STEP) as half:
                    for norm in norms:
                        norm.pool_rstd(nc, pool, half, g.minus_half)

            @block.vector
            def _(dve):
                def weigh(p, s):
                    i, half, norm = p + s * STEP, p // 2, norms[s]
                    dve.wait_ge(loaded[s], p * (per_batch // (2 * STEP)) + per_batch)
                    col = i // (STEP // QT)
                    wait_reuse(dve, norm.done, half)
                    for qt in range(QT):
                        last = nc.vector.scalar_tensor_tensor(
                            part[:, 0, qt, :], rows[:, s, 0, qt, :], r.weights[:, bass.ds(col + qt, 1)],
                            tile_of(g.x_all, i, qt), ALU.mult, ALU.add)
                    last.then_inc(part_ready, STEP)
                    dve.wait_ge(part_ready, i + STEP)
                    for qt in range(QT):
                        last = nc.vector.scalar_tensor_tensor(
                            (part[:, 1, qt, :] if twice else norm.y[:, qt, :]), rows[:, s, 1, qt, :],
                            r.weights[:, bass.ds(NT + col + qt, 1)], part[:, 0, qt, :],
                            ALU.mult, ALU.add)
                    if twice:
                        last.then_inc(both_ready, STEP)
                        dve.wait_ge(both_ready, i + STEP)
                        last = nc.vector.tensor_tensor(norm.y[:, :, :], part[:, 1, :, :],
                                                       fold(batch_of(g.x_all, i), QT), ALU.add)
                    last.then_inc(norm.summed, STEP)

                def pair(p):
                    for s in range(2):
                        weigh(p, s)
                        norms[s].vector_moments(nc, dve, p // 2)
                    for s in range(2):
                        norms[s].vector_scale(nc, dve, p // 2, g.x_all, p + s * STEP)

                pair(0)
                with dve.Fori(2 * STEP, (B - 2) * STEP + 1, 2 * STEP) as p:
                    pair(p)

            @block.sync
            def _(sp):
                if out is not None:
                    def store(p):
                        for s in range(2):
                            sp.wait_ge(norms[s].done, p // 2 + STEP)
                            sp.dma_start(out[bass.ds((p + s * STEP) * (S // STEP), S), :]
                                         .rearrange("(t p) c -> p t c", p=P),
                                         fold(batch_of(g.x_all, p + s * STEP), QT)).then_inc(stored, 16)

                    store(0)
                    with sp.Fori(2 * STEP, (B - 2) * STEP + 1, 2 * STEP) as p:
                        store(p)
                    sp.wait_ge(stored, B * 16)


class Weights:

    def __init__(self, core, a, tag, mats=(), cols=(), rows=(), narrow=()):
        self.loaded = core.sem(f"{tag}_loaded")
        self.parts = []
        tiles = {}
        for name, source in mats + narrow:
            tiles[name] = core.sb(f"{tag}_{name}", [P, KC * a[source].shape[1]])
            self.parts.append((fold(tiles[name][:, :], KC), a[source].rearrange("(k p) c -> p k c", p=P)))
        for name, source in cols:
            tiles[name] = core.sb(f"{tag}_{name}", [P, KC])
            self.parts.append((tiles[name][:, :], a[source]))
        for name, source in rows:
            n = a[source].shape[1]
            tiles[name] = core.sb(f"{tag}_{name}", [P, n])
            self.parts.append((tiles[name][:, :], a[source].broadcast_to([P, n])))
        self.loads = 16 * len(self.parts)
        self.wq, self.wk, self.wv, self.wo = (tiles.get(name) for name in ("wq", "wk", "wv", "wo"))
        self.bq, self.bk, self.bv, self.bo = (tiles.get(name) for name in ("bq", "bk", "bv", "bo"))
        self.router, self.rw1, self.rb1, self.rb2 = (tiles.get(name) for name in ("router", "rw1", "rb1", "rb2"))

    def load(self, queue):
        for tile, source in self.parts:
            queue.dma_start(tile, source).then_inc(self.loaded, 16)


class Routing:

    def __init__(self, core, layer):
        tag = f"r{layer}"
        self.layer = layer
        self.weights = core.sb(f"{tag}_weights", [P, TOPK * NT])
        self.expert = core.sb(f"{tag}_expert", [P, ROUTED + 1], I32)
        self.tokens = core.sb(f"{tag}_tokens", [P, ROUTED], U32)
        self.results = core.sb(f"{tag}_results", [P, ROUTED], U32)
        self.bias_up = core.sb(f"{tag}_bias_up", [P, E * U])
        self.logits = core.sb(f"{tag}_logits", [P, NT, E])
        self.bias_loaded = core.sem(f"{tag}_bias_loaded")


class Shared:

    def __init__(self, nc, core, a):
        self.nc, self.a = nc, a
        self.x_all = core.sb("x_all", [P, NT * D])
        self.w_up = core.sb("w_up", [P, E * KC * U])
        self.w_down = core.sb("w_down", [P, E * UC * D])
        self.ident = core.sb("ident", [P, P])
        self.ident16 = core.sb("ident16", [P, P], BF16)
        self.before16 = core.sb("before16", [P, P], BF16)
        self.ones16 = core.sb("ones16", [P, P], BF16)
        self.causal16 = core.sb("causal16", [P, 2, P], BF16)
        self.pair_mask = core.sb("pair_mask", [P, 2])
        self.head_mask = core.sb("head_mask", [P, NH // KC])
        self.iota = core.sb("iota", [P, P])
        self.row = core.sb("row", [P, 1])
        self.minus_half = core.sb("minus_half", [P, QT])
        self.ones_row = core.sb("ones_row", [1, P])
        self.minus_one = core.sb("minus_one", [P, 2])
        self.x_loaded = core.sem("x_loaded")
        self.const_loaded = core.sem("const_loaded")
        self.experts_loaded = core.sem("experts_loaded")

    def load_experts(self, queue, up, down):
        for e in range(E):
            queue.dma_start(fold(self.w_up[:, e * KC * U:(e + 1) * KC * U], KC),
                            up[e].rearrange("(k p) u -> p k u", p=P)).then_inc(self.experts_loaded, 16)
            queue.dma_start(fold(self.w_down[:, e * UC * D:(e + 1) * UC * D], UC),
                            down[e].rearrange("(n p) c -> p n c", p=P)).then_inc(self.experts_loaded, 16)


class Mixer:

    def __init__(self, core):
        self.dft = core.sb("dft", [P, QT * FFT])
        self.idft = core.sb("idft", [P, NF * S])
        self.spec_re = core.sb("spec_re", [P, KC * D])
        self.spec_re2 = core.sb("spec_re2", [P, KC * D])
        self.spec_im = core.sb("spec_im", [P, KC * D])
        self.ss_w = core.sb("ss_w", [P, KC * D])
        self.gate_w = core.sb("gate_w", [P, KC * D])
        self.fin_w = core.sb("fin_w", [P, KC * D])
        self.ss_b = core.sb("ss_b", [P, KC])
        self.gate_b = core.sb("gate_b", [P, KC])
        self.fin_b = core.sb("fin_b", [P, D])
        self.dft_loaded = core.sem("dft_loaded")
        self.loaded = core.sem("mixer_loaded")
        self.loads = 7 * 16

    def load(self, queue, a):
        queue.dma_start(fold(self.dft[:, :], QT), a["dft"].rearrange("(t p) f -> p t f", p=P))\
            .then_inc(self.dft_loaded, 16)
        for tile, name, n in ((self.idft, "idft", NF), (self.ss_w, "ss_wT", KC), (self.gate_w, "gate_wT", KC),
                              (self.fin_w, "fin_wT", KC)):
            queue.dma_start(fold(tile[:, :], n), a[name].rearrange("(t p) f -> p t f", p=P))\
                .then_inc(self.loaded, 16)
        queue.dma_start(self.ss_b[:, :], a["ss_b"]).then_inc(self.loaded, 16)
        queue.dma_start(self.gate_b[:, :], a["gate_b"]).then_inc(self.loaded, 16)
        queue.dma_start(self.fin_b[:, :], a["fin_b"].broadcast_to([P, D])).then_inc(self.loaded, 16)


def decoder(nc, a, out):
    x_rows = [nc.dram_tensor(f"x_rows{n}", (N, D), F32) for n in range(2)]
    ys = [nc.dram_tensor(f"ys{n}", (TOPK * N + P, D), F32) for n in range(2)]
    with ExitStack() as stack:
        core = Core(nc, stack)
        g = Shared(nc, core, a)

        with ExitStack() as first:
            w0 = Weights(Core(nc, first), a, "c0", mats=(("wq", "L0_wqT"), ("wk", "L0_wkT"),
                                                         ("wv", "L0_wvT"), ("wo", "L0_woT")))
            with ExitStack() as early:
                mx = Mixer(Core(nc, early))

                def load_first(sp):
                    mx.load(sp, a)
                    w0.load(sp)
                    g.load_experts(sp, a["L0_up"], a["L0_down"])

                kernel_spectrum(nc, a, g, mx, load_first)
                mixer_phase(nc, a, g, mx)
            attention_phase(nc, a, g, "c0", w0, cross=True, causal=True, top=False, project=True,
                            scale=DK ** -0.5)
        experts(nc, a, g, 0, x_rows[0], ys[0], out)
        with ExitStack() as second:
            ws = Weights(Core(nc, second), a, "s1", mats=(("wq", "L1_wq"), ("wk", "L1_wk"), ("wv", "L1_wv")))

            def prefetch(sp):
                g.load_experts(sp, a["L1_up"], a["L1_down"])

            attention_phase(nc, a, g, "s1", ws, cross=False, causal=False, top=False, project=False,
                            scale=D ** -0.5, load_own=True, prefetch=prefetch)
        with ExitStack() as third:
            wc = Weights(Core(nc, third), a, "c1", mats=(("wq", "L1_wqT"), ("wk", "L1_wkT"),
                                                         ("wv", "L1_wvT"), ("wo", "L1_woT")),
                         cols=(("bq", "L1_bq"), ("bk", "L1_bk")), rows=(("bv", "L1_bv"), ("bo", "L1_bo")))
            attention_phase(nc, a, g, "c1", wc, cross=True, causal=False, top=True,
                            project=True, scale=DK ** -0.5, load_own=True)
        experts(nc, a, g, 1, x_rows[1], ys[1], out)


def experts(nc, a, g, layer, x_rows, ys, out):
    with ExitStack() as stack:
        core = Core(nc, stack)
        r = Routing(core, layer)
        if layer == 0:
            w = Weights(core, a, "t0", narrow=(("router", "L0_router"),))
            w.b_up, w.b_down, func = a["L0_b_up"], a["L0_b_down"], ACT.Gelu
        else:
            w = Weights(core, a, "t1", mats=(("rw1", "L1_rw1"),), narrow=(("router", "L1_rw2"),),
                        cols=(("rb1", "L1_rb1"),), rows=(("rb2", "L1_rb2"),))
            w.b_up, w.b_down, func = a["L1_b_up"], a["L1_b_down"], ACT.Silu
        logit_phase(nc, a, g, f"l{layer}", w, r, x_rows)
        place_phase(nc, g, f"t{layer}", r)
        expert_phase(nc, g, f"e{layer}", r, w.b_down, x_rows, ys, func)
        combine_phase(nc, g, f"k{layer}", r, ys, layer == 1, out if layer == 1 else None)



def _laid_out(i):
    c = np.ascontiguousarray

    def col(v):
        return c(v.reshape(KC, P).T)

    f = np.arange(FFT // 2)
    t = np.arange(S)
    turn = 2 * np.pi * np.outer(t, f) / FFT
    nyquist = (-1.0) ** t
    dft = np.concatenate([np.cos(turn), -np.sin(turn)], axis=1)
    dft[:, FFT // 2] = nyquist
    idft = 2 * np.concatenate([np.cos(turn.T), -np.sin(turn.T)], axis=0) / FFT
    idft[0] = 1 / FFT
    idft[FFT // 2] = nyquist / FFT
    p = np.arange(P)
    const = np.zeros((P, 4 * P + 3 + NH // KC), np.float32)
    const[:, 0:P] = np.eye(P)
    const[:, P:2 * P] = p[:, None] < p[None, :]
    const[:, 2 * P:3 * P] = np.where(p[None, :] > p[:, None], -1e30, 0)
    const[:, 3 * P] = (p // DK) % 2 == 0
    const[:, 3 * P + 1] = (p // DK) % 2 == 1
    const[:, 3 * P + 2:3 * P + 2 + NH // KC] = p[:, None] // DK == np.arange(NH // KC)
    const[:, 3 * P + 2 + NH // KC:-1] = p
    const[:, -1] = p
    qkv = i["L1_attn_w_qkv"]
    return {
        "x": i["x"].reshape(N, D),
        "ctxT": c(i["ctx_1024"].transpose(0, 2, 1)).reshape(B * D, S),
        "decays": i["L0_attn_decays"].reshape(STATES, 1),
        "frequencies": i["L0_attn_frequencies"].reshape(STATES, 1),
        "in_projT": c(i["L0_attn_in_proj"].T),
        "out_proj": i["L0_attn_out_proj"],
        "lag": np.tile(np.arange(S, dtype=np.float32), (STATES, 1)),
        "dft": dft.astype(np.float32), "idft": idft.astype(np.float32), "const": const,
        "ss_wT": c(i["L0_attn_ss_W"].T), "gate_wT": c(i["L0_attn_gate_W"].T), "fin_wT": c(i["L0_attn_fin_W"].T),
        "ss_b": col(i["L0_attn_ss_b"]), "gate_b": col(i["L0_attn_gate_b"]),
        "fin_b": i["L0_attn_fin_b"].reshape(1, D),
        "L0_wqT": c(i["L0_xattn_Wq"].T), "L0_wkT": c(i["L0_xattn_Wk"].T), "L0_wvT": c(i["L0_xattn_Wv"].T),
        "L0_woT": c(i["L0_xattn_Wo"].T),
        "L0_up": c(i["L0_ffn_w_up"].transpose(0, 2, 1)), "L0_down": c(i["L0_ffn_w_down"].transpose(0, 2, 1)),
        "L0_b_up": i["L0_ffn_b_up"].reshape(1, E * U), "L0_b_down": i["L0_ffn_b_down"].reshape(1, E * D),
        "L0_router": c(i["L0_ffn_w_router"].T),
        "L1_wq": c(qkv[:, 0:D]), "L1_wk": c(qkv[:, D:2 * D]), "L1_wv": c(qkv[:, 2 * D:]),
        "L1_wqT": c(i["L1_xattn_Wq"].T), "L1_wkT": c(i["L1_xattn_Wk"].T), "L1_wvT": c(i["L1_xattn_Wv"].T),
        "L1_woT": c(i["L1_xattn_Wo"].T),
        "L1_bq": col(i["L1_xattn_bq"]), "L1_bk": col(i["L1_xattn_bk"]),
        "L1_bv": i["L1_xattn_bv"].reshape(1, D), "L1_bo": i["L1_xattn_bo"].reshape(1, D),
        "L1_rw1": i["L1_ffn_rw1"], "L1_rb1": col(i["L1_ffn_rb1"]), "L1_rw2": i["L1_ffn_rw2"],
        "L1_rb2": i["L1_ffn_rb2"].reshape(1, E),
        "L1_up": i["L1_ffn_we1"], "L1_down": i["L1_ffn_we2"],
        "L1_b_up": i["L1_ffn_be1"].reshape(1, E * U), "L1_b_down": i["L1_ffn_be2"].reshape(1, E * D),
    }


def kernel(**inputs):
    import concourse.bacc as bacc
    from concourse.bass_utils import run_bass_kernel_spmd

    arrays = {n: np.ascontiguousarray(v) for n, v in
              _laid_out({n: np.asarray(v) for n, v in inputs.items()}).items()}
    nc = bacc.Bacc("TRN2", target_bir_lowering=False, num_devices=1)
    a = {n: nc.dram_tensor(f"in_{n}", v.shape, F32, kind="ExternalInput").ap() for n, v in arrays.items()}
    out = nc.dram_tensor("out", (N, D), F32, kind="ExternalOutput").ap()
    decoder(nc, a, out)
    result = run_bass_kernel_spmd(nc, [{f"in_{n}": v for n, v in arrays.items()}], core_ids=[0])
    return result.results[0]["out"].reshape(B, S, D)
```
